# Optimizing a Trainium2 kernel written in Bass

```python
import numpy as np
import jax
import jax.numpy as jnp

def _softmax(x, axis=-1):
    return jax.nn.softmax(x, axis=axis)

def _gelu(x):
    return jax.nn.gelu(x, approximate=True)

def _silu(x):
    return jax.nn.silu(x)

def _sigmoid(x):
    return jax.nn.sigmoid(x)

def _layernorm(x, axis=-1, eps=1e-05):
    m = jnp.mean(x, axis=axis, keepdims=True)
    v = jnp.var(x, axis=axis, keepdims=True)
    return (x - m) / jnp.sqrt(v + eps)

def _scatter_add(tgt, idx, src, axis=0):
    return tgt.at[idx].add(src)

def _segment_sum(src, seg, n):
    return jax.ops.segment_sum(src, seg, n)
kernel_name = 'mk_hybrid_d1_jaxref_r8_e776b6'

def setup_inputs(seed: int=0):
    np.random.seed(seed)
    _w = jnp.asarray

    def _L0_attn_a_setup():
        import jax, jax.numpy as jnp
        import numpy as np
        B, T, C = (8, 256, 128)
        H = 4 * C
        N_LAYER, LAYER_ID = (12, 2)
        K_CLAMP = 60.0
        LN_EPS = 1e-05

        def _ln(x, g, b):
            m = jnp.mean(x, axis=-1, keepdims=True)
            v = jnp.var(x, axis=-1, keepdims=True)
            return (x - m) * jax.lax.rsqrt(v + LN_EPS) * g + b

        def _mix(x, time_mix, combined_mix):
            c = x.shape[-1]
            xm1 = jnp.pad(x[:, :-1], ((0, 0), (1, 0), (0, 0)))
            xp1 = jnp.pad(x[:, 1:], ((0, 0), (0, 1), (0, 0)))
            xc = jnp.concatenate([xm1[..., :c // 2], xp1[..., c // 2:]], axis=-1)
            return x * time_mix + xm1 * (1.0 - time_mix) + xc * combined_mix

        def _wkv(time_decay, time_first, k, v):
            ed = jnp.exp(-jnp.exp(time_decay))
            eu = jnp.exp(time_first)

            def step(carry, kv_t):
                a, b = carry
                kt, vt = kv_t
                y = (a + eu * kt * vt) / (b + eu * kt)
                return ((ed * a + kt * vt, ed * b + kt), y)
            kT = jnp.swapaxes(k, 0, 1)
            vT = jnp.swapaxes(v, 0, 1)
            z = jnp.zeros_like(kT[0])
            _, y = jax.lax.scan(step, (z, z), (kT, vT))
            return jnp.swapaxes(y, 0, 1)

        def _time_mix_block(x, time_mix, combined_mix, time_decay, time_first, Wk, Wv, Wr, Wo):
            xm = _mix(x, time_mix, combined_mix)
            k = jnp.exp(jnp.minimum(xm @ Wk.T, K_CLAMP))
            v = xm @ Wv.T
            r = xm @ Wr.T
            wkv = _wkv(time_decay, time_first, k, v)
            return jax.nn.sigmoid(r) * wkv @ Wo.T

        def _channel_mix_block(x, time_mix, combined_mix, Fk, Fv, Fr):
            xm = _mix(x, time_mix, combined_mix)
            k = jnp.square(jax.nn.relu(xm @ Fk.T))
            kv = k @ Fv.T
            return jax.nn.sigmoid(xm @ Fr.T) * kv
        key = jax.random.key(seed)
        ks = jax.random.split(key, 9)
        s = 0.02
        x = jax.random.normal(ks[0], (B, T, C), jnp.float32)
        h = np.arange(C, dtype=np.float64)
        frac = (LAYER_ID - 1) / (N_LAYER - 2)
        f1 = 3.0 + frac * (1.2 - 3.0)
        f2 = 0.65 + frac * (0.4 - 0.65)
        decay_speed = np.power(f2, h / (C - 1) * 7.0) * f1
        tm = jnp.concatenate([jnp.zeros(C // 2), jnp.ones(C // 2)]).reshape(1, 1, C).astype(jnp.float32)
        return dict(x=x, ln1_g=jnp.ones((C,), jnp.float32), ln1_b=jnp.zeros((C,), jnp.float32), ln2_g=jnp.ones((C,), jnp.float32), ln2_b=jnp.zeros((C,), jnp.float32), att_time_mix=tm, att_combined_mix=jnp.full((1, 1, C), 0.01, jnp.float32), time_decay=jnp.asarray(np.log(decay_speed), jnp.float32), time_first=jnp.full((C,), float(np.log(0.3)), jnp.float32), Wk=jax.random.normal(ks[1], (C, C), jnp.float32) * s, Wv=jax.random.normal(ks[2], (C, C), jnp.float32) * s, Wr=jax.random.normal(ks[3], (C, C), jnp.float32) * s, Wo=jax.random.normal(ks[4], (C, C), jnp.float32) * s, ffn_time_mix=tm, ffn_combined_mix=jnp.full((1, 1, C), 0.01, jnp.float32), Fk=jax.random.normal(ks[5], (H, C), jnp.float32) * s, Fv=jax.random.normal(ks[6], (C, H), jnp.float32) * s, Fr=jax.random.normal(ks[7], (C, C), jnp.float32) * s)
    _L0_attn_a_in = _L0_attn_a_setup()

    def _L0_attn_b_setup():
        import jax, jax.numpy as jnp
        import numpy as np
        B, N, DIM, H = (4, 512, 128, 16)
        HD = DIM // H
        SCALE = HD ** (-0.5)

        def _heads(t, bsz, ntok):
            return t.reshape(bsz, ntok, H, HD).transpose(0, 2, 1, 3)

        def _fwd(x, q_w1, q_b1, q_w2, q_b2, k_w1, k_b1, k_w2, k_b2, v_w, v_b, g_w, g_b, p_w, p_b):
            bsz, ntok, dim = x.shape
            gelu = lambda t: jax.nn.gelu(t, approximate=False)
            q = _heads(jax.nn.softplus(gelu(x @ q_w1.T + q_b1) @ q_w2.T + q_b2), bsz, ntok)
            k = _heads(jax.nn.softplus(gelu(x @ k_w1.T + k_b1) @ k_w2.T + k_b2), bsz, ntok)
            v = _heads(gelu(x @ v_w.T + v_b), bsz, ntok)
            g = _heads(gelu(x @ g_w.T + g_b), bsz, ntok)
            z = jnp.einsum('bhcn,bhc->bhn', q, k.sum(axis=-1)) * SCALE
            z = 1.0 / (z + dim)
            A = jnp.einsum('bhcn,bhcm->bhnm', q, k)
            out = jnp.einsum('bhnm,bhdm->bhdn', A, v) * SCALE
            out = (out + v) * z[:, :, None, :]
            out = out.reshape(bsz, ntok, dim)
            out = out * g.reshape(bsz, ntok, dim)
            return out @ p_w.T + p_b
        key = jax.random.key(seed)
        ks = jax.random.split(key, 16)
        w = lambda k: jax.random.normal(k, (DIM, DIM), jnp.float32) * 0.02
        b = lambda k: jax.random.normal(k, (DIM,), jnp.float32) * 0.02
        return {'x': jax.random.normal(ks[0], (B, N, DIM), jnp.float32), 'q_w1': w(ks[1]), 'q_b1': b(ks[2]), 'q_w2': w(ks[3]), 'q_b2': b(ks[4]), 'k_w1': w(ks[5]), 'k_b1': b(ks[6]), 'k_w2': w(ks[7]), 'k_b2': b(ks[8]), 'v_w': w(ks[9]), 'v_b': b(ks[10]), 'g_w': w(ks[11]), 'g_b': b(ks[12]), 'p_w': w(ks[13]), 'p_b': b(ks[14])}
    _L0_attn_b_in = _L0_attn_b_setup()

    def _L0_ffn_setup():
        import jax, jax.numpy as jnp
        import numpy as np
        B, S, D, F, E, K = (4, 256, 128, 512, 8, 2)
        key = jax.random.key(seed)
        ks = jax.random.split(key, 8)
        x = jax.random.normal(ks[0], (B, S, D), dtype=jnp.float32)
        router_w = jax.random.normal(ks[1], (E, D), dtype=jnp.float32) * 0.02
        w1_w = jax.random.normal(ks[2], (E, F, D), dtype=jnp.float32) * 0.02
        w1_b = jax.random.normal(ks[3], (E, F), dtype=jnp.float32) * 0.02
        w2_w = jax.random.normal(ks[4], (E, D, F), dtype=jnp.float32) * 0.02
        w2_b = jax.random.normal(ks[5], (E, D), dtype=jnp.float32) * 0.02
        wg_w = jax.random.normal(ks[6], (E, F, D), dtype=jnp.float32) * 0.02
        wg_b = jax.random.normal(ks[7], (E, F), dtype=jnp.float32) * 0.02
        return {'x': x, 'router_w': router_w, 'w1_w': w1_w, 'w1_b': w1_b, 'w2_w': w2_w, 'w2_b': w2_b, 'wg_w': wg_w, 'wg_b': wg_b}
    _L0_ffn_in = _L0_ffn_setup()
    _d = {'L0_attn_a_x': _L0_attn_a_in['x'], 'L0_attn_a_ln1_g': _L0_attn_a_in['ln1_g'], 'L0_attn_a_ln1_b': _L0_attn_a_in['ln1_b'], 'L0_attn_a_ln2_g': _L0_attn_a_in['ln2_g'], 'L0_attn_a_ln2_b': _L0_attn_a_in['ln2_b'], 'L0_attn_a_att_time_mix': _L0_attn_a_in['att_time_mix'], 'L0_attn_a_att_combined_mix': _L0_attn_a_in['att_combined_mix'], 'L0_attn_a_time_decay': _L0_attn_a_in['time_decay'], 'L0_attn_a_time_first': _L0_attn_a_in['time_first'], 'L0_attn_a_Wk': _L0_attn_a_in['Wk'], 'L0_attn_a_Wv': _L0_attn_a_in['Wv'], 'L0_attn_a_Wr': _L0_attn_a_in['Wr'], 'L0_attn_a_Wo': _L0_attn_a_in['Wo'], 'L0_attn_a_ffn_time_mix': _L0_attn_a_in['ffn_time_mix'], 'L0_attn_a_ffn_combined_mix': _L0_attn_a_in['ffn_combined_mix'], 'L0_attn_a_Fk': _L0_attn_a_in['Fk'], 'L0_attn_a_Fv': _L0_attn_a_in['Fv'], 'L0_attn_a_Fr': _L0_attn_a_in['Fr'], 'L0_attn_b_q_w1': _L0_attn_b_in['q_w1'], 'L0_attn_b_q_b1': _L0_attn_b_in['q_b1'], 'L0_attn_b_q_w2': _L0_attn_b_in['q_w2'], 'L0_attn_b_q_b2': _L0_attn_b_in['q_b2'], 'L0_attn_b_k_w1': _L0_attn_b_in['k_w1'], 'L0_attn_b_k_b1': _L0_attn_b_in['k_b1'], 'L0_attn_b_k_w2': _L0_attn_b_in['k_w2'], 'L0_attn_b_k_b2': _L0_attn_b_in['k_b2'], 'L0_attn_b_v_w': _L0_attn_b_in['v_w'], 'L0_attn_b_v_b': _L0_attn_b_in['v_b'], 'L0_attn_b_g_w': _L0_attn_b_in['g_w'], 'L0_attn_b_g_b': _L0_attn_b_in['g_b'], 'L0_attn_b_p_w': _L0_attn_b_in['p_w'], 'L0_attn_b_p_b': _L0_attn_b_in['p_b'], 'L0_ffn_router_w': _L0_ffn_in['router_w'], 'L0_ffn_w1_w': _L0_ffn_in['w1_w'], 'L0_ffn_w1_b': _L0_ffn_in['w1_b'], 'L0_ffn_w2_w': _L0_ffn_in['w2_w'], 'L0_ffn_w2_b': _L0_ffn_in['w2_b'], 'L0_ffn_wg_w': _L0_ffn_in['wg_w'], 'L0_ffn_wg_b': _L0_ffn_in['wg_b']}
    _x0 = _d['L0_attn_a_x']
    _d['L0_attn_a_x'] = jax.random.normal(jax.random.fold_in(jax.random.key(seed), 1), (16, 512, 128), dtype=_x0.dtype)
    del _x0
    return _d

def reference(L0_attn_a_x, L0_attn_a_ln1_g, L0_attn_a_ln1_b, L0_attn_a_ln2_g, L0_attn_a_ln2_b, L0_attn_a_att_time_mix, L0_attn_a_att_combined_mix, L0_attn_a_time_decay, L0_attn_a_time_first, L0_attn_a_Wk, L0_attn_a_Wv, L0_attn_a_Wr, L0_attn_a_Wo, L0_attn_a_ffn_time_mix, L0_attn_a_ffn_combined_mix, L0_attn_a_Fk, L0_attn_a_Fv, L0_attn_a_Fr, L0_attn_b_q_w1, L0_attn_b_q_b1, L0_attn_b_q_w2, L0_attn_b_q_b2, L0_attn_b_k_w1, L0_attn_b_k_b1, L0_attn_b_k_w2, L0_attn_b_k_b2, L0_attn_b_v_w, L0_attn_b_v_b, L0_attn_b_g_w, L0_attn_b_g_b, L0_attn_b_p_w, L0_attn_b_p_b, L0_ffn_router_w, L0_ffn_w1_w, L0_ffn_w1_b, L0_ffn_w2_w, L0_ffn_w2_b, L0_ffn_wg_w, L0_ffn_wg_b):

    def _L0_attn_a_ref(x, ln1_g, ln1_b, ln2_g, ln2_b, att_time_mix, att_combined_mix, time_decay, time_first, Wk, Wv, Wr, Wo, ffn_time_mix, ffn_combined_mix, Fk, Fv, Fr):
        import jax, jax.numpy as jnp
        import numpy as np
        B, T, C = (8, 256, 128)
        H = 4 * C
        N_LAYER, LAYER_ID = (12, 2)
        K_CLAMP = 60.0
        LN_EPS = 1e-05

        def _ln(x, g, b):
            m = jnp.mean(x, axis=-1, keepdims=True)
            v = jnp.var(x, axis=-1, keepdims=True)
            return (x - m) * jax.lax.rsqrt(v + LN_EPS) * g + b

        def _mix(x, time_mix, combined_mix):
            c = x.shape[-1]
            xm1 = jnp.pad(x[:, :-1], ((0, 0), (1, 0), (0, 0)))
            xp1 = jnp.pad(x[:, 1:], ((0, 0), (0, 1), (0, 0)))
            xc = jnp.concatenate([xm1[..., :c // 2], xp1[..., c // 2:]], axis=-1)
            return x * time_mix + xm1 * (1.0 - time_mix) + xc * combined_mix

        def _wkv(time_decay, time_first, k, v):
            ed = jnp.exp(-jnp.exp(time_decay))
            eu = jnp.exp(time_first)

            def step(carry, kv_t):
                a, b = carry
                kt, vt = kv_t
                y = (a + eu * kt * vt) / (b + eu * kt)
                return ((ed * a + kt * vt, ed * b + kt), y)
            kT = jnp.swapaxes(k, 0, 1)
            vT = jnp.swapaxes(v, 0, 1)
            z = jnp.zeros_like(kT[0])
            _, y = jax.lax.scan(step, (z, z), (kT, vT))
            return jnp.swapaxes(y, 0, 1)

        def _time_mix_block(x, time_mix, combined_mix, time_decay, time_first, Wk, Wv, Wr, Wo):
            xm = _mix(x, time_mix, combined_mix)
            k = jnp.exp(jnp.minimum(xm @ Wk.T, K_CLAMP))
            v = xm @ Wv.T
            r = xm @ Wr.T
            wkv = _wkv(time_decay, time_first, k, v)
            return jax.nn.sigmoid(r) * wkv @ Wo.T

        def _channel_mix_block(x, time_mix, combined_mix, Fk, Fv, Fr):
            xm = _mix(x, time_mix, combined_mix)
            k = jnp.square(jax.nn.relu(xm @ Fk.T))
            kv = k @ Fv.T
            return jax.nn.sigmoid(xm @ Fr.T) * kv
        x = _ln(x, ln1_g, ln1_b)
        x = x + _time_mix_block(x, att_time_mix, att_combined_mix, time_decay, time_first, Wk, Wv, Wr, Wo)
        x = _ln(x, ln2_g, ln2_b)
        x = x + _channel_mix_block(x, ffn_time_mix, ffn_combined_mix, Fk, Fv, Fr)
        return x

    def _L0_attn_b_ref(x, q_w1, q_b1, q_w2, q_b2, k_w1, k_b1, k_w2, k_b2, v_w, v_b, g_w, g_b, p_w, p_b):
        import jax, jax.numpy as jnp
        import numpy as np
        B, N, DIM, H = (4, 512, 128, 16)
        HD = DIM // H
        SCALE = HD ** (-0.5)

        def _heads(t, bsz, ntok):
            return t.reshape(bsz, ntok, H, HD).transpose(0, 2, 1, 3)

        def _fwd(x, q_w1, q_b1, q_w2, q_b2, k_w1, k_b1, k_w2, k_b2, v_w, v_b, g_w, g_b, p_w, p_b):
            bsz, ntok, dim = x.shape
            gelu = lambda t: jax.nn.gelu(t, approximate=False)
            q = _heads(jax.nn.softplus(gelu(x @ q_w1.T + q_b1) @ q_w2.T + q_b2), bsz, ntok)
            k = _heads(jax.nn.softplus(gelu(x @ k_w1.T + k_b1) @ k_w2.T + k_b2), bsz, ntok)
            v = _heads(gelu(x @ v_w.T + v_b), bsz, ntok)
            g = _heads(gelu(x @ g_w.T + g_b), bsz, ntok)
            z = jnp.einsum('bhcn,bhc->bhn', q, k.sum(axis=-1)) * SCALE
            z = 1.0 / (z + dim)
            A = jnp.einsum('bhcn,bhcm->bhnm', q, k)
            out = jnp.einsum('bhnm,bhdm->bhdn', A, v) * SCALE
            out = (out + v) * z[:, :, None, :]
            out = out.reshape(bsz, ntok, dim)
            out = out * g.reshape(bsz, ntok, dim)
            return out @ p_w.T + p_b
        return _fwd(x, q_w1, q_b1, q_w2, q_b2, k_w1, k_b1, k_w2, k_b2, v_w, v_b, g_w, g_b, p_w, p_b)

    def _L0_ffn_ref(x, router_w, w1_w, w1_b, w2_w, w2_b, wg_w, wg_b):
        import jax, jax.numpy as jnp
        import numpy as np
        B, S, D, F, E, K = (4, 256, 128, 512, 8, 2)
        probs = jax.nn.softmax(jnp.einsum('bsd,ed->bse', x, router_w), axis=-1)
        token_probs, probs_idx = jax.lax.top_k(probs, K)
        gates = jnp.sum(token_probs[..., None] * jax.nn.one_hot(probs_idx, E, dtype=x.dtype), axis=-2)
        gates_e = jnp.moveaxis(gates, -1, 0)

        def body(acc, params):
            w1w, w1b, w2w, w2b, wgw, wgb, g = params
            y = jax.nn.gelu(jnp.einsum('bsd,fd->bsf', x, wgw) + wgb, approximate=False)
            h = y * (jnp.einsum('bsd,fd->bsf', x, w1w) + w1b)
            out = jnp.einsum('bsf,df->bsd', h, w2w) + w2b
            return (acc + out * g[..., None], None)
        acc0 = jnp.zeros_like(x)
        out, _ = jax.lax.scan(body, acc0, (w1_w, w1_b, w2_w, w2_b, wg_w, wg_b, gates_e))
        return out
    x = L0_attn_a_x
    x = x + _L0_attn_a_ref(_layernorm(x, axis=-1), L0_attn_a_ln1_g, L0_attn_a_ln1_b, L0_attn_a_ln2_g, L0_attn_a_ln2_b, L0_attn_a_att_time_mix, L0_attn_a_att_combined_mix, L0_attn_a_time_decay, L0_attn_a_time_first, L0_attn_a_Wk, L0_attn_a_Wv, L0_attn_a_Wr, L0_attn_a_Wo, L0_attn_a_ffn_time_mix, L0_attn_a_ffn_combined_mix, L0_attn_a_Fk, L0_attn_a_Fv, L0_attn_a_Fr)
    x = x + _L0_ffn_ref(_layernorm(x, axis=-1), L0_ffn_router_w, L0_ffn_w1_w, L0_ffn_w1_b, L0_ffn_w2_w, L0_ffn_w2_b, L0_ffn_wg_w, L0_ffn_wg_b)
    x = x + _L0_attn_b_ref(_layernorm(x, axis=-1), L0_attn_b_q_w1, L0_attn_b_q_b1, L0_attn_b_q_w2, L0_attn_b_q_b2, L0_attn_b_k_w1, L0_attn_b_k_b1, L0_attn_b_k_w2, L0_attn_b_k_b2, L0_attn_b_v_w, L0_attn_b_v_b, L0_attn_b_g_w, L0_attn_b_g_b, L0_attn_b_p_w, L0_attn_b_p_b)
    x = x + _L0_ffn_ref(_layernorm(x, axis=-1), L0_ffn_router_w, L0_ffn_w1_w, L0_ffn_w1_b, L0_ffn_w2_w, L0_ffn_w2_b, L0_ffn_wg_w, L0_ffn_wg_b)
    return x

_drawn_inputs = setup_inputs


def setup_inputs(seed=0):
    import zlib

    import numpy as np

    out = dict(_drawn_inputs(seed))
    spreads = {'L0_attn_a_ln1_g': (1.0, 0.2),
     'L0_attn_a_ln1_b': (0.0, 0.1),
     'L0_attn_a_ln2_g': (1.0, 0.2),
     'L0_attn_a_ln2_b': (0.0, 0.294),
     'L0_attn_a_att_combined_mix': (0.009999999776482582, 0.6),
     'L0_attn_a_time_first': (-1.2039728164672852, 0.6),
     'L0_attn_a_ffn_combined_mix': (0.009999999776482582, 0.6)}
    factors = {'L0_attn_a_att_time_mix': 8.0,
     'L0_attn_a_time_decay': 8.0,
     'L0_attn_a_Wk': 8.0,
     'L0_attn_a_Wv': 8.0,
     'L0_attn_a_Wr': 8.0,
     'L0_attn_a_Wo': 7.997,
     'L0_attn_a_ffn_time_mix': 8.0,
     'L0_attn_a_Fk': 7.745,
     'L0_attn_a_Fv': 7.117,
     'L0_attn_a_Fr': 8.0,
     'L0_attn_b_q_w1': 64.0,
     'L0_attn_b_q_b1': 200.0,
     'L0_attn_b_q_w2': 64.0,
     'L0_attn_b_q_b2': 200.0,
     'L0_attn_b_k_w1': 64.0,
     'L0_attn_b_k_b1': 64.0,
     'L0_attn_b_k_w2': 64.0,
     'L0_attn_b_k_b2': 200.0,
     'L0_attn_b_v_w': 64.0,
     'L0_attn_b_v_b': 64.0,
     'L0_attn_b_g_w': 64.0,
     'L0_attn_b_g_b': 64.0,
     'L0_attn_b_p_w': 64.0,
     'L0_attn_b_p_b': 200.0,
     'L0_ffn_router_w': 8.0,
     'L0_ffn_w1_w': 8.0,
     'L0_ffn_w1_b': 200.0,
     'L0_ffn_w2_w': 8.0,
     'L0_ffn_w2_b': 200.0,
     'L0_ffn_wg_w': 22.903,
     'L0_ffn_wg_b': 200.0}
    for name, (base, spread) in spreads.items():
        noise = np.random.default_rng([zlib.crc32(name.encode()), seed]).standard_normal(out[name].shape)
        drawn = base * np.exp(spread * noise) if base else spread * noise
        out[name] = jnp.asarray(drawn.astype(out[name].dtype))
    for name, factor in factors.items():
        out[name] = (out[name] * factor).astype(out[name].dtype)
    return out
```

```python
import concourse.bass as bass
from concourse import mybir
from contextlib import ExitStack

FP32 = mybir.dt.float32
I32 = mybir.dt.int32
U32 = mybir.dt.uint32
ALU = mybir.AluOpType
ACT = mybir.ActivationFunctionType
AX = mybir.AxisListType.X

P = 128
SEQS, SEQ = 16, 512
T4 = SEQ // P
TILES = SEQS * T4
HID = 4
E = 8
HEADS = 16
HD = P // HEADS
ROWS = 512
CAP = TILES * P + ROWS
DUMMY = E * CAP
XTILES = 2 * TILES * P // ROWS + E
WUP = 2 * HID * P + 2 * HID
WCOLS = WUP + HID * P + P
LN_EPS = 1e-5
K_CLAMP = 60.0
SCALE = float(HD) ** -0.5

(G1, B1, G2, B2, TM1, CM1, TD, TF, TM2, CM2, QB1, KB1, VB, GB) = range(14)
NVEC = 14
C_ID, C_UP, C_HEAD = 0, 128, 256
C_IM8 = 384
C_TILE0 = C_IM8 + E
C_J = C_TILE0 + 16
C_BASE = C_J + XTILES
NCONST = C_BASE + E


def past(i, n):
    return not isinstance(i, int) or i >= n


def pipelined(eng, n, *parts):
    lag_max = max(lag for lag, _ in parts)
    head = (lag_max + 3) // 2 * 2
    end = n // 2 * 2

    def step(s):
        for lag, part in parts:
            if 0 <= s - lag < n:
                part(s - lag, (s - lag) % 2, (s - lag) // 2)

    for s in range(min(head, end)):
        step(s)
    if head < end:
        with eng.Fori(head // 2, end // 2) as h:
            for u in range(2):
                for lag, part in parts:
                    k = u - lag
                    part(h * 2 + k, k % 2, h + k // 2)
    for s in range(end, n + lag_max):
        step(s)


class Memory:

    def __init__(self, nc, ctx):
        def sb(name, shape, dt=FP32):
            return ctx.enter_context(nc.sbuf_tensor(name, shape, dt))

        self.X = sb("residual", [P, TILES, P])
        self.vec = sb("vectors", [P, NVEC])
        self.const = sb("constants", [P, NCONST])
        self.wa = sb("mix_weights", [P, 5 * P + 2 * HID * P])
        self.wb = sb("attention_weights", [P, 7 * P])
        self.wr = sb("router_weights", [P, E])
        self.rows = sb("bias_rows", [1, 3, T4 * P])
        self.ones = sb("ones", [P, P])
        self.slot = sb("slots_in", [P, TILES, 2])
        self.pos = sb("slots_out", [P, TILES, 2], U32)
        self.gates = sb("gates", [P, TILES, 2])
        self.carry = sb("next_slot", [P, E])
        self.tile_expert = sb("tile_expert", [1, XTILES], I32)
        self.tile_row = sb("tile_row", [1, XTILES], I32)
        self.tail_row = sb("tail_row", [1, E], I32)
        self.zeros = sb("zeros", [P, ROWS // P * P])
        self.half = sb("minus_half", [P, T4])
        self.banks = [ctx.enter_context(nc.psum_tensor(f"bank{b}", [P, 512], FP32)) for b in range(8)]
        self.carrier = ctx.enter_context(nc.semaphore("carrier"))
        self.ident = self.const[:, C_ID:C_ID + P]

    def col(self, k):
        return self.vec[:, k:k + 1]


def phase(nc, tag):
    ctx = ExitStack()

    def sb(name, shape, dt=FP32):
        return ctx.enter_context(nc.sbuf_tensor(f"{tag}_{name}", shape, dt))

    def sem(name):
        return ctx.enter_context(nc.semaphore(f"{tag}_{name}"))

    return ctx, sb, sem


def setup(nc, m, x, vecs, consts, wa, wb, wr, rows):
    ctx, sb, sem = phase(nc, "setup")
    with ctx:
        loaded = sem("loaded")
        block = ctx.enter_context(nc.Block())
        xv = x.rearrange("(t p) d -> p t d", p=P)

        @block.sync
        def _(sp):
            for q in range(4):
                sp.dma_start(m.X[:, 16 * q:16 * q + 16, :], xv[:, 16 * q:16 * q + 16, :]).then_inc(loaded, 16)
            sp.dma_start(m.rows[:], rows).then_inc(loaded, 16)
            sp.wait_ge(loaded, 10 * 16)

        @block.scalar
        def _(act):
            act.dma_start(m.vec[:], vecs).then_inc(loaded, 16)
            act.dma_start(m.const[:], consts).then_inc(loaded, 16)
            act.dma_start(m.wa[:], wa).then_inc(loaded, 16)
            act.dma_start(m.wb[:], wb).then_inc(loaded, 16)
            act.dma_start(m.wr[:], wr).then_inc(loaded, 16)
            act.wait_ge(loaded, 10 * 16)

        @block.gpsimd
        def _(pool):
            pool.memset(m.ones[:], 1.0)
            pool.memset(m.zeros[:], 0.0)
            pool.memset(m.half[:], -0.5)


def time_mix(nc, m, XP):
    ctx, sb, sem = phase(nc, "tmix")
    with ctx:
        coef = sb("coefficients", [P, 8])
        TMG, TMB, CPREV, CNEXT, ED, EU, TMP = range(7)
        decay = sb("decay", [P, 2, SEQ + 1])
        st = [sb(f"stats{b}", [P, T4, 6]) for b in range(2)]
        mv = [sb(f"mean_var{b}", [P, T4, 2]) for b in range(2)]
        rv = [sb(f"var_eps{b}", [P, T4]) for b in range(2)]
        rs = [sb(f"rstd{b}", [P, T4]) for b in range(2)]
        nt = [sb(f"normed{b}", [P, T4, P]) for b in range(2)]
        xf = [sb(f"x_fm{b}", [P, SEQ + 2]) for b in range(2)]
        xm = [sb(f"x_mixed{b}", [P, SEQ]) for b in range(2)]
        kc = sb("k_clamped", [P, SEQ])
        kk = [sb(f"k_kv{b}", [P, 2, SEQ + 1]) for b in range(2)]
        ab = sb("a_b", [P, 2, SEQ + 1])
        nd = sb("num_den", [P, 2, SEQ])
        th = [sb(f"tanh_r{b}", [P, SEQ]) for b in range(2)]
        rd = sb("one_over_den", [P, SEQ])
        y = [sb(f"y_fm{b}", [P, SEQ]) for b in range(2)]
        psT, psK, psV, psR, psO = m.banks[0:2], m.banks[2], m.banks[3], m.banks[4], m.banks[5:7]

        cleared, coef_a, coef_b, decay_ready = sem("cleared"), sem("coef_a"), sem("coef_b"), sem("decay_ready")
        stats_done, aggr_done, var_ready, rstd_ready = sem("stats_done"), sem("aggr_done"), sem("var_ready"), sem("rstd_ready")
        normed, transposed, x_ready, scaled = sem("normed"), sem("transposed"), sem("x_ready"), sem("scaled")
        mixed_prev, mixed, kvr_done = sem("mixed_prev"), sem("mixed"), sem("kvr_done")
        k_clamped, k_ready, tanh_ready, kv_ready = sem("k_clamped"), sem("k_ready"), sem("tanh_ready"), sem("kv_ready")
        scanned, num_den, recip_done, u_ready, y_ready = sem("scanned"), sem("num_den"), sem("recip_done"), sem("u_ready"), sem("y_ready")
        o_done, xp_ready = sem("o_done"), sem("xp_ready")
        block = ctx.enter_context(nc.Block())
        W = {k: m.wa[:, i * P:(i + 1) * P] for i, k in enumerate("kvro")}

        @block.gpsimd
        def _(pool):
            for b in range(2):
                pool.memset(xf[b][:, 0:1], 0.0)
                pool.memset(xf[b][:, SEQ + 1:SEQ + 2], 0.0)
                pool.memset(kk[b][:, :, 0:1], 0.0)
            pool.memset(decay[:, :, 0:1], 0.0).then_inc(cleared, 1)

            def rstd(i, b, h):
                pool.wait_ge(var_ready, i + 1)
                pool.tensor_tensor(rs[b][:], rv[b][:], m.half[:], ALU.pow).then_inc(rstd_ready, 1)

            pipelined(pool, SEQS, (0, rstd))

        @block.vector
        def _(dve):
            dve.tensor_tensor(coef[:, TMG:TMG + 1], m.col(TM1), m.col(G1), ALU.mult)
            dve.tensor_tensor(coef[:, TMB:TMB + 1], m.col(TM1), m.col(B1), ALU.mult)
            dve.tensor_scalar(coef[:, CPREV:CPREV + 1], m.col(TM1), -1.0, 1.0, ALU.mult, ALU.add)
            dve.tensor_copy(coef[:, CNEXT:CNEXT + 1], m.col(CM1)).then_inc(coef_a, 1)
            dve.wait_ge(coef_a, 1)
            dve.tensor_tensor(coef[0:64, CPREV:CPREV + 1], coef[0:64, CPREV:CPREV + 1], m.vec[0:64, CM1:CM1 + 1], ALU.add).then_inc(coef_a, 1)
            dve.wait_ge(coef_b, 3)
            dve.tensor_scalar(decay[:, 0, 1:], m.zeros[:], coef[:, ED:ED + 1], None, ALU.add)
            dve.tensor_scalar(decay[:, 1, 1:], m.zeros[:], coef[:, ED:ED + 1], None, ALU.add).then_inc(decay_ready, 1)
            dve.wait_ge(cleared, 1)
            dve.wait_ge(coef_a, 2)
            dve.wait_ge(decay_ready, 1)

            def stats(i, b, h):
                for j in range(T4):
                    last = dve.bn_stats(st[b][:, j, :], m.X[:, i * T4 + j, :])
                last.then_inc(stats_done, 1)

            def aggregate(i, b, h):
                if isinstance(i, int):
                    dve.wait_ge(stats_done, i + 1)
                for j in range(T4):
                    last = dve.bn_aggr(mv[b][:, j, :], st[b][:, j, :])
                last.then_inc(aggr_done, 1)
                dve.wait_ge(aggr_done, i + 1)
                dve.tensor_scalar(rv[b][:], mv[b][:, :, 1], 1.0 + LN_EPS, LN_EPS * LN_EPS, ALU.mult, ALU.add).then_inc(var_ready, 1)

            def normalize(i, b, h):
                dve.wait_ge(stats_done, min(i + 2, SEQS) if isinstance(i, int) else i + 2)
                dve.wait_ge(rstd_ready, i + 1)
                if past(i, 2):
                    dve.wait_ge(transposed, i - 1)
                for j in range(T4):
                    last = dve.tensor_scalar(nt[b][:, j, :], m.X[:, i * T4 + j, :], mv[b][:, j, 0:1], rs[b][:, j:j + 1],
                                             ALU.subtract, ALU.mult)
                last.then_inc(normed, 1)

            def mix(i, b, h):
                dve.wait_ge(x_ready, i + 1)
                dve.wait_ge(scaled, i + 1)
                dve.scalar_tensor_tensor(xm[b][:], xf[b][:, 0:SEQ], coef[:, CPREV:CPREV + 1], xm[b][:],
                                         ALU.mult, ALU.add).then_inc(mixed_prev, 1)
                dve.wait_ge(mixed_prev, i + 1)
                dve.scalar_tensor_tensor(xm[b][64:P, :], xf[b][64:P, 2:], coef[64:P, CNEXT:CNEXT + 1], xm[b][64:P, :],
                                         ALU.mult, ALU.add).then_inc(mixed, 1)

            def wkv(i, b, h):
                dve.wait_ge(kvr_done, i + 1)
                if past(i, 1):
                    dve.wait_ge(k_ready, i)
                dve.tensor_scalar(kc[:], psK[:], K_CLAMP, None, ALU.min).then_inc(k_clamped, 1)
                dve.wait_ge(k_ready, i + 1)
                dve.tensor_tensor(kk[b][:, 0, 1:], kk[b][:, 1, 1:], psV[:], ALU.mult).then_inc(kv_ready, 1)
                dve.wait_ge(kv_ready, i + 1)
                dve.tensor_tensor_scan(ab[:].rearrange("p s t -> p (s t)"), decay[:].rearrange("p s t -> p (s t)"),
                                       kk[b][:].rearrange("p s t -> p (s t)"), 0.0, ALU.mult, ALU.add).then_inc(scanned, 1)
                dve.wait_ge(scanned, i + 1)
                dve.scalar_tensor_tensor(nd[:], kk[b][:, :, 1:], coef[:, EU:EU + 1], ab[:, :, 0:SEQ],
                                         ALU.mult, ALU.add).then_inc(num_den, 1)
                dve.wait_ge(num_den, i + 1)
                dve.reciprocal(rd[:], nd[:, 1, :]).then_inc(recip_done, 1)
                dve.wait_ge(tanh_ready, i + 1)
                if past(i, 2):
                    dve.wait_ge(o_done, i - 1)
                dve.scalar_tensor_tensor(y[b][:], th[b][:], 1.0, nd[:, 0, :], ALU.add, ALU.mult).then_inc(u_ready, 1)
                dve.wait_ge(recip_done, i + 1)
                dve.wait_ge(u_ready, i + 1)
                dve.scalar_tensor_tensor(y[b][:], y[b][:], 0.5, rd[:], ALU.mult, ALU.mult).then_inc(y_ready, 1)

            pipelined(dve, SEQS, (0, stats), (1, normalize), (0, aggregate), (2, wkv), (1, mix))

        @block.scalar
        def _(act):
            act.activation(coef[:, ED:ED + 1], m.col(TD), ACT.Exp).then_inc(coef_b, 1)
            act.activation(coef[:, EU:EU + 1], m.col(TF), ACT.Exp).then_inc(coef_b, 1)
            act.wait_ge(coef_b, 2)
            act.activation(coef[:, ED:ED + 1], coef[:, ED:ED + 1], ACT.Exp, scale=-1.0).then_inc(coef_b, 1)
            act.wait_ge(coef_a, 2)

            def affine(i, b, h):
                act.wait_ge(transposed, i + 1)
                if past(i, 2):
                    act.wait_ge(o_done, i - 1)
                act.activation(xf[b][:, 1:SEQ + 1], psT[b][:], ACT.Identity, bias=m.col(B1), scale=m.col(G1)).then_inc(x_ready, 1)
                if past(i, 2):
                    act.wait_ge(kvr_done, i - 1)
                act.activation(xm[b][:], psT[b][:], ACT.Identity, bias=coef[:, TMB:TMB + 1],
                               scale=coef[:, TMG:TMG + 1]).then_inc(scaled, 1)

            def exponentials(i, b, h):
                act.wait_ge(k_clamped, i + 1)
                if past(i, 2):
                    act.wait_ge(num_den, i - 1)
                act.activation(kk[b][:, 1, 1:], kc[:], ACT.Exp).then_inc(k_ready, 1)
                if past(i, 2):
                    act.wait_ge(y_ready, i - 1)
                act.activation(th[b][:], psR[:], ACT.Tanh, scale=0.5).then_inc(tanh_ready, 1)

            def store(i, b, h):
                act.wait_ge(o_done, i + 1)
                act.activation(XP[:, bass.ds(i * T4, T4), :] if not isinstance(i, int) else XP[:, i * T4:i * T4 + T4, :],
                               psO[b][:].rearrange("p (j c) -> p j c", c=P), ACT.Copy).then_inc(xp_ready, 1)

            pipelined(act, SEQS, (1, affine), (2, exponentials), (2, store))

        @block.tensor
        def _(pe):
            def transpose(i, b, h):
                pe.wait_ge(normed, i + 1)
                if past(i, 2):
                    pe.wait_ge(scaled, i - 1)
                for j in range(T4):
                    last = pe.transpose(psT[b][:, j * P:(j + 1) * P], nt[b][:, j, :], m.ident)
                last.then_inc(transposed, 1)

            def kvr(i, b, h):
                pe.wait_ge(mixed, i + 1)
                if past(i, 1):
                    pe.wait_ge(tanh_ready, i)
                if past(i, 1):
                    pe.wait_ge(kv_ready, i)
                pe.matmul(psK[:], W["k"], xm[b][:], start=True, stop=True)
                pe.matmul(psV[:], W["v"], xm[b][:], start=True, stop=True)
                pe.matmul(psR[:], W["r"], xm[b][:], start=True, stop=True).then_inc(kvr_done, 1)

            def project(i, b, h):
                pe.wait_ge(y_ready, i + 1)
                if past(i, 2):
                    pe.wait_ge(xp_ready, i - 1)
                for j in range(T4):
                    out = psO[b][:, j * P:(j + 1) * P]
                    pe.matmul(out, y[b][:, j * P:(j + 1) * P], W["o"], start=True, stop=False)
                    last = pe.matmul(out, xf[b][:, 1 + j * P:1 + (j + 1) * P], m.ident, start=False, stop=True)
                last.then_inc(o_done, 1)

            pipelined(pe, SEQS, (1, transpose), (2, project), (1, kvr))


def channel_mix(nc, m, XP):
    ctx, sb, sem = phase(nc, "cmix")
    with ctx:
        coef = sb("coefficients", [P, 4])
        TMG, TMB, CPREV, CNEXT = range(4)
        st = [sb(f"stats{b}", [P, T4, 6]) for b in range(2)]
        mv = [sb(f"mean_var{b}", [P, T4, 2]) for b in range(2)]
        rv = [sb(f"var_eps{b}", [P, T4]) for b in range(2)]
        rs = [sb(f"rstd{b}", [P, T4]) for b in range(2)]
        nt = [sb(f"normed{b}", [P, T4, P]) for b in range(2)]
        xf = [sb(f"x_fm{b}", [P, SEQ + 2]) for b in range(2)]
        xm = [sb(f"x_mixed{b}", [P, SEQ]) for b in range(2)]
        rl = [sb(f"relu{b}", [P, HID, SEQ]) for b in range(2)]
        kq = [sb(f"k_fm{b}", [P, HID, SEQ]) for b in range(2)]
        th = sb("tanh_r", [P, SEQ])
        u = sb("gated", [P, SEQ])
        w = sb("gated_plus_x", [P, SEQ])
        psT, psF, psKV, psG, psX = m.banks[0:2], m.banks[2:4], m.banks[4], m.banks[5], m.banks[6]

        cleared, coef_a = sem("cleared"), sem("coef_a")
        stats_done, aggr_done, var_ready, rstd_ready = sem("stats_done"), sem("aggr_done"), sem("var_ready"), sem("rstd_ready")
        normed, transposed, x_ready, scaled = sem("normed"), sem("transposed"), sem("x_ready"), sem("scaled")
        mixed_prev, mixed = sem("mixed_prev"), sem("mixed")
        fk_done, relu_done, k_ready = sem("fk_done"), sem("relu_done"), sem("k_ready")
        out_done, tanh_ready, gated, summed, x_updated = sem("out_done"), sem("tanh_ready"), sem("gated"), sem("summed"), sem("x_updated")
        block = ctx.enter_context(nc.Block())
        WR = m.wa[:, 4 * P:5 * P]
        FK = m.wa[:, 5 * P:5 * P + HID * P]
        FV = m.wa[:, (5 + HID) * P:]

        @block.gpsimd
        def _(pool):
            for b in range(2):
                pool.memset(xf[b][:, 0:1], 0.0)
                last = pool.memset(xf[b][:, SEQ + 1:SEQ + 2], 0.0)
            last.then_inc(cleared, 1)

            def rstd(i, b, h):
                pool.wait_ge(var_ready, i + 1)
                pool.tensor_tensor(rs[b][:], rv[b][:], m.half[:], ALU.pow).then_inc(rstd_ready, 1)

            def square(i, b, h):
                if past(i, 2):
                    pool.wait_ge(out_done, i - 1)
                for c in range(HID):
                    pool.wait_ge(relu_done, i * HID + c + 1)
                    pool.tensor_tensor(kq[b][:, c, :], rl[b][:, c, :], rl[b][:, c, :], ALU.mult).then_inc(k_ready, 1)

            pipelined(pool, SEQS, (0, rstd), (1, square))

        @block.vector
        def _(dve):
            dve.tensor_tensor(coef[:, TMG:TMG + 1], m.col(TM2), m.col(G2), ALU.mult)
            dve.tensor_tensor(coef[:, TMB:TMB + 1], m.col(TM2), m.col(B2), ALU.mult)
            dve.tensor_scalar(coef[:, CPREV:CPREV + 1], m.col(TM2), -1.0, 1.0, ALU.mult, ALU.add)
            dve.tensor_copy(coef[:, CNEXT:CNEXT + 1], m.col(CM2)).then_inc(coef_a, 1)
            dve.wait_ge(coef_a, 1)
            dve.tensor_tensor(coef[0:64, CPREV:CPREV + 1], coef[0:64, CPREV:CPREV + 1], m.vec[0:64, CM2:CM2 + 1], ALU.add).then_inc(coef_a, 1)
            dve.wait_ge(cleared, 1)
            dve.wait_ge(coef_a, 2)

            def stats(i, b, h):
                for j in range(T4):
                    last = dve.bn_stats(st[b][:, j, :], XP[:, i * T4 + j, :])
                last.then_inc(stats_done, 1)

            def aggregate(i, b, h):
                if isinstance(i, int):
                    dve.wait_ge(stats_done, i + 1)
                for j in range(T4):
                    last = dve.bn_aggr(mv[b][:, j, :], st[b][:, j, :])
                last.then_inc(aggr_done, 1)
                dve.wait_ge(aggr_done, i + 1)
                dve.tensor_scalar(rv[b][:], mv[b][:, :, 1], 1.0, LN_EPS, ALU.mult, ALU.add).then_inc(var_ready, 1)

            def normalize(i, b, h):
                dve.wait_ge(stats_done, min(i + 2, SEQS) if isinstance(i, int) else i + 2)
                dve.wait_ge(rstd_ready, i + 1)
                if past(i, 2):
                    dve.wait_ge(transposed, i - 1)
                for j in range(T4):
                    last = dve.tensor_scalar(nt[b][:, j, :], XP[:, i * T4 + j, :], mv[b][:, j, 0:1], rs[b][:, j:j + 1],
                                             ALU.subtract, ALU.mult)
                last.then_inc(normed, 1)

            def mix(i, b, h):
                dve.wait_ge(x_ready, i + 1)
                dve.wait_ge(scaled, i + 1)
                dve.scalar_tensor_tensor(xm[b][:], xf[b][:, 0:SEQ], coef[:, CPREV:CPREV + 1], xm[b][:],
                                         ALU.mult, ALU.add).then_inc(mixed_prev, 1)
                dve.wait_ge(mixed_prev, i + 1)
                dve.scalar_tensor_tensor(xm[b][64:P, :], xf[b][64:P, 2:], coef[64:P, CNEXT:CNEXT + 1], xm[b][64:P, :],
                                         ALU.mult, ALU.add).then_inc(mixed, 1)

            def update(i, b, h):
                dve.wait_ge(tanh_ready, i + 1)
                dve.scalar_tensor_tensor(u[:], th[:], 1.0, psKV[:], ALU.add, ALU.mult).then_inc(gated, 1)
                dve.wait_ge(gated, i + 1)
                dve.scalar_tensor_tensor(w[:], u[:], 0.5, psX[:], ALU.mult, ALU.add).then_inc(summed, 1)
                dve.wait_ge(summed, i + 1)
                xs = tiles(m.X, i)
                dve.tensor_tensor(xs, w[:].rearrange("p (j c) -> p j c", c=P), xs, ALU.add).then_inc(x_updated, 1)

            pipelined(dve, SEQS, (0, stats), (1, normalize), (0, aggregate), (1, mix), (2, update))

        @block.scalar
        def _(act):
            act.wait_ge(coef_a, 2)

            def affine(i, b, h):
                act.wait_ge(transposed, i + 1)
                if past(i, 2):
                    act.wait_ge(out_done, i - 1)
                act.activation(xf[b][:, 1:SEQ + 1], psT[b][:], ACT.Identity, bias=m.col(B2), scale=m.col(G2)).then_inc(x_ready, 1)
                act.activation(xm[b][:], psT[b][:], ACT.Identity, bias=coef[:, TMB:TMB + 1],
                               scale=coef[:, TMG:TMG + 1]).then_inc(scaled, 1)

            def relu(i, b, h):
                if past(i, 2):
                    act.wait_ge(k_ready, (i - 1) * HID)
                for c in range(HID):
                    act.wait_ge(fk_done, i * HID + c + 1)
                    act.activation(rl[b][:, c, :], psF[c % 2][:], ACT.Relu).then_inc(relu_done, 1)

            def gate(i, b, h):
                act.wait_ge(out_done, i + 1)
                if past(i, 1):
                    act.wait_ge(gated, i)
                act.activation(th[:], psG[:], ACT.Tanh, scale=0.5).then_inc(tanh_ready, 1)

            pipelined(act, SEQS, (1, affine), (2, gate), (1, relu))

        @block.tensor
        def _(pe):
            def transpose(i, b, h):
                pe.wait_ge(normed, i + 1)
                if past(i, 2):
                    pe.wait_ge(scaled, i - 1)
                for j in range(T4):
                    last = pe.transpose(psT[b][:, j * P:(j + 1) * P], nt[b][:, j, :], m.ident)
                last.then_inc(transposed, 1)

            def up(i, b, h):
                pe.wait_ge(mixed, i + 1)
                for c in range(HID):
                    if past(i, 1) or c > 1:
                        pe.wait_ge(relu_done, i * HID + c - 1)
                    pe.matmul(psF[c % 2][:], FK[:, c * P:(c + 1) * P], xm[b][:], start=True, stop=True).then_inc(fk_done, 1)

            def down(i, b, h):
                pe.wait_ge(k_ready, (i + 1) * HID)
                if past(i, 1):
                    pe.wait_ge(summed, i)
                for j in range(T4):
                    for c in range(HID):
                        pe.matmul(psKV[:, j * P:(j + 1) * P], kq[b][:, c, j * P:(j + 1) * P], FV[:, c * P:(c + 1) * P],
                                  start=c == 0, stop=c == HID - 1)
                for j in range(T4):
                    pe.matmul(psG[:, j * P:(j + 1) * P], xm[b][:, j * P:(j + 1) * P], WR, start=True, stop=True)
                for j in range(T4):
                    last = pe.matmul(psX[:, j * P:(j + 1) * P], xf[b][:, 1 + j * P:1 + (j + 1) * P], m.ident,
                                     start=True, stop=True)
                last.then_inc(out_done, 1)

            pipelined(pe, SEQS, (0, lambda i, b, h: None), (1, transpose), (2, down), (1, up))


def tiles(t, i):
    if isinstance(i, int):
        return t[:, i * T4:(i + 1) * T4, :]
    return t[:, bass.ds(i * T4, T4), :]


def route(nc, m, xs, tag):
    ctx, sb, sem = phase(nc, tag)
    with ctx:
        st = [sb(f"stats{b}", [P, T4, 6]) for b in range(2)]
        mv = [sb(f"mean_var{b}", [P, T4, 2]) for b in range(2)]
        rv = [sb(f"var_eps{b}", [P, T4]) for b in range(2)]
        rs = [sb(f"rstd{b}", [P, T4]) for b in range(2)]
        nt = [sb(f"normed{b}", [P, T4, P]) for b in range(2)]
        xf = [sb(f"x_fm{b}", [P, SEQ]) for b in range(2)]
        lg = sb("logits", [P, T4, E])
        m1 = sb("max1", [P, T4])
        m2 = sb("max2", [P, T4])
        first = sb("first", [P, T4, 2])
        eq = sb("equals", [P, T4, E])
        mask = [sb(f"mask{k}", [P, T4, E]) for k in range(2)]
        lg2 = sb("logits2", [P, T4, E])
        both = sb("both_masks", [P, T4, E])
        d = [sb(f"less_max{b}", [P, T4, E]) for b in range(2)]
        d2 = [sb(f"max2_less_max1{b}", [P, T4]) for b in range(2)]
        ex = sb("exps", [P, T4, E])
        e2 = sb("exp2", [P, T4])
        ssum = sb("exp_sum", [P, T4])
        inv = sb("exp_sum_inverse", [P, T4])
        incl = sb("slots_after", [P, E, T4])
        slot = sb("slot", [P, T4, E])
        pk = [sb(f"slot_masked{k}", [P, T4, E]) for k in range(2)]
        pf = sb("slots_float", [P, T4, 2])
        idx = [sb(f"slot_lists{b}", [P, T4, 2], U32) for b in range(2)]
        tile_w = sb("tile_work", [1, 6, XTILES, E])
        small = sb("small_work", [P, 7, E])
        cmp16 = sb("count_compare", [P, E, 16])
        moved = [sb(f"slot_moved{k}", [P, TILES * 2]) for k in range(2)]
        trow = sb("tile_rows", [1, 4, XTILES])
        psT, psL, psC = m.banks[0:2], m.banks[2], m.banks[3]
        im8 = m.const[:, C_IM8:C_IM8 + E].unsqueeze(1).to_broadcast([P, T4, E])

        stats_done, aggr_done, var_ready, rstd_ready = sem("stats_done"), sem("aggr_done"), sem("var_ready"), sem("rstd_ready")
        normed, transposed, x_ready, logits_done = sem("normed"), sem("transposed"), sem("x_ready"), sem("logits_done")
        chain = sem("dve_step")
        d_ready, exps_done, both_ready, counted = sem("less_max_ready"), sem("exps_done"), sem("both_ready"), sem("counted")
        count_read = sem("count_read")
        idx_ready = sem("idx_ready")
        sent = [sem(f"sent{b}") for b in range(2)]
        carry_set, rows_ready, zeroed = sem("carry_set"), sem("rows_ready"), sem("zeroed")
        block = ctx.enter_context(nc.Block())
        STEPS = 19

        @block.gpsimd
        def _(pool):
            def rstd(i, b, h):
                pool.wait_ge(var_ready, i + 1)
                pool.tensor_tensor(rs[b][:], rv[b][:], m.half[:], ALU.pow).then_inc(rstd_ready, 1)

            def send(i, b, h):
                pool.wait_ge(idx_ready, i + 1)
                pool.sem_inc(m.carrier, 1)
                for j in range(T4):
                    for k in range(2):
                        pool.indirect_dma_start(xs, bass.IndirectOffsetOnAxis(ap=idx[b][:, j, k:k + 1], axis=0),
                                                nt[b][:, j, :], None).then_inc(sent[b], 16)

            pipelined(pool, SEQS, (0, rstd), (1, send))
            for b in range(2):
                pool.wait_ge(sent[b], SEQS // 2 * T4 * 2 * 16)

        @block.vector
        def _(dve):
            def stats(i, b, h):
                for j in range(T4):
                    last = dve.bn_stats(st[b][:, j, :], m.X[:, i * T4 + j, :])
                last.then_inc(stats_done, 1)

            def aggregate(i, b, h):
                if isinstance(i, int):
                    dve.wait_ge(stats_done, i + 1)
                for j in range(T4):
                    last = dve.bn_aggr(mv[b][:, j, :], st[b][:, j, :])
                last.then_inc(aggr_done, 1)
                dve.wait_ge(aggr_done, i + 1)
                dve.tensor_scalar(rv[b][:], mv[b][:, :, 1], 1.0, LN_EPS, ALU.mult, ALU.add).then_inc(var_ready, 1)

            def normalize(i, b, h):
                dve.wait_ge(stats_done, min(i + 2, SEQS) if isinstance(i, int) else i + 2)
                dve.wait_ge(rstd_ready, i + 1)
                if past(h, 1):
                    dve.wait_ge(sent[b], h * (T4 * 2 * 16))
                for j in range(T4):
                    last = dve.tensor_scalar(nt[b][:, j, :], m.X[:, i * T4 + j, :], mv[b][:, j, 0:1], rs[b][:, j:j + 1],
                                             ALU.subtract, ALU.mult)
                last.then_inc(normed, 1)

            def rank(i, b, h):
                n = [0]

                def done(ins):
                    n[0] += 1
                    ins.then_inc(chain, 1)
                    dve.wait_ge(chain, i * STEPS + n[0])

                def over(x):
                    return x.unsqueeze(2).to_broadcast([P, T4, E])

                dve.wait_ge(logits_done, i + 1)
                done(dve.tensor_copy(lg[:], psL[:, 0:T4 * E].rearrange("p (j e) -> p j e", e=E)))
                done(dve.tensor_reduce(m1[:], lg[:], AX, ALU.max))
                dve.tensor_tensor(d[b][:], lg[:], over(m1[:]), ALU.subtract)
                done(dve.tensor_tensor(eq[:], lg[:], over(m1[:]), ALU.is_equal))
                done(dve.tensor_tensor(eq[:], eq[:], im8, ALU.mult))
                done(dve.tensor_reduce(first[:, :, 0], eq[:], AX, ALU.min))
                done(dve.tensor_tensor(mask[0][:], im8, over(first[:, :, 0]), ALU.is_equal))
                done(dve.scalar_tensor_tensor(lg2[:], mask[0][:], -3e38, lg[:], ALU.mult, ALU.add))
                done(dve.tensor_reduce(m2[:], lg2[:], AX, ALU.max))
                dve.tensor_tensor(d2[b][:], m2[:], m1[:], ALU.subtract).then_inc(d_ready, 1)
                done(dve.tensor_tensor(eq[:], lg2[:], over(m2[:]), ALU.is_equal))
                done(dve.tensor_tensor(eq[:], eq[:], im8, ALU.mult))
                done(dve.tensor_reduce(first[:, :, 1], eq[:], AX, ALU.min))
                done(dve.tensor_tensor(mask[1][:], im8, over(first[:, :, 1]), ALU.is_equal))
                dve.tensor_tensor(both[:], mask[0][:], mask[1][:], ALU.add).then_inc(both_ready, 1)
                dve.wait_ge(exps_done, i + 1)
                done(dve.tensor_reduce(ssum[:], ex[:], AX, ALU.add))
                done(dve.reciprocal(inv[:], ssum[:]))
                g = tiles(m.gates, i)
                dve.tensor_copy(g[:, :, 0], inv[:])
                dve.tensor_tensor(g[:, :, 1], e2[:], inv[:], ALU.mult)
                dve.wait_ge(counted, i + 1)
                total = psC[:, T4 * E:2 * T4 * E].rearrange("p (j e) -> p e j", e=E)
                for e in range(E):
                    last = dve.tensor_tensor_scan(incl[:, e, :], m.ones[:, 0:T4], total[:, e, :], m.carry[:, e:e + 1],
                                                  ALU.mult, ALU.add)
                done(last)
                dve.tensor_copy(m.carry[:], incl[:, :, T4 - 1])
                done(dve.tensor_tensor(slot[:], incl[:].rearrange("p e j -> p j e"), total.rearrange("p e j -> p j e"), ALU.subtract))
                done(dve.tensor_tensor(slot[:], slot[:], psC[:, 0:T4 * E].rearrange("p (j e) -> p j e", e=E), ALU.add))
                dve.tensor_tensor(pk[0][:], slot[:], mask[0][:], ALU.mult).then_inc(count_read, 1)
                done(dve.tensor_tensor(pk[1][:], slot[:], mask[1][:], ALU.mult))
                dve.tensor_reduce(pf[:, :, 0], pk[0][:], AX, ALU.add)
                done(dve.tensor_reduce(pf[:, :, 1], pk[1][:], AX, ALU.add))
                assert n[0] == STEPS, n[0]
                dve.tensor_copy(tiles(m.slot, i), pf[:])
                dve.tensor_copy(idx[b][:], pf[:]).then_inc(idx_ready, 1)

            dve.tensor_copy(m.carry[:], m.const[:, C_BASE:C_BASE + E]).then_inc(carry_set, 1)
            dve.wait_ge(carry_set, 1)
            pipelined(dve, SEQS, (0, stats), (1, normalize), (0, aggregate), (1, rank))

            n = [0]

            def link(ins):
                n[0] += 1
                ins.then_inc(chain, 1)
                dve.wait_ge(chain, SEQS * STEPS + n[0])

            dve.wait_ge(idx_ready, SEQS)
            base = m.const[:, C_BASE:C_BASE + E]
            cnt, nt8, inc8, exc8, rb, drop = (small[:, k, :] for k in range(6))
            dve.tensor_copy(m.tail_row[:], m.carry[0:1, :])
            link(dve.tensor_tensor(cnt, m.carry[:], base, ALU.subtract))
            link(dve.tensor_tensor(cmp16[:], cnt.unsqueeze(2).to_broadcast([P, E, 16]),
                                   m.const[:, C_TILE0:C_TILE0 + 16].unsqueeze(1).to_broadcast([P, E, 16]), ALU.is_gt))
            link(dve.tensor_reduce(nt8, cmp16[:], AX, ALU.add))
            link(dve.tensor_tensor_scan(inc8, m.ones[:, 0:E], nt8, 0.0, ALU.mult, ALU.add))
            link(dve.tensor_tensor(exc8, inc8, nt8, ALU.subtract))
            link(dve.scalar_tensor_tensor(rb, exc8, -float(ROWS), base, ALU.mult, ALU.add))
            link(dve.tensor_tensor(drop[:, 1:E], rb[:, 0:E - 1], rb[:, 1:E], ALU.subtract))
            last_slot = m.slot[:].rearrange("p t k -> p (t k)")
            for e in range(1, E):
                link(dve.tensor_scalar(moved[0][:], m.slot[:].rearrange("p t k -> p (t k)"), float(e * CAP), drop[:, e:e + 1],
                                       ALU.is_ge, ALU.mult))
                link(dve.tensor_tensor(moved[1][:], moved[0][:], last_slot, ALU.add))
                last_slot = moved[1][:]
            dve.tensor_copy(m.pos[:].rearrange("p t k -> p (t k)"), last_slot)
            jj = m.const[0:1, C_J:C_J + XTILES].unsqueeze(2).to_broadcast([1, XTILES, E])

            def by_tile(x):
                return x.unsqueeze(1).to_broadcast([1, XTILES, E])

            after, begun, own, roff, sel = (tile_w[:, k] for k in range(5))
            dve.tensor_tensor(after, jj, by_tile(inc8[0:1]), ALU.is_ge)
            dve.tensor_scalar(trow[:, 0, :], m.const[0:1, C_J:C_J + XTILES], float(ROWS), -float(DUMMY), ALU.mult, ALU.add)
            link(dve.tensor_tensor(begun, jj, by_tile(exc8[0:1]), ALU.is_ge))
            link(dve.tensor_tensor(own, begun, after, ALU.subtract))
            link(dve.tensor_tensor(roff, trow[:, 0, :].unsqueeze(2).to_broadcast([1, XTILES, E]), by_tile(rb[0:1]), ALU.add))
            link(dve.tensor_tensor(sel, own, roff, ALU.mult))
            dve.tensor_reduce(trow[:, 1, :], sel, AX, ALU.add)
            link(dve.tensor_reduce(trow[:, 2, :], after, AX, ALU.add))
            dve.tensor_scalar(m.tile_row[:], trow[:, 1, :], float(DUMMY), None, ALU.add)
            dve.tensor_scalar(m.tile_expert[:], trow[:, 2, :], float(E - 1), None, ALU.min).then_inc(rows_ready, 1)

        @block.scalar
        def _(act):
            def copy(i, b, h):
                act.wait_ge(transposed, i + 1)
                if past(i, 2):
                    act.wait_ge(logits_done, i - 1)
                act.activation(xf[b][:], psT[b][:], ACT.Copy).then_inc(x_ready, 1)

            def exps(i, b, h):
                act.wait_ge(d_ready, i + 1)
                act.activation(ex[:], d[b][:], ACT.Exp)
                act.activation(e2[:], d2[b][:], ACT.Exp).then_inc(exps_done, 1)

            pipelined(act, SEQS, (1, copy), (1, exps))

        @block.tensor
        def _(pe):
            def transpose(i, b, h):
                pe.wait_ge(normed, i + 1)
                if past(i, 2):
                    pe.wait_ge(x_ready, i - 1)
                for j in range(T4):
                    last = pe.transpose(psT[b][:, j * P:(j + 1) * P], nt[b][:, j, :], m.ident)
                last.then_inc(transposed, 1)

            def logits(i, b, h):
                pe.wait_ge(x_ready, i + 1)
                if past(i, 1):
                    pe.wait_ge(chain, (i - 1) * STEPS + 1)
                for j in range(T4):
                    last = pe.matmul(psL[:, j * E:(j + 1) * E], xf[b][:, j * P:(j + 1) * P], m.wr[:], start=True, stop=True)
                last.then_inc(logits_done, 1)

            def count(i, b, h):
                pe.wait_ge(both_ready, i + 1)
                if past(i, 1):
                    pe.wait_ge(count_read, i)
                rhs = both[:].rearrange("p j e -> p (j e)")
                pe.matmul(psC[:, 0:T4 * E], m.const[:, C_UP:C_UP + P], rhs, start=True, stop=True)
                pe.matmul(psC[:, T4 * E:2 * T4 * E], m.ones[:], rhs, start=True, stop=True).then_inc(counted, 1)

            pipelined(pe, SEQS, (1, transpose), (1, logits), (1, count))

        @block.sync
        def _(sp):
            rows = xs[DUMMY:DUMMY + ROWS, :].rearrange("(p r) d -> p (r d)", p=P)
            sp.dma_start(rows, m.zeros[:]).then_inc(zeroed, 16)
            sp.wait_ge(rows_ready, 1)
            for e in range(E):
                r = sp.value_load(m.tail_row[0:1, e:e + 1], min_val=e * CAP, max_val=e * CAP + TILES * P)
                rows = xs[bass.ds(r, ROWS), :].rearrange("(p r) d -> p (r d)", p=P)
                sp.dma_start(rows, m.zeros[:]).then_inc(zeroed, 16)
            sp.wait_ge(zeroed, (E + 1) * 16)


def experts(nc, m, xs, ys, moe_w, tag):
    ctx, sb, sem = phase(nc, tag)
    with ctx:
        wu = [sb(f"w_up{b}", [P, WUP]) for b in range(2)]
        wd = [sb(f"w_down{b}", [P, WCOLS - WUP]) for b in range(2)]
        xt = [sb(f"x_tm{b}", [P, T4, P]) for b in range(2)]
        xf = [sb(f"x_fm{b}", [P, ROWS]) for b in range(2)]
        gl = [sb(f"gelu{b}", [P, ROWS]) for b in range(2)]
        hh = [sb(f"hidden{b}", [P, HID, ROWS]) for b in range(2)]
        yt = [sb(f"y_tm{b}", [P, T4, P]) for b in range(2)]
        psT, psG, psU, psY = m.banks[0], m.banks[1:3], m.banks[3:5], m.banks[5:7]
        wu_in = [sem(f"w_up_in{b}") for b in range(2)]
        wd_in = [sem(f"w_down_in{b}") for b in range(2)]
        x_in = [sem(f"x_in{b}") for b in range(2)]
        y_out = [sem(f"y_out{b}") for b in range(2)]
        transposed, x_ready, gate_done, up_done = sem("transposed"), sem("x_ready"), sem("gate_done"), sem("up_done")
        gelu_done, hidden_ready, down_done, y_ready = sem("gelu_done"), sem("hidden_ready"), sem("down_done"), sem("y_ready")
        block = ctx.enter_context(nc.Block())
        H = HID * P
        B1c, BGc = 2 * H, 2 * H + HID

        @block.sync
        def _(sp):
            def load_x(i, b, h):
                r = sp.value_load(m.tile_row[0:1, bass.ds(i, 1)], min_val=0, max_val=DUMMY)
                if past(i, 2):
                    sp.wait_ge(transposed, i - 1)
                sp.dma_start(xt[b][:], xs[bass.ds(r, ROWS), :].rearrange("(p r) d -> p r d", p=P)).then_inc(x_in[b], 16)

            def load_w(i, b, h):
                e = sp.value_load(m.tile_expert[0:1, bass.ds(i, 1)], min_val=0, max_val=E - 1)
                src = moe_w[bass.ds(e, 1), :, :].rearrange("a p c -> (a p) c")
                if past(i, 2):
                    sp.wait_ge(hidden_ready, (i - 1) * HID)
                sp.dma_start(wu[b][:], src[:, 0:WUP]).then_inc(wu_in[b], 16)
                if past(i, 2):
                    sp.wait_ge(y_ready, i - 1)
                sp.dma_start(wd[b][:], src[:, WUP:]).then_inc(wd_in[b], 16)

            pipelined(sp, XTILES, (0, load_x), (1, load_w))

        @block.gpsimd
        def _(pool):
            def store(i, b, h):
                pool.wait_ge(y_ready, i + 1)
                pool.dma_start(ys[bass.ds(i * ROWS, ROWS), :].rearrange("(p r) d -> p r d", p=P), yt[b][:]).then_inc(y_out[b], 16)

            pipelined(pool, XTILES, (0, store))
            for b in range(2):
                pool.wait_ge(y_out[b], XTILES // 2 * 16)

        @block.tensor
        def _(pe):
            def transpose(i, b, h):
                pe.wait_ge(x_in[b], h * 16 + 16)
                if past(i, 1):
                    pe.wait_ge(x_ready, i)
                for j in range(T4):
                    last = pe.transpose(psT[:, j * P:(j + 1) * P], xt[b][:, j, :], m.ident)
                last.then_inc(transposed, 1)

            def up(chunks):
                def part(i, b, h):
                    if chunks[0] == 0:
                        pe.wait_ge(wu_in[b], h * 16 + 16)
                        pe.wait_ge(x_ready, i + 1)
                    for c in chunks:
                        if past(i, 1) or c > 1:
                            pe.wait_ge(hidden_ready, i * HID + c - 1)
                        pe.matmul(psG[c % 2][:], wu[b][:, H + c * P:H + (c + 1) * P], xf[b][:], start=True, stop=True).then_inc(gate_done, 1)
                        pe.matmul(psU[c % 2][:], wu[b][:, c * P:(c + 1) * P], xf[b][:], start=True, stop=True).then_inc(up_done, 1)
                return part

            def down(i, b, h):
                pe.wait_ge(wd_in[b], h * 16 + 16)
                pe.wait_ge(hidden_ready, (i + 1) * HID)
                if past(i, 2):
                    pe.wait_ge(y_ready, i - 1)
                for j in range(T4):
                    for c in range(HID):
                        last = pe.matmul(psY[b][:, j * P:(j + 1) * P], hh[b][:, c, j * P:(j + 1) * P],
                                         wd[b][:, c * P:(c + 1) * P], start=c == 0, stop=c == HID - 1)
                last.then_inc(down_done, 1)

            pipelined(pe, XTILES, (0, transpose), (1, up((0,))), (2, down), (1, up((1, 2, 3))))

        @block.scalar
        def _(act):
            def copy(i, b, h):
                act.wait_ge(transposed, i + 1)
                if past(i, 2):
                    act.wait_ge(up_done, (i - 1) * HID)
                act.activation(xf[b][:], psT[:], ACT.Copy).then_inc(x_ready, 1)

            def gelu(i, b, h):
                act.wait_ge(wu_in[b], h * 16 + 16)
                for c in range(HID):
                    act.wait_ge(gate_done, i * HID + c + 1)
                    if past(i, 1) or c > 1:
                        act.wait_ge(hidden_ready, i * HID + c - 1)
                    act.activation(gl[c % 2][:], psG[c % 2][:], ACT.Gelu, bias=wu[b][:, BGc + c:BGc + c + 1]).then_inc(gelu_done, 1)

            pipelined(act, XTILES, (0, copy), (1, gelu))

        @block.vector
        def _(dve):
            def hidden(chunks):
                def part(i, b, h):
                    if chunks[0] == 0:
                        dve.wait_ge(wu_in[b], h * 16 + 16)
                        if past(i, 2):
                            dve.wait_ge(down_done, i - 1)
                    for c in chunks:
                        dve.wait_ge(gelu_done, i * HID + c + 1)
                        dve.wait_ge(up_done, i * HID + c + 1)
                        dve.scalar_tensor_tensor(hh[b][:, c, :], psU[c % 2][:], wu[b][:, B1c + c:B1c + c + 1], gl[c % 2][:],
                                                 ALU.add, ALU.mult).then_inc(hidden_ready, 1)
                return part

            def bias(i, b, h):
                dve.wait_ge(wd_in[b], h * 16 + 16)
                dve.wait_ge(down_done, i + 1)
                if past(h, 1):
                    dve.wait_ge(y_out[b], h * 16)
                b2 = wd[b][:, H:H + P].unsqueeze(1).to_broadcast([P, T4, P])
                dve.tensor_tensor(yt[b][:], psY[b][:].rearrange("p (j c) -> p j c", c=P), b2, ALU.add).then_inc(y_ready, 1)

            pipelined(dve, XTILES, (1, hidden((0, 1))), (2, bias), (1, hidden((2, 3))))


def combine_parts(m, ys, sem, sb):
    yy = [sb(f"y_rows{b}", [P, 2 * T4, P]) for b in range(2)]
    ix = [sb(f"slot_list{b}", [P, T4, 2], U32) for b in range(2)]
    gt = [sb(f"gates{b}", [P, T4, 2]) for b in range(2)]
    listed, combined = sem("listed"), sem("combined")
    fetched = [sem(f"fetched{b}") for b in range(2)]

    def lists(dve):
        def part(i, b, h):
            if past(h, 1):
                dve.wait_ge(fetched[b], h * (2 * T4 * 16))
            if past(i, 2):
                dve.wait_ge(combined, 2 * i - 2)
            dve.tensor_copy(gt[b][:], tiles(m.gates, i))
            dve.tensor_copy(ix[b][:], tiles(m.pos, i)).then_inc(listed, 1)
        return part

    def fetch(pool):
        def part(i, b, h):
            pool.wait_ge(listed, i + 1)
            if past(i, 2):
                pool.wait_ge(combined, 2 * i - 2)
            pool.sem_inc(m.carrier, 1)
            for j in range(T4):
                for k in range(2):
                    pool.indirect_dma_start(yy[b][:, 2 * j + k, :], None, ys,
                                            bass.IndirectOffsetOnAxis(ap=ix[b][:, j, k:k + 1], axis=0)).then_inc(fetched[b], 16)
        return part

    def add(dve):
        def part(i, b, h):
            dve.wait_ge(fetched[b], h * (2 * T4 * 16) + 2 * T4 * 16)
            dve.wait_ge(listed, i + 1)
            for k in range(2):
                for j in range(T4):
                    x = m.X[:, i * T4 + j, :]
                    last = dve.scalar_tensor_tensor(x, yy[b][:, 2 * j + k, :], gt[b][:, j, k:k + 1], x, ALU.mult, ALU.add)
                last.then_inc(combined, 1)
                if k == 0:
                    dve.wait_ge(combined, 2 * i + 1)
        return part

    return lists, fetch, add, combined, fetched


def attention(nc, m, ys):
    ctx, sb, sem = phase(nc, "attn")
    with ctx:
        lists, fetch, add, combined, fetched = combine_parts(m, ys, sem, sb)
        st = [sb(f"stats{b}", [P, T4, 6]) for b in range(2)]
        mv = [sb(f"mean_var{b}", [P, T4, 2]) for b in range(2)]
        rv = [sb(f"var_eps{b}", [P, T4]) for b in range(2)]
        rs = [sb(f"rstd{b}", [P, T4]) for b in range(2)]
        nt = [sb(f"normed{b}", [P, T4, P]) for b in range(2)]
        xf = [sb(f"x_fm{b}", [P, SEQ]) for b in range(2)]
        hq = [sb(f"hidden_qk{b}", [P, 2, SEQ]) for b in range(2)]
        vf = [sb(f"v_fm{b}", [P, SEQ]) for b in range(2)]
        gf = [sb(f"g_fm{b}", [P, SEQ]) for b in range(2)]
        nabs = sb("minus_abs", [P, 2, SEQ])
        mx = sb("above_zero", [P, 2, SEQ])
        ee = sb("exp_minus_abs", [P, 2, SEQ])
        ln = [sb(f"log1p{b}", [P, 2, SEQ]) for b in range(2)]
        qk = [sb(f"q_k_tm{b}", [P, 2, SEQ]) for b in range(2)]
        am = sb("a_masked", [P, P])
        ai = sb("a_plus_identity", [P, P])
        zz = sb("z", [P, 2])
        of = sb("out_fm", [P, SEQ])
        ot = sb("out_turned", [P, SEQ])
        sf = [sb(f"out_prime_fm{b}", [P, SEQ]) for b in range(2)]
        psT, psH, psQ, psA, psO, psP = m.banks[0], m.banks[1:3], m.banks[3:5], m.banks[5], m.banks[6], m.banks[7]
        wq1, wq2, wk1, wk2, wv, wg, wp = (m.wb[:, k * P:(k + 1) * P] for k in range(7))

        stats_done, aggr_done, var_ready, rstd_ready = sem("stats_done"), sem("aggr_done"), sem("var_ready"), sem("rstd_ready")
        normed, transposed, x_ready = sem("normed"), sem("transposed"), sem("x_ready")
        up_done, gelu_done = sem("up_done"), sem("gelu_done")
        qk_done, nabs_ready, relu_ready, exp_done, ln_done, qk_ready = (
            sem("qk_done"), sem("nabs_ready"), sem("relu_ready"), sem("exp_done"), sem("ln_done"), sem("qk_ready"))
        a_done, a_masked, a_ready, z_done, z_shift, z_ready = (
            sem("a_done"), sem("a_masked"), sem("a_ready"), sem("z_done"), sem("z_shift"), sem("z_ready"))
        o_done, gated, p_done, x_updated = sem("o_done"), sem("gated"), sem("p_done"), sem("x_updated")
        turned, prime_done, prime_ready = sem("turned"), sem("prime_done"), sem("prime_ready")
        block = ctx.enter_context(nc.Block())

        @block.gpsimd
        def _(pool):
            def rstd(i, b, h):
                pool.wait_ge(var_ready, i + 1)
                pool.tensor_tensor(rs[b][:], rv[b][:], m.half[:], ALU.pow).then_inc(rstd_ready, 1)

            pipelined(pool, SEQS, (0, fetch(pool)), (1, rstd))

        @block.vector
        def _(dve):
            def stats(i, b, h):
                dve.wait_ge(combined, 2 * i + 2)
                dve.sem_inc(m.carrier, 1)
                for j in range(T4):
                    last = dve.bn_stats(st[b][:, j, :], m.X[:, i * T4 + j, :])
                last.then_inc(stats_done, 1)

            def aggregate(i, b, h):
                if isinstance(i, int):
                    dve.wait_ge(stats_done, i + 1)
                for j in range(T4):
                    last = dve.bn_aggr(mv[b][:, j, :], st[b][:, j, :])
                last.then_inc(aggr_done, 1)
                dve.wait_ge(aggr_done, i + 1)
                dve.tensor_scalar(rv[b][:], mv[b][:, :, 1], 1.0, LN_EPS, ALU.mult, ALU.add).then_inc(var_ready, 1)

            def normalize(i, b, h):
                dve.wait_ge(stats_done, min(i + 2, SEQS) if isinstance(i, int) else i + 2)
                dve.wait_ge(rstd_ready, i + 1)
                if past(i, 2):
                    dve.wait_ge(transposed, i - 1)
                for j in range(T4):
                    last = dve.tensor_scalar(nt[b][:, j, :], m.X[:, i * T4 + j, :], mv[b][:, j, 0:1], rs[b][:, j:j + 1],
                                             ALU.subtract, ALU.mult)
                last.then_inc(normed, 1)

            def minus_abs(i, b, h):
                dve.wait_ge(qk_done, i + 1)
                if past(i, 1):
                    dve.wait_ge(exp_done, i)
                if past(i, 1):
                    dve.wait_ge(qk_ready, i)
                for k in range(2):
                    dve.tensor_scalar(mx[:, k, :], psQ[k][:], 0.0, None, ALU.max)
                dve_last = mx
                last = None
                for k in range(2):
                    last = dve.tensor_scalar(nabs[:, k, :], psQ[k][:], 0.0, None, ALU.min)
                last.then_inc(relu_ready, 1)
                dve.wait_ge(relu_ready, i + 1)
                dve.tensor_tensor(nabs[:], nabs[:], mx[:], ALU.subtract).then_inc(nabs_ready, 1)

            def softplus(i, b, h):
                dve.wait_ge(ln_done, i + 1)
                if past(i, 2):
                    dve.wait_ge(a_done, i - 1)
                dve.tensor_tensor(qk[b][:], ln[b][:], mx[:], ALU.add).then_inc(qk_ready, 1)

            def heads(i, b, h):
                dve.wait_ge(a_done, i + 1)
                if past(i, 1):
                    dve.wait_ge(o_done, i)
                dve.tensor_tensor(am[:], psA[:, 0:P], m.const[:, C_HEAD:C_HEAD + P], ALU.mult).then_inc(a_masked, 1)
                dve.wait_ge(a_masked, i + 1)
                dve.tensor_tensor(ai[:], am[:], m.ident, ALU.add).then_inc(a_ready, 1)
                dve.wait_ge(z_done, i + 1)
                dve.tensor_scalar(zz[:, 0:1], psA[:, P:P + 1], float(P), None, ALU.add).then_inc(z_shift, 1)
                dve.wait_ge(z_shift, i + 1)
                dve.reciprocal(zz[:, 1:2], zz[:, 0:1]).then_inc(z_ready, 1)
                dve.wait_ge(z_ready, i + 1)
                dve.wait_ge(o_done, i + 1)
                dve.scalar_tensor_tensor(of[:], psO[:], zz[:, 1:2], gf[b][:], ALU.mult, ALU.mult).then_inc(gated, 1)
                if past(i, 1):
                    dve.wait_ge(prime_done, i)
                dve.wait_ge(gated, i + 1)
                dve.transpose(ot[:].rearrange("p (q r n) -> p r q n", q=4, n=HD), of[:].rearrange("p (r q n) -> p r q n", q=4, n=HD)).then_inc(turned, 1)

            def update(i, b, h):
                dve.wait_ge(p_done, i + 1)
                xs = tiles(m.X, i)
                dve.tensor_tensor(xs, psP[:].rearrange("p (j c) -> p j c", c=P), xs, ALU.add).then_inc(x_updated, 1)

            pipelined(dve, SEQS, (0, lists(dve)), (1, add(dve)), (1, stats), (2, normalize), (1, aggregate), (3, softplus), (3, heads),
                      (2, minus_abs), (3, update))

        @block.scalar
        def _(act):
            def copy(i, b, h):
                act.wait_ge(transposed, i + 1)
                if past(i, 2):
                    act.wait_ge(up_done, (i - 1) * 4)
                act.activation(xf[b][:].rearrange("p (r j a) -> p j a r", r=16, j=T4), psT[:].rearrange("p (j a r) -> p j a r", j=T4, r=16),
                               ACT.Copy).then_inc(x_ready, 1)

            def primed(i, b, h):
                act.wait_ge(prime_done, i + 1)
                if past(i, 2):
                    act.wait_ge(p_done, i - 1)
                act.activation(sf[b][:].rearrange("p (j q t) -> p q j t", q=4, j=T4), psO[:].rearrange("p (q j t) -> p q j t", q=4, j=T4), ACT.Copy).then_inc(prime_ready, 1)

            def gelus(i, b, h):
                if past(i, 2):
                    act.wait_ge(qk_done, i - 1)
                if past(i, 2):
                    act.wait_ge(gated, i - 1)
                outs = (hq[b][:, 0, :], hq[b][:, 1, :], vf[b][:], gf[b][:])
                for c, (out, bias) in enumerate(zip(outs, (QB1, KB1, VB, GB))):
                    act.wait_ge(up_done, i * 4 + c + 1)
                    act.activation(out, psH[c % 2][:], ACT.Gelu, bias=m.col(bias)).then_inc(gelu_done, 1)

            def log1p(i, b, h):
                act.wait_ge(nabs_ready, i + 1)
                act.activation(ee[:], nabs[:], ACT.Exp).then_inc(exp_done, 1)
                act.wait_ge(exp_done, i + 1)
                act.activation(ln[b][:], ee[:], ACT.Ln, bias=1.0).then_inc(ln_done, 1)

            pipelined(act, SEQS, (2, copy), (2, gelus), (3, primed), (2, log1p))

        @block.tensor
        def _(pe):
            def transpose(i, b, h):
                pe.wait_ge(normed, i + 1)
                if past(i, 1):
                    pe.wait_ge(x_ready, i)
                for j in range(T4):
                    last = pe.transpose(psT[:, j * P:(j + 1) * P], nt[b][:, j, :], m.ident)
                last.then_inc(transposed, 1)

            def up(i, b, h):
                pe.wait_ge(x_ready, i + 1)
                for c, w in enumerate((wq1, wk1, wv, wg)):
                    if past(i, 1) or c > 1:
                        pe.wait_ge(gelu_done, i * 4 + c - 1)
                    pe.matmul(psH[c % 2][:], w, xf[b][:], start=True, stop=True).then_inc(up_done, 1)

            def q_and_k(i, b, h):
                pe.wait_ge(gelu_done, i * 4 + 2)
                if past(i, 1):
                    pe.wait_ge(nabs_ready, i)
                for k, w in enumerate((wq2, wk2)):
                    pe.matmul(psQ[k][:], m.ones[0:1, :], m.rows[0:1, k, :], start=True, stop=False, skip_group_check=True)
                    for j in range(T4):
                        last = pe.matmul(psQ[k][:, j * P:(j + 1) * P], hq[b][:, k, j * P:(j + 1) * P], w,
                                         start=False, stop=j == T4 - 1, skip_group_check=True)
                last.then_inc(qk_done, 1)

            def attend(i, b, h):
                pe.wait_ge(qk_ready, i + 1)
                if past(i, 1):
                    pe.wait_ge(z_shift, i)
                for j in range(T4):
                    last = pe.matmul(psA[:, 0:P], qk[b][:, 1, j * P:(j + 1) * P], qk[b][:, 0, j * P:(j + 1) * P],
                                     start=j == 0, stop=j == T4 - 1)
                last.then_inc(a_done, 1)
                pe.wait_ge(a_masked, i + 1)
                pe.matmul(psA[:, P:P + 1], am[:], m.ones[:, 0:1], start=True, stop=True).then_inc(z_done, 1)
                pe.wait_ge(a_ready, i + 1)
                pe.wait_ge(gelu_done, i * 4 + 4)
                if past(i, 1):
                    pe.wait_ge(prime_ready, i)
                pe.matmul(psO[:], ai[:], vf[b][:], start=True, stop=True).then_inc(o_done, 1)
                pe.wait_ge(turned, i + 1)
                for q in range(4):
                    last = pe.transpose(psO[:, q * P:(q + 1) * P], ot[:, q * P:(q + 1) * P], m.ident)
                last.then_inc(prime_done, 1)
                pe.wait_ge(prime_ready, i + 1)
                if past(i, 1):
                    pe.wait_ge(x_updated, i)
                pe.matmul(psP[:], m.ones[0:1, :], m.rows[0:1, 2, :], start=True, stop=False, skip_group_check=True)
                for j in range(T4):
                    last = pe.matmul(psP[:, j * P:(j + 1) * P], sf[b][:, j * P:(j + 1) * P], wp,
                                     start=False, stop=j == T4 - 1, skip_group_check=True)
                last.then_inc(p_done, 1)

            pipelined(pe, SEQS, (2, transpose), (2, up), (3, attend), (2, q_and_k))


def finish(nc, m, ys, out):
    ctx, sb, sem = phase(nc, "fin")
    with ctx:
        lists, fetch, add, combined, fetched = combine_parts(m, ys, sem, sb)
        stored = sem("stored")
        block = ctx.enter_context(nc.Block())
        ov = out.rearrange("(s t p) d -> s p t d", p=P, t=T4)

        @block.gpsimd
        def _(pool):
            pipelined(pool, SEQS, (0, fetch(pool)))

        @block.vector
        def _(dve):
            pipelined(dve, SEQS, (0, lists(dve)), (1, add(dve)))

        @block.sync
        def _(sp):
            def store(i, b, h):
                sp.wait_ge(combined, 2 * i + 2)
                dst = ov[i] if isinstance(i, int) else ov[bass.ds(i, 1)].rearrange("a p t d -> (a p) t d")
                sp.dma_start(dst, tiles(m.X, i)).then_inc(stored, 16)

            pipelined(sp, SEQS, (0, store))
            sp.wait_ge(stored, SEQS * 16)


def program(nc, x, vecs, consts, wa, wb, wr, rows, moe_w, out):
    xs = nc.dram_tensor("expert_rows_in", [DUMMY + ROWS, P], FP32, kind="Internal").ap()
    ys = nc.dram_tensor("expert_rows_out", [XTILES * ROWS, P], FP32, kind="Internal").ap()
    with ExitStack() as ctx:
        m = Memory(nc, ctx)
        setup(nc, m, x, vecs, consts, wa, wb, wr, rows)
        with nc.sbuf_tensor("after_time_mix", [P, TILES, P], FP32) as XP:
            time_mix(nc, m, XP)
            channel_mix(nc, m, XP)
        route(nc, m, xs, "route1")
        experts(nc, m, xs, ys, moe_w, "experts1")
        attention(nc, m, ys)
        route(nc, m, xs, "route2")
        experts(nc, m, xs, ys, moe_w, "experts2")
        finish(nc, m, ys, out)


def constants():
    import numpy as np
    c = np.zeros((P, NCONST), np.float32)
    c[:, C_ID:C_ID + P] = np.eye(P)
    c[:, C_UP:C_UP + P] = np.triu(np.ones((P, P)), 1)
    c[:, C_HEAD:C_HEAD + P] = np.kron(np.eye(HEADS), np.full((HD, HD), SCALE))
    c[:, C_IM8:C_IM8 + E] = np.arange(E) - 8
    c[:, C_TILE0:C_TILE0 + 16] = np.arange(16) * ROWS
    c[:, C_J:C_J + XTILES] = np.arange(XTILES)
    c[:, C_BASE:C_BASE + E] = np.arange(E) * CAP
    return c


def kernel(**inputs):
    import numpy as np
    import concourse.bacc as bacc
    from concourse.bass_utils import run_bass_kernel_spmd

    v = {k: np.asarray(a) for k, a in inputs.items()}
    A, B, F = "L0_attn_a_", "L0_attn_b_", "L0_ffn_"
    vec_names = [A + k for k in ("ln1_g", "ln1_b", "ln2_g", "ln2_b", "att_time_mix", "att_combined_mix", "time_decay",
                                 "time_first", "ffn_time_mix", "ffn_combined_mix")] + [B + k for k in ("q_b1", "k_b1", "v_b", "g_b")]
    hid = HID * P
    w1, wg = v[F + "w1_w"].transpose(0, 2, 1), v[F + "wg_w"].transpose(0, 2, 1)
    w2 = v[F + "w2_w"].transpose(0, 2, 1).reshape(E, HID, P, P).transpose(0, 2, 1, 3).reshape(E, P, hid)
    b1, bg = (v[F + k].reshape(E, HID, P).transpose(0, 2, 1) for k in ("w1_b", "wg_b"))
    b2 = np.broadcast_to(v[F + "w2_b"][:, None, :], (E, P, P))
    arrays = {
        "x": v[A + "x"].reshape(SEQS * SEQ, P),
        "vecs": np.stack([v[k].reshape(P) for k in vec_names], 1),
        "consts": constants(),
        "wa": np.concatenate([v[A + k].T for k in ("Wk", "Wv", "Wr", "Wo", "Fr", "Fk")]
                             + [v[A + "Fv"].T.reshape(HID, P, P).transpose(1, 0, 2).reshape(P, hid)], 1),
        "wb": np.concatenate([v[B + k].T for k in ("q_w1", "q_w2", "k_w1", "k_w2", "v_w", "g_w", "p_w")], 1),
        "wr": v[F + "router_w"].T,
        "rows": np.stack([np.tile(v[B + k], T4) for k in ("q_b2", "k_b2", "p_b")])[None],
        "moe_w": np.concatenate([w1, wg, b1, bg, w2, b2], 2),
    }
    arrays = {f"in_{k}": np.ascontiguousarray(a) for k, a in arrays.items()}
    nc = bacc.Bacc("TRN2", target_bir_lowering=False, num_devices=1)
    args = [nc.dram_tensor(k, list(a.shape), FP32, kind="ExternalInput").ap() for k, a in arrays.items()]
    out = nc.dram_tensor("out", [SEQS * SEQ, P], FP32, kind="ExternalOutput").ap()
    program(nc, *args, out)
    r = run_bass_kernel_spmd(nc, [arrays], core_ids=[0])
    return r.results[0]["out"].reshape(SEQS, SEQ, P)
```

```python
import concourse.bass as bass
from concourse import mybir
from contextlib import ExitStack

FP32 = mybir.dt.float32
FP32R = mybir.dt.float32r
I32 = mybir.dt.int32
U32 = mybir.dt.uint32
ALU = mybir.AluOpType
ACT = mybir.ActivationFunctionType
AX = mybir.AxisListType.X

P = 128
SEQS, SEQ = 16, 512
T4 = SEQ // P
TILES = SEQS * T4
HID = 4
E = 8
HEADS = 16
HD = P // HEADS
ROWS = 512
CAP = TILES * P + ROWS
DUMMY = E * CAP
XTILES = 2 * TILES * P // ROWS + E
LN_EPS = 1e-5
K_CLAMP = 60.0
SCALE = float(HD) ** -0.5

(G1, B1, G2, B2, TM1, CM1, TD, TF, TM2, CM2, QB1, KB1, VB, GB) = range(14)
NVEC = 14
C_ID, C_UP, C_HEAD = 0, 128, 256
C_IM8 = 384
C_TILE0 = C_IM8 + E
C_J = C_TILE0 + 16
C_BASE = C_J + XTILES
NCONST = C_BASE + E


def past(i, n):
    return not isinstance(i, int) or i >= n


def pipelined(eng, n, *parts):
    lag_max = max(lag for lag, _ in parts)
    head = (lag_max + 3) // 2 * 2
    end = n // 2 * 2

    def step(s):
        for lag, part in parts:
            if 0 <= s - lag < n:
                part(s - lag, (s - lag) % 2, (s - lag) // 2)

    for s in range(min(head, end)):
        step(s)
    if head < end:
        with eng.Fori(head // 2, end // 2) as h:
            for u in range(2):
                for lag, part in parts:
                    k = u - lag
                    part(h * 2 + k, k % 2, h + k // 2)
    for s in range(end, n + lag_max):
        step(s)


class Memory:

    def __init__(self, nc, ctx):
        def sb(name, shape, dt=FP32):
            return ctx.enter_context(nc.sbuf_tensor(name, shape, dt))

        self.X = sb("residual", [P, TILES, P])
        self.vec = sb("vectors", [P, NVEC])
        self.const = sb("constants", [P, NCONST])
        self.wa = sb("mix_weights", [P, 5 * P + 2 * HID * P])
        self.wb = sb("attention_weights", [P, 7 * P])
        self.wr = sb("router_weights", [P, E])
        self.rows = sb("bias_rows", [1, 3, T4 * P])
        self.ones = sb("ones", [P, P])
        self.slot = sb("slots_in", [P, TILES, 2])
        self.pos = sb("slots_out", [P, TILES, 2], U32)
        self.gates = sb("gates", [P, TILES, 2])
        self.carry = sb("next_slot", [P, E])
        self.tile_expert = sb("tile_expert", [1, XTILES], I32)
        self.tile_row = sb("tile_row", [1, XTILES], I32)
        self.tail_row = sb("tail_row", [1, E], I32)
        self.zeros = sb("zeros", [P, ROWS // P * P])
        self.half = sb("minus_half", [P, T4])
        self.banks = [ctx.enter_context(nc.psum_tensor(f"bank{b}", [P, 512], FP32)) for b in range(8)]
        self.carrier = ctx.enter_context(nc.semaphore("carrier"))
        self.ident = self.const[:, C_ID:C_ID + P]

    def col(self, k):
        return self.vec[:, k:k + 1]


def phase(nc, tag):
    ctx = ExitStack()

    def sb(name, shape, dt=FP32):
        return ctx.enter_context(nc.sbuf_tensor(f"{tag}_{name}", shape, dt))

    def sem(name):
        return ctx.enter_context(nc.semaphore(f"{tag}_{name}"))

    return ctx, sb, sem


def setup(nc, m, x, vecs, consts, wa, wb, wr, rows):
    ctx, sb, sem = phase(nc, "setup")
    with ctx:
        loaded = sem("loaded")
        block = ctx.enter_context(nc.Block())
        xv = x.rearrange("(t p) d -> p t d", p=P)

        @block.sync
        def _(sp):
            for q in range(4):
                sp.dma_start(m.X[:, 16 * q:16 * q + 16, :], xv[:, 16 * q:16 * q + 16, :]).then_inc(loaded, 16)
            sp.dma_start(m.rows[:], rows).then_inc(loaded, 16)
            sp.wait_ge(loaded, 10 * 16)

        @block.scalar
        def _(act):
            act.dma_start(m.vec[:], vecs).then_inc(loaded, 16)
            act.dma_start(m.const[:], consts).then_inc(loaded, 16)
            act.dma_start(m.wa[:], wa).then_inc(loaded, 16)
            act.dma_start(m.wb[:], wb).then_inc(loaded, 16)
            act.dma_start(m.wr[:], wr).then_inc(loaded, 16)
            act.wait_ge(loaded, 10 * 16)

        @block.gpsimd
        def _(pool):
            pool.memset(m.ones[:], 1.0)
            pool.memset(m.zeros[:], 0.0)
            pool.memset(m.half[:], -0.5)


def time_mix(nc, m, XP):
    ctx, sb, sem = phase(nc, "tmix")
    with ctx:
        coef = sb("coefficients", [P, 8])
        TMG, TMB, CPREV, CNEXT, ED, EU, TMP = range(7)
        decay = sb("decay", [P, 2, SEQ + 1])
        st = [sb(f"stats{b}", [P, T4, 6]) for b in range(2)]
        mv = [sb(f"mean_var{b}", [P, T4, 2]) for b in range(2)]
        rv = [sb(f"var_eps{b}", [P, T4]) for b in range(2)]
        rs = [sb(f"rstd{b}", [P, T4]) for b in range(2)]
        nt = [sb(f"normed{b}", [P, T4, P]) for b in range(2)]
        xf = [sb(f"x_fm{b}", [P, SEQ + 2]) for b in range(2)]
        xm = [sb(f"x_mixed{b}", [P, SEQ]) for b in range(2)]
        kc = sb("k_clamped", [P, SEQ])
        kk = [sb(f"k_kv{b}", [P, 2, SEQ + 1]) for b in range(2)]
        ab = sb("a_b", [P, 2, SEQ + 1])
        nd = sb("num_den", [P, 2, SEQ])
        th = [sb(f"tanh_r{b}", [P, SEQ]) for b in range(2)]
        rd = sb("one_over_den", [P, SEQ])
        y = [sb(f"y_fm{b}", [P, SEQ]) for b in range(2)]
        psT, psK, psV, psR, psO = m.banks[0:2], m.banks[2], m.banks[3], m.banks[4], m.banks[5:7]

        cleared, coef_a, coef_b, decay_ready = sem("cleared"), sem("coef_a"), sem("coef_b"), sem("decay_ready")
        stats_done, aggr_done, var_ready, rstd_ready = sem("stats_done"), sem("aggr_done"), sem("var_ready"), sem("rstd_ready")
        normed, transposed, x_ready, scaled = sem("normed"), sem("transposed"), sem("x_ready"), sem("scaled")
        mixed_prev, mixed, kvr_done = sem("mixed_prev"), sem("mixed"), sem("kvr_done")
        k_clamped, k_ready, tanh_ready, kv_ready = sem("k_clamped"), sem("k_ready"), sem("tanh_ready"), sem("kv_ready")
        scanned, num_den, u_ready, y_ready = sem("scanned"), sem("num_den"), sem("u_ready"), sem("y_ready")
        o_done, xp_ready = sem("o_done"), sem("xp_ready")
        block = ctx.enter_context(nc.Block())
        W = {k: m.wa[:, i * P:(i + 1) * P] for i, k in enumerate("kvro")}

        @block.gpsimd
        def _(pool):
            for b in range(2):
                pool.memset(xf[b][:, 0:1], 0.0)
                pool.memset(xf[b][:, SEQ + 1:SEQ + 2], 0.0)
                pool.memset(kk[b][:, :, 0:1], 0.0)
            pool.memset(decay[:, :, 0:1], 0.0).then_inc(cleared, 1)

            def rstd(i, b, h):
                pool.wait_ge(var_ready, i + 1)
                pool.tensor_tensor(rs[b][:], rv[b][:], m.half[:], ALU.pow).then_inc(rstd_ready, 1)

            pipelined(pool, SEQS, (0, rstd))

        @block.vector
        def _(dve):
            dve.tensor_tensor(coef[:, TMG:TMG + 1], m.col(TM1), m.col(G1), ALU.mult)
            dve.tensor_tensor(coef[:, TMB:TMB + 1], m.col(TM1), m.col(B1), ALU.mult)
            dve.tensor_scalar(coef[:, CPREV:CPREV + 1], m.col(TM1), -1.0, 1.0, ALU.mult, ALU.add)
            dve.tensor_copy(coef[:, CNEXT:CNEXT + 1], m.col(CM1)).then_inc(coef_a, 1)
            dve.wait_ge(coef_a, 1)
            dve.tensor_tensor(coef[0:64, CPREV:CPREV + 1], coef[0:64, CPREV:CPREV + 1], m.vec[0:64, CM1:CM1 + 1], ALU.add).then_inc(coef_a, 1)
            dve.wait_ge(coef_b, 3)
            dve.tensor_scalar(decay[:, 0, 1:], m.zeros[:], coef[:, ED:ED + 1], None, ALU.add)
            dve.tensor_scalar(decay[:, 1, 1:], m.zeros[:], coef[:, ED:ED + 1], None, ALU.add).then_inc(decay_ready, 1)
            dve.wait_ge(cleared, 1)
            dve.wait_ge(coef_a, 2)
            dve.wait_ge(decay_ready, 1)

            def stats(i, b, h):
                for j in range(T4):
                    last = dve.bn_stats(st[b][:, j, :], m.X[:, i * T4 + j, :])
                last.then_inc(stats_done, 1)

            def aggregate(i, b, h):
                dve.wait_ge(stats_done, i + 1)
                dve.sem_inc(m.carrier, 1)
                for j in range(T4):
                    last = dve.bn_aggr(mv[b][:, j, :], st[b][:, j, :])
                last.then_inc(aggr_done, 1)
                dve.wait_ge(aggr_done, i + 1)
                dve.tensor_scalar(rv[b][:], mv[b][:, :, 1], 1.0 + LN_EPS, LN_EPS * LN_EPS, ALU.mult, ALU.add).then_inc(var_ready, 1)

            def normalize(i, b, h):
                dve.wait_ge(rstd_ready, i + 1)
                if past(i, 2):
                    dve.wait_ge(transposed, i - 1)
                for j in range(T4):
                    last = dve.tensor_scalar(nt[b][:, j, :], m.X[:, i * T4 + j, :], mv[b][:, j, 0:1], rs[b][:, j:j + 1],
                                             ALU.subtract, ALU.mult)
                last.then_inc(normed, 1)

            def mix(i, b, h):
                dve.wait_ge(x_ready, i + 1)
                dve.wait_ge(scaled, i + 1)
                dve.scalar_tensor_tensor(xm[b][:], xf[b][:, 0:SEQ], coef[:, CPREV:CPREV + 1], xm[b][:],
                                         ALU.mult, ALU.add).then_inc(mixed_prev, 1)
                dve.wait_ge(mixed_prev, i + 1)
                dve.scalar_tensor_tensor(xm[b][64:P, :], xf[b][64:P, 2:], coef[64:P, CNEXT:CNEXT + 1], xm[b][64:P, :],
                                         ALU.mult, ALU.add).then_inc(mixed, 1)

            def wkv(i, b, h):
                dve.wait_ge(kvr_done, i + 1)
                if past(i, 1):
                    dve.wait_ge(k_ready, i)
                dve.tensor_scalar(kc[:], psK[:], K_CLAMP, None, ALU.min).then_inc(k_clamped, 1)
                dve.wait_ge(k_ready, i + 1)
                dve.tensor_tensor(kk[b][:, 0, 1:], kk[b][:, 1, 1:], psV[:], ALU.mult).then_inc(kv_ready, 1)
                dve.wait_ge(kv_ready, i + 1)
                dve.tensor_tensor_scan(ab[:].rearrange("p s t -> p (s t)"), decay[:].rearrange("p s t -> p (s t)"),
                                       kk[b][:].rearrange("p s t -> p (s t)"), 0.0, ALU.mult, ALU.add).then_inc(scanned, 1)
                dve.wait_ge(scanned, i + 1)
                dve.scalar_tensor_tensor(nd[:], kk[b][:, :, 1:], coef[:, EU:EU + 1], ab[:, :, 0:SEQ],
                                         ALU.mult, ALU.add).then_inc(num_den, 1)
                dve.wait_ge(num_den, i + 1)
                dve.reciprocal(rd[:], nd[:, 1, :])
                dve.wait_ge(tanh_ready, i + 1)
                if past(i, 2):
                    dve.wait_ge(o_done, i - 1)
                dve.scalar_tensor_tensor(y[b][:], th[b][:], 1.0, nd[:, 0, :], ALU.add, ALU.mult).then_inc(u_ready, 1)
                dve.wait_ge(u_ready, i + 1)
                dve.scalar_tensor_tensor(y[b][:], y[b][:], 0.5, rd[:], ALU.mult, ALU.mult).then_inc(y_ready, 1)

            pipelined(dve, SEQS, (0, stats), (1, normalize), (0, aggregate), (2, wkv), (1, mix))

        @block.scalar
        def _(act):
            act.activation(coef[:, ED:ED + 1], m.col(TD), ACT.Exp).then_inc(coef_b, 1)
            act.activation(coef[:, EU:EU + 1], m.col(TF), ACT.Exp).then_inc(coef_b, 1)
            act.wait_ge(coef_b, 2)
            act.activation(coef[:, ED:ED + 1], coef[:, ED:ED + 1], ACT.Exp, scale=-1.0).then_inc(coef_b, 1)
            act.wait_ge(coef_a, 2)

            def affine(i, b, h):
                act.wait_ge(transposed, i + 1)
                if past(i, 2):
                    act.wait_ge(o_done, i - 1)
                act.activation(xf[b][:, 1:SEQ + 1], psT[b][:], ACT.Identity, bias=m.col(B1), scale=m.col(G1)).then_inc(x_ready, 1)
                if past(i, 2):
                    act.wait_ge(kvr_done, i - 1)
                act.activation(xm[b][:], psT[b][:], ACT.Identity, bias=coef[:, TMB:TMB + 1],
                               scale=coef[:, TMG:TMG + 1]).then_inc(scaled, 1)

            def exponentials(i, b, h):
                act.wait_ge(k_clamped, i + 1)
                if past(i, 2):
                    act.wait_ge(num_den, i - 1)
                act.activation(kk[b][:, 1, 1:], kc[:], ACT.Exp).then_inc(k_ready, 1)
                if past(i, 2):
                    act.wait_ge(y_ready, i - 1)
                act.activation(th[b][:], psR[:], ACT.Tanh, scale=0.5).then_inc(tanh_ready, 1)

            def store(i, b, h):
                act.wait_ge(o_done, i + 1)
                act.activation(XP[:, bass.ds(i * T4, T4), :] if not isinstance(i, int) else XP[:, i * T4:i * T4 + T4, :],
                               psO[b][:].rearrange("p (j c) -> p j c", c=P), ACT.Copy).then_inc(xp_ready, 1)

            pipelined(act, SEQS, (1, affine), (2, exponentials), (2, store))

        @block.tensor
        def _(pe):
            def transpose(i, b, h):
                pe.wait_ge(normed, i + 1)
                if past(i, 2):
                    pe.wait_ge(scaled, i - 1)
                for j in range(T4):
                    last = pe.transpose(psT[b][:, j * P:(j + 1) * P], nt[b][:, j, :], m.ident)
                last.then_inc(transposed, 1)

            def kvr(i, b, h):
                pe.wait_ge(mixed, i + 1)
                if past(i, 1):
                    pe.wait_ge(tanh_ready, i)
                if past(i, 1):
                    pe.wait_ge(kv_ready, i)
                pe.matmul(psK[:], W["k"], xm[b][:], start=True, stop=True)
                pe.matmul(psV[:], W["v"], xm[b][:], start=True, stop=True)
                pe.matmul(psR[:], W["r"], xm[b][:], start=True, stop=True).then_inc(kvr_done, 1)

            def project(i, b, h):
                pe.wait_ge(y_ready, i + 1)
                if past(i, 2):
                    pe.wait_ge(xp_ready, i - 1)
                for j in range(T4):
                    out = psO[b][:, j * P:(j + 1) * P]
                    pe.matmul(out, y[b][:, j * P:(j + 1) * P], W["o"], start=True, stop=False)
                    last = pe.matmul(out, xf[b][:, 1 + j * P:1 + (j + 1) * P], m.ident, start=False, stop=True)
                last.then_inc(o_done, 1)

            pipelined(pe, SEQS, (1, transpose), (2, project), (1, kvr))


def channel_mix(nc, m, XP, xs):
    ctx, sb, sem = phase(nc, "cmix")
    with ctx:
        coef = sb("coefficients", [P, 4])
        TMG, TMB, CPREV, CNEXT = range(4)
        st = [sb(f"stats{b}", [P, T4, 6]) for b in range(2)]
        mv = [sb(f"mean_var{b}", [P, T4, 2]) for b in range(2)]
        rv = [sb(f"var_eps{b}", [P, T4]) for b in range(2)]
        rs = [sb(f"rstd{b}", [P, T4]) for b in range(2)]
        nt = [sb(f"normed{b}", [P, T4, P]) for b in range(2)]
        xf = [sb(f"x_fm{b}", [P, SEQ + 2]) for b in range(2)]
        xm = [sb(f"x_mixed{b}", [P, SEQ]) for b in range(2)]
        rl = sb("relu", [P, 2, SEQ])
        kq = [sb(f"k_fm{b}", [P, HID, SEQ]) for b in range(2)]
        th = sb("tanh_r", [P, SEQ])
        u = sb("gated", [P, SEQ])
        w = sb("gated_plus_x", [P, SEQ])
        psT, psF, psKV, psG, psX = m.banks[0], m.banks[1:3], m.banks[3], m.banks[4], m.banks[5]

        cleared, coef_a = sem("cleared"), sem("coef_a")
        stats_done, aggr_done, var_ready, rstd_ready = sem("stats_done"), sem("aggr_done"), sem("var_ready"), sem("rstd_ready")
        normed, transposed, x_ready, scaled = sem("normed"), sem("transposed"), sem("x_ready"), sem("scaled")
        mixed_prev, mixed = sem("mixed_prev"), sem("mixed")
        fk_done, relu_done, k_ready = sem("fk_done"), sem("relu_done"), sem("k_ready")
        out_done, tanh_ready, gated, summed, x_updated = sem("out_done"), sem("tanh_ready"), sem("gated"), sem("summed"), sem("x_updated")
        route = Route(m, xs, sem, sb, x_updated, m.banks[6], m.banks[7])
        block = ctx.enter_context(nc.Block())
        WR = m.wa[:, 4 * P:5 * P]
        FK = m.wa[:, 5 * P:5 * P + HID * P]
        FV = m.wa[:, (5 + HID) * P:]

        @block.gpsimd
        def _(pool):
            for b in range(2):
                pool.memset(xf[b][:, 0:1], 0.0)
                last = pool.memset(xf[b][:, SEQ + 1:SEQ + 2], 0.0)
            last.then_inc(cleared, 1)

            def rstd(i, b, h):
                pool.wait_ge(var_ready, i + 1)
                pool.tensor_tensor(rs[b][:], rv[b][:], m.half[:], ALU.pow).then_inc(rstd_ready, 1)

            pipelined(pool, SEQS, (5, route.send(pool)), (3, route.rstd(pool)), (0, rstd))
            route.all_sent(pool)

        @block.vector
        def _(dve):
            dve.tensor_tensor(coef[:, TMG:TMG + 1], m.col(TM2), m.col(G2), ALU.mult)
            dve.tensor_tensor(coef[:, TMB:TMB + 1], m.col(TM2), m.col(B2), ALU.mult)
            dve.tensor_scalar(coef[:, CPREV:CPREV + 1], m.col(TM2), -1.0, 1.0, ALU.mult, ALU.add)
            dve.tensor_copy(coef[:, CNEXT:CNEXT + 1], m.col(CM2)).then_inc(coef_a, 1)
            dve.wait_ge(coef_a, 1)
            dve.tensor_tensor(coef[0:64, CPREV:CPREV + 1], coef[0:64, CPREV:CPREV + 1], m.vec[0:64, CM2:CM2 + 1], ALU.add).then_inc(coef_a, 1)
            dve.wait_ge(cleared, 1)
            dve.wait_ge(coef_a, 2)

            def stats(i, b, h):
                for j in range(T4):
                    last = dve.bn_stats(st[b][:, j, :], XP[:, i * T4 + j, :])
                last.then_inc(stats_done, 1)

            def aggregate(i, b, h):
                dve.wait_ge(stats_done, i + 1)
                dve.sem_inc(m.carrier, 1)
                for j in range(T4):
                    last = dve.bn_aggr(mv[b][:, j, :], st[b][:, j, :])
                last.then_inc(aggr_done, 1)
                dve.wait_ge(aggr_done, i + 1)
                dve.tensor_scalar(rv[b][:], mv[b][:, :, 1], 1.0, LN_EPS, ALU.mult, ALU.add).then_inc(var_ready, 1)

            def normalize(i, b, h):
                dve.wait_ge(rstd_ready, i + 1)
                if past(i, 2):
                    dve.wait_ge(transposed, i - 1)
                for j in range(T4):
                    last = dve.tensor_scalar(nt[b][:, j, :], XP[:, i * T4 + j, :], mv[b][:, j, 0:1], rs[b][:, j:j + 1],
                                             ALU.subtract, ALU.mult)
                last.then_inc(normed, 1)

            def mix(i, b, h):
                dve.wait_ge(x_ready, i + 1)
                dve.wait_ge(scaled, i + 1)
                dve.scalar_tensor_tensor(xm[b][:], xf[b][:, 0:SEQ], coef[:, CPREV:CPREV + 1], xm[b][:],
                                         ALU.mult, ALU.add).then_inc(mixed_prev, 1)
                dve.wait_ge(mixed_prev, i + 1)
                dve.scalar_tensor_tensor(xm[b][64:P, :], xf[b][64:P, 2:], coef[64:P, CNEXT:CNEXT + 1], xm[b][64:P, :],
                                         ALU.mult, ALU.add).then_inc(mixed, 1)

            def update(i, b, h):
                dve.wait_ge(tanh_ready, i + 1)
                dve.scalar_tensor_tensor(u[:], th[:], 1.0, psKV[:], ALU.add, ALU.mult).then_inc(gated, 1)
                dve.wait_ge(gated, i + 1)
                dve.scalar_tensor_tensor(w[:], u[:], 0.5, psX[:], ALU.mult, ALU.add).then_inc(summed, 1)
                dve.wait_ge(summed, i + 1)
                xs = tiles(m.X, i)
                dve.tensor_tensor(xs, w[:].rearrange("p (j c) -> p j c", c=P), xs, ALU.add).then_inc(x_updated, 1)

            route.begin(dve)
            pipelined(dve, SEQS, (5, route.place(dve)), (2, mix), (1, normalize), (4, route.rank(dve)),
                      (3, update), (3, route.stats(dve)), (0, stats), (0, aggregate), (3, route.normalize(dve)))
            route.plan(dve)

        @block.scalar
        def _(act):
            act.wait_ge(coef_a, 2)

            def affine(i, b, h):
                act.wait_ge(transposed, i + 1)
                if past(i, 2):
                    act.wait_ge(out_done, i - 1)
                act.activation(xf[b][:, 1:SEQ + 1], psT[:], ACT.Identity, bias=m.col(B2), scale=m.col(G2)).then_inc(x_ready, 1)
                act.activation(xm[b][:], psT[:], ACT.Identity, bias=coef[:, TMB:TMB + 1],
                               scale=coef[:, TMG:TMG + 1]).then_inc(scaled, 1)

            def relu(pair):
                def part(i, b, h):
                    for c in pair:
                        act.wait_ge(fk_done, i * HID + c + 1)
                        if past(i, 1) or c > 1:
                            act.wait_ge(k_ready, i * 2 + c // 2)
                        act.activation(rl[:, c % 2, :], psF[c % 2][:], ACT.Relu).then_inc(relu_done, 1)
                    act.wait_ge(relu_done, i * HID + pair[-1] + 1)
                    if past(i, 2):
                        act.wait_ge(out_done, i - 1)
                    act.activation(kq[b][:, pair[0]:pair[0] + 2, :], rl[:], ACT.Square).then_inc(k_ready, 1)
                return part

            def gate(i, b, h):
                act.wait_ge(out_done, i + 1)
                if past(i, 1):
                    act.wait_ge(gated, i)
                act.activation(th[:], psG[:], ACT.Tanh, scale=0.5).then_inc(tanh_ready, 1)

            pipelined(act, SEQS, (5, route.exps(act)), (2, affine), (4, route.copy(act)), (3, gate), (2, relu((0, 1))), (2, relu((2, 3))))

        @block.sync
        def _(sp):
            route.zero_tails(sp)

        @block.tensor
        def _(pe):
            def transpose(i, b, h):
                pe.wait_ge(normed, i + 1)
                if past(i, 1):
                    pe.wait_ge(scaled, i)
                for j in range(T4):
                    last = pe.transpose(psT[:, j * P:(j + 1) * P], nt[b][:, j, :], m.ident)
                last.then_inc(transposed, 1)

            def up(i, b, h):
                pe.wait_ge(mixed, i + 1)
                for c in range(HID):
                    if past(i, 1) or c > 1:
                        pe.wait_ge(relu_done, i * HID + c - 1)
                    pe.matmul(psF[c % 2][:], FK[:, c * P:(c + 1) * P], xm[b][:], start=True, stop=True).then_inc(fk_done, 1)

            def down(js):
                def part(i, b, h):
                    pe.wait_ge(k_ready, (i + 1) * 2)
                    if past(i, 1):
                        pe.wait_ge(summed, i)
                    for j in js:
                        for c in range(HID):
                            pe.matmul(psKV[:, j * P:(j + 1) * P], kq[b][:, c, j * P:(j + 1) * P], FV[:, c * P:(c + 1) * P],
                                      start=c == 0, stop=c == HID - 1)
                return part

            def gate_and_x(i, b, h):
                for j in range(T4):
                    pe.matmul(psG[:, j * P:(j + 1) * P], xm[b][:, j * P:(j + 1) * P], WR, start=True, stop=True)
                for j in range(T4):
                    last = pe.matmul(psX[:, j * P:(j + 1) * P], xf[b][:, 1 + j * P:1 + (j + 1) * P], m.ident,
                                     start=True, stop=True)
                last.then_inc(out_done, 1)

            pipelined(pe, SEQS, (5, route.count(pe)), (2, transpose), (4, route.transpose(pe)), (3, down((0, 1))),
                      (4, route.logits(pe)), (3, down((2, 3))), (3, gate_and_x), (2, up))


def tiles(t, i):
    if isinstance(i, int):
        return t[:, i * T4:(i + 1) * T4, :]
    return t[:, bass.ds(i * T4, T4), :]


class Route:

    def __init__(self, m, xs, sem, sb, x_updated, psT, psLC):
        self.m, self.xs, self.x_updated = m, xs, x_updated
        self.st = sb("r_stats", [P, T4, 6])
        self.mv = [sb(f"r_mean_var{b}", [P, T4, 2]) for b in range(2)]
        self.rv = sb("r_var_eps", [P, T4])
        self.rs = [sb(f"r_rstd{b}", [P, T4]) for b in range(2)]
        self.nt = [sb(f"r_normed{b}", [P, T4, P]) for b in range(2)]
        self.xf = sb("r_x_fm", [P, SEQ])
        self.lg = sb("logits", [P, T4, E])
        self.lg2 = sb("logits_but_max", [P, T4, E])
        self.mx = sb("max_1_2", [P, 2, T4])
        self.eq = sb("equals", [P, T4, E])
        self.first = sb("first", [P, 2, T4])
        self.mask = sb("masks", [P, 2, T4, E])
        self.both = sb("both_masks", [P, T4, E])
        self.d = sb("less_max", [P, T4, E + 1])
        self.ex = sb("exps", [P, T4, E + 1])
        self.ssum = sb("exp_sum", [P, T4])
        self.inv = sb("exp_sum_inverse", [P, T4])
        self.pk = sb("slot_masked", [P, 2, T4, E])
        self.pf = sb("slots_float", [P, 2, T4])
        self.idx = [sb(f"slot_lists{b}", [P, 2, T4], U32) for b in range(2)]
        self.tile_w = sb("tile_work", [1, 5, XTILES, E])
        self.small = sb("small_work", [P, 6, E])
        self.cmp16 = sb("count_compare", [P, E, 16])
        self.moved = [sb(f"slot_moved{k}", [P, TILES * 2]) for k in range(2)]
        self.trow = sb("tile_rows", [1, 3, XTILES])
        self.psT = psT
        self.psL = psLC[:, 0:T4 * E].rearrange("p (j e) -> p j e", e=E)
        self.psC = psLC[:, T4 * E:(2 * T4 + 1) * E].rearrange("p (j e) -> p j e", e=E)
        self.stats_done, self.aggr_done, self.var_ready, self.rstd_ready = (
            sem("r_stats_done"), sem("r_aggr_done"), sem("r_var_ready"), sem("r_rstd_ready"))
        self.normed, self.transposed, self.x_ready, self.logits_done = (
            sem("r_normed"), sem("r_transposed"), sem("r_x_ready"), sem("r_logits_done"))
        self.step = sem("r_step")
        self.d_ready, self.exps_done, self.both_ready, self.counted = (
            sem("r_less_max_ready"), sem("r_exps_done"), sem("r_both_ready"), sem("r_counted"))
        self.idx_ready, self.rows_ready, self.zeroed = sem("r_idx_ready"), sem("r_rows_ready"), sem("r_zeroed")
        self.sent = [sem(f"r_sent{b}") for b in range(2)]

    RANK, PLACE = 13, 5
    STEPS = RANK + PLACE

    def rstd(self, pool):
        def part(i, b, h):
            pool.wait_ge(self.var_ready, i + 1)
            pool.tensor_tensor(self.rs[b][:], self.rv[:], self.m.half[:], ALU.pow).then_inc(self.rstd_ready, 1)
        return part

    def send(self, pool):
        def part(i, b, h):
            pool.wait_ge(self.idx_ready, i + 1)
            pool.sem_inc(self.m.carrier, 1)
            for j in range(T4):
                for k in range(2):
                    pool.indirect_dma_start(self.xs, bass.IndirectOffsetOnAxis(ap=self.idx[b][:, k, j:j + 1], axis=0),
                                            self.nt[b][:, j, :], None).then_inc(self.sent[b], 16)
        return part

    def all_sent(self, pool):
        for b in range(2):
            pool.wait_ge(self.sent[b], SEQS // 2 * T4 * 2 * 16)

    def stats(self, dve):
        def part(i, b, h):
            dve.wait_ge(self.x_updated, i + 1)
            dve.sem_inc(self.m.carrier, 1)
            for j in range(T4):
                last = dve.bn_stats(self.st[:, j, :], self.m.X[:, i * T4 + j, :])
            last.then_inc(self.stats_done, 1)
            dve.wait_ge(self.stats_done, i + 1)
            dve.sem_inc(self.m.carrier, 1)
            for j in range(T4):
                last = dve.bn_aggr(self.mv[b][:, j, :], self.st[:, j, :])
            last.then_inc(self.aggr_done, 1)
            dve.wait_ge(self.aggr_done, i + 1)
            if past(i, 1):
                dve.wait_ge(self.rstd_ready, i)
            dve.tensor_scalar(self.rv[:], self.mv[b][:, :, 1], 1.0, LN_EPS, ALU.mult, ALU.add).then_inc(self.var_ready, 1)
        return part

    def normalize(self, dve):
        def part(i, b, h):
            dve.wait_ge(self.rstd_ready, i + 1)
            if past(h, 1):
                dve.wait_ge(self.sent[b], h * (T4 * 2 * 16))
            for j in range(T4):
                last = dve.tensor_scalar(self.nt[b][:, j, :], self.m.X[:, i * T4 + j, :], self.mv[b][:, j, 0:1],
                                         self.rs[b][:, j:j + 1], ALU.subtract, ALU.mult)
            last.then_inc(self.normed, 1)
        return part

    def rank(self, dve):
        m, lg, lg2, mx, eq, first, mask, d = self.m, self.lg, self.lg2, self.mx, self.eq, self.first, self.mask, self.d
        im8 = m.const[:, C_IM8:C_IM8 + E].unsqueeze(1).to_broadcast([P, T4, E])

        def over(x):
            return x.unsqueeze(2).to_broadcast([P, T4, E])

        def part(i, b, h):
            n = [0]

            def done(ins):
                n[0] += 1
                ins.then_inc(self.step, 1)
                dve.wait_ge(self.step, i * self.STEPS + n[0])

            dve.wait_ge(self.logits_done, i + 1)
            done(dve.tensor_copy(lg[:], self.psL))
            done(dve.tensor_reduce(mx[:, 0, :], lg[:], AX, ALU.max))
            dve.tensor_tensor(d[:, :, 0:E], lg[:], over(mx[:, 0, :]), ALU.subtract)
            done(dve.tensor_tensor(eq[:], lg[:], over(mx[:, 0, :]), ALU.is_equal))
            done(dve.tensor_tensor(eq[:], eq[:], im8, ALU.mult))
            done(dve.tensor_reduce(first[:, 0, :], eq[:], AX, ALU.min))
            done(dve.tensor_tensor(mask[:, 0], im8, over(first[:, 0, :]), ALU.is_equal))
            done(dve.scalar_tensor_tensor(lg2[:], mask[:, 0], -3e38, lg[:], ALU.mult, ALU.add))
            done(dve.tensor_reduce(mx[:, 1, :], lg2[:], AX, ALU.max))
            dve.tensor_tensor(d[:, :, E], mx[:, 1, :], mx[:, 0, :], ALU.subtract).then_inc(self.d_ready, 1)
            done(dve.tensor_tensor(eq[:], lg2[:], over(mx[:, 1, :]), ALU.is_equal))
            done(dve.tensor_tensor(eq[:], eq[:], im8, ALU.mult))
            done(dve.tensor_reduce(first[:, 1, :], eq[:], AX, ALU.min))
            done(dve.tensor_tensor(mask[:, 1], im8, over(first[:, 1, :]), ALU.is_equal))
            done(dve.tensor_tensor(self.both[:], mask[:, 0], mask[:, 1], ALU.add))
            assert n[0] == self.RANK, n[0]
        return part

    def place(self, dve):
        m = self.m

        def part(i, b, h):
            n = [self.RANK]

            def done(ins):
                n[0] += 1
                ins.then_inc(self.step, 1)
                dve.wait_ge(self.step, i * self.STEPS + n[0])

            dve.wait_ge(self.exps_done, i + 1)
            done(dve.tensor_reduce(self.ssum[:], self.ex[:, :, 0:E], AX, ALU.add))
            done(dve.reciprocal(self.inv[:], self.ssum[:]))
            g = tiles(m.gates, i)
            dve.tensor_copy(g[:, :, 0], self.inv[:])
            dve.tensor_tensor(g[:, :, 1], self.ex[:, :, E], self.inv[:], ALU.mult)
            dve.wait_ge(self.counted, i + 1)
            done(dve.tensor_tensor(self.pk[:], self.psC[:, 0:T4, :].unsqueeze(1).to_broadcast([P, 2, T4, E]), self.mask[:], ALU.mult))
            dve.tensor_copy(m.carry[:], self.psC[:, T4, :])
            done(dve.tensor_reduce(self.pf[:], self.pk[:], AX, ALU.add))
            if past(h, 1):
                dve.wait_ge(self.sent[b], h * (T4 * 2 * 16))
            dve.tensor_copy(self.idx[b][:], self.pf[:]).then_inc(self.idx_ready, 1)
            done(dve.tensor_copy(tiles(m.slot, i), self.pf[:].rearrange("p k t -> p t k")))
            assert n[0] == self.STEPS, n[0]
        return part

    def copy(self, act):
        def part(i, b, h):
            act.wait_ge(self.transposed, i + 1)
            if past(i, 1):
                act.wait_ge(self.logits_done, i)
            act.activation(self.xf[:], self.psT[:], ACT.Copy).then_inc(self.x_ready, 1)
        return part

    def exps(self, act):
        def part(i, b, h):
            act.wait_ge(self.d_ready, i + 1)
            if past(i, 1):
                act.wait_ge(self.step, i * self.STEPS)
            act.activation(self.ex[:], self.d[:], ACT.Exp).then_inc(self.exps_done, 1)
        return part

    def transpose(self, pe):
        def part(i, b, h):
            pe.wait_ge(self.normed, i + 1)
            if past(i, 1):
                pe.wait_ge(self.x_ready, i)
            for j in range(T4):
                last = pe.transpose(self.psT[:, j * P:(j + 1) * P], self.nt[b][:, j, :], self.m.ident)
            last.then_inc(self.transposed, 1)
        return part

    def logits(self, pe):
        def part(i, b, h):
            pe.wait_ge(self.x_ready, i + 1)
            if past(i, 1):
                pe.wait_ge(self.step, i * self.STEPS)
            for j in range(T4):
                last = pe.matmul(self.psL[:, j, :], self.xf[:, j * P:(j + 1) * P], self.m.wr[:], start=True, stop=True)
            last.then_inc(self.logits_done, 1)
        return part

    def count(self, pe):
        m = self.m

        def part(i, b, h):
            pe.wait_ge(self.step, i * self.STEPS + self.RANK)
            pe.matmul(self.psC, m.ident, m.carry[:].unsqueeze(1).to_broadcast([P, T4 + 1, E]),
                      start=True, stop=False, skip_group_check=True)
            for j in range(T4):
                later = self.both[:, j, :].unsqueeze(1).to_broadcast([P, T4 - j, E])
                pe.matmul(self.psC[:, j + 1:, :], m.ones[:], later, start=False, stop=False, skip_group_check=True)
            pe.matmul(self.psC[:, 0:T4, :], m.const[:, C_UP:C_UP + P], self.both[:],
                      start=False, stop=True, skip_group_check=True).then_inc(self.counted, 1)
        return part

    def begin(self, dve):
        dve.tensor_copy(self.m.carry[:], self.m.const[:, C_BASE:C_BASE + E])

    def plan(self, dve):
        m, trow, moved = self.m, self.trow, self.moved
        n = [0]

        def link(ins):
            n[0] += 1
            ins.then_inc(self.step, 1)
            dve.wait_ge(self.step, SEQS * self.STEPS + n[0])

        dve.wait_ge(self.step, SEQS * self.STEPS)
        base = m.const[:, C_BASE:C_BASE + E]
        cnt, nt8, inc8, exc8, rb, drop = (self.small[:, k, :] for k in range(6))
        link(dve.tensor_copy(m.tail_row[:], m.carry[0:1, :]))
        link(dve.tensor_tensor(cnt, m.carry[:], base, ALU.subtract))
        link(dve.tensor_tensor(self.cmp16[:], cnt.unsqueeze(2).to_broadcast([P, E, 16]),
                               m.const[:, C_TILE0:C_TILE0 + 16].unsqueeze(1).to_broadcast([P, E, 16]), ALU.is_gt))
        link(dve.tensor_reduce(nt8, self.cmp16[:], AX, ALU.add))
        link(dve.tensor_tensor_scan(inc8, m.ones[:, 0:E], nt8, 0.0, ALU.mult, ALU.add))
        link(dve.tensor_tensor(exc8, inc8, nt8, ALU.subtract))
        link(dve.scalar_tensor_tensor(rb, exc8, -float(ROWS), base, ALU.mult, ALU.add))
        link(dve.tensor_tensor(drop[:, 1:E], rb[:, 0:E - 1], rb[:, 1:E], ALU.subtract))
        jj = m.const[0:1, C_J:C_J + XTILES].unsqueeze(2).to_broadcast([1, XTILES, E])

        def by_tile(x):
            return x.unsqueeze(1).to_broadcast([1, XTILES, E])

        after, begun, own, roff, sel = (self.tile_w[:, k] for k in range(5))
        dve.tensor_tensor(after, jj, by_tile(inc8[0:1]), ALU.is_ge)
        dve.tensor_scalar(trow[:, 0, :], m.const[0:1, C_J:C_J + XTILES], float(ROWS), -float(DUMMY), ALU.mult, ALU.add)
        link(dve.tensor_tensor(begun, jj, by_tile(exc8[0:1]), ALU.is_ge))
        link(dve.tensor_tensor(own, begun, after, ALU.subtract))
        link(dve.tensor_tensor(roff, trow[:, 0, :].unsqueeze(2).to_broadcast([1, XTILES, E]), by_tile(rb[0:1]), ALU.add))
        link(dve.tensor_tensor(sel, own, roff, ALU.mult))
        dve.tensor_reduce(trow[:, 1, :], sel, AX, ALU.add)
        link(dve.tensor_reduce(trow[:, 2, :], after, AX, ALU.add))
        dve.tensor_scalar(m.tile_row[:], trow[:, 1, :], float(DUMMY), None, ALU.add)
        dve.tensor_scalar(m.tile_expert[:], trow[:, 2, :], float(E - 1), None, ALU.min).then_inc(self.rows_ready, 1)
        slots = m.slot[:].rearrange("p t k -> p (t k)")
        last_slot = slots
        for e in range(1, E):
            link(dve.tensor_scalar(moved[0][:], slots, float(e * CAP), drop[:, e:e + 1], ALU.is_ge, ALU.mult))
            link(dve.tensor_tensor(moved[1][:], moved[0][:], last_slot, ALU.add))
            last_slot = moved[1][:]
        dve.tensor_copy(m.pos[:].rearrange("p t k -> p (t k)"), last_slot)

    def zero_tails(self, sp):
        rows = self.xs[DUMMY:DUMMY + ROWS, :].rearrange("(p r) d -> p (r d)", p=P)
        sp.dma_start(rows, self.m.zeros[:]).then_inc(self.zeroed, 16)
        sp.wait_ge(self.step, SEQS * self.STEPS + 1)
        for e in range(E):
            r = sp.value_load(self.m.tail_row[0:1, e:e + 1], min_val=e * CAP, max_val=e * CAP + TILES * P)
            rows = self.xs[bass.ds(r, ROWS), :].rearrange("(p r) d -> p (r d)", p=P)
            sp.dma_start(rows, self.m.zeros[:]).then_inc(self.zeroed, 16)
        sp.wait_ge(self.zeroed, (E + 1) * 16)


def experts(nc, m, xs, ys, moe_up, moe_b, moe_down, tag):
    ctx, sb, sem = phase(nc, tag)
    with ctx:
        H = HID * P
        w = [sb(f"w_up{b}", [P, 2 * H]) for b in range(2)]
        wh = [sb(f"w_up_high{b}", [P, 2 * H], FP32R) for b in range(2)]
        wl = [sb(f"w_up_low{b}", [P, 2 * H], FP32R) for b in range(2)]
        bu = [sb(f"b1_bg{b}", [P, 2 * HID]) for b in range(2)]
        wd = [sb(f"w_down{b}", [P, H + P]) for b in range(2)]
        xt = [sb(f"x_tm{b}", [P, T4, P]) for b in range(2)]
        xh = [sb(f"x_high{b}", [P, ROWS], FP32R) for b in range(2)]
        xl = [sb(f"x_low{b}", [P, ROWS], FP32R) for b in range(2)]
        gl = [sb(f"gelu{b}", [P, ROWS]) for b in range(2)]
        hd = [sb(f"hidden{b}", [P, HID, ROWS]) for b in range(2)]
        yt = [sb(f"y_tm{b}", [P, T4, P]) for b in range(2)]
        psT, psG, psU, psY = m.banks[0], m.banks[1:3], m.banks[3:5], m.banks[5:7]
        w_in, x_in, b_in, y_out = ([sem(f"{k}{b}") for b in range(2)] for k in ("w_in", "x_in", "b_in", "y_out"))
        wh_ready, wl_ready = sem("w_high_ready"), sem("w_low_ready")
        transposed, xh_ready, xl_ready, gate_done, up_done = (
            sem("transposed"), sem("x_high_ready"), sem("x_low_ready"), sem("gate_done"), sem("up_done"))
        gelu_done, h_ready = sem("gelu_done"), sem("h_ready")
        down_done, y_ready = sem("down_done"), sem("y_ready")
        block = ctx.enter_context(nc.Block())

        @block.sync
        def _(sp):
            def expert(i, t):
                e = sp.value_load(m.tile_expert[0:1, bass.ds(i, 1)], min_val=0, max_val=E - 1)
                return t[bass.ds(e, 1), :, :].rearrange("a p c -> (a p) c")

            def load_w(i, b, h):
                src = expert(i, moe_up)
                if past(i, 2):
                    sp.wait_ge(wl_ready, i - 1)
                sp.dma_start(w[b][:], src).then_inc(w_in[b], 16)

            def load_x(i, b, h):
                r = sp.value_load(m.tile_row[0:1, bass.ds(i, 1)], min_val=0, max_val=DUMMY)
                if past(i, 2):
                    sp.wait_ge(transposed, i - 1)
                sp.dma_start(xt[b][:], xs[bass.ds(r, ROWS), :].rearrange("(p r) d -> p r d", p=P)).then_inc(x_in[b], 16)

            def load_biases(i, b, h):
                src = expert(i, moe_b)
                if past(i, 2):
                    sp.wait_ge(h_ready, (i - 1) * HID)
                sp.dma_start(bu[b][:], src).then_inc(b_in[b], 16)

            def load_down(i, b, h):
                src = expert(i, moe_down)
                if past(i, 2):
                    sp.wait_ge(y_ready, i - 1)
                sp.dma_start(wd[b][:], src).then_inc(b_in[b], 16)

            pipelined(sp, XTILES, (0, load_w), (0, load_x), (1, load_biases), (1, load_down))

        @block.gpsimd
        def _(pool):
            def low(i, b, h):
                pool.wait_ge(wh_ready, i + 1)
                if past(i, 2):
                    pool.wait_ge(up_done, (i - 1) * HID)
                pool.tensor_tensor(wl[b][:], w[b][:], wh[b][:], ALU.subtract).then_inc(wl_ready, 1)

            def store(i, b, h):
                pool.wait_ge(y_ready, i + 1)
                pool.dma_start(ys[bass.ds(i * ROWS, ROWS), :].rearrange("(p r) d -> p r d", p=P), yt[b][:]).then_inc(y_out[b], 16)

            pipelined(pool, XTILES, (1, low), (3, store))
            for b in range(2):
                pool.wait_ge(y_out[b], XTILES // 2 * 16)

        @block.tensor
        def _(pe):
            def transpose(i, b, h):
                pe.wait_ge(x_in[b], h * 16 + 16)
                if past(i, 1):
                    pe.wait_ge(xl_ready, i)
                for j in range(T4):
                    last = pe.transpose(psT[:, j * P:(j + 1) * P], xt[b][:, j, :], m.ident)
                last.then_inc(transposed, 1)

            def product(out, lhs, rhs):
                (lh, ll), (rh, rl) = lhs, rhs
                pe.matmul(out, lh, rh, start=True, stop=False)
                pe.matmul(out, lh, rl, start=False, stop=False)
                return pe.matmul(out, ll, rh, start=False, stop=True)

            def up(chunks):
                def part(i, b, h):
                    if chunks[0] == 0:
                        pe.wait_ge(wl_ready, i + 1)
                        pe.wait_ge(xl_ready, i + 1)
                    for c in chunks:
                        if past(i, 1) or c > 1:
                            pe.wait_ge(h_ready, i * HID + c - 1)
                        x = (xh[b][:], xl[b][:])
                        wg, w1 = (slice(k * H + c * P, k * H + (c + 1) * P) for k in (1, 0))
                        product(psG[c % 2][:], (wh[b][:, wg], wl[b][:, wg]), x).then_inc(gate_done, 1)
                        product(psU[c % 2][:], (wh[b][:, w1], wl[b][:, w1]), x).then_inc(up_done, 1)
                return part

            def down(i, b, h):
                pe.wait_ge(b_in[b], h * 32 + 32)
                pe.wait_ge(h_ready, (i + 1) * HID)
                if past(i, 2):
                    pe.wait_ge(y_ready, i - 1)
                for j in range(T4):
                    for c in range(HID):
                        last = pe.matmul(psY[b][:, j * P:(j + 1) * P], hd[b][:, c, j * P:(j + 1) * P],
                                         wd[b][:, c * P:(c + 1) * P], start=c == 0, stop=c == HID - 1)
                last.then_inc(down_done, 1)

            pipelined(pe, XTILES, (1, transpose), (2, up((0, 1))), (3, down), (2, up((2, 3))))

        @block.scalar
        def _(act):
            def x_high(i, b, h):
                act.wait_ge(transposed, i + 1)
                if past(i, 2):
                    act.wait_ge(up_done, (i - 1) * HID)
                act.activation(xh[b][:], psT[:], ACT.Copy).then_inc(xh_ready, 1)

            def w_high(i, b, h):
                act.wait_ge(w_in[b], h * 16 + 16)
                if past(i, 2):
                    act.wait_ge(up_done, (i - 1) * HID)
                act.activation(wh[b][:], w[b][:], ACT.Copy).then_inc(wh_ready, 1)

            def gelu(chunks):
                def part(i, b, h):
                    if chunks[0] == 0:
                        act.wait_ge(b_in[b], h * 32 + 32)
                    for c in chunks:
                        act.wait_ge(gate_done, i * HID + c + 1)
                        if past(i, 1) or c > 1:
                            act.wait_ge(h_ready, i * HID + c - 1)
                        act.activation(gl[c % 2][:], psG[c % 2][:], ACT.Gelu, bias=bu[b][:, HID + c:HID + c + 1]).then_inc(gelu_done, 1)
                return part

            pipelined(act, XTILES, (1, x_high), (2, gelu((0, 1))), (1, w_high), (2, gelu((2, 3))))

        @block.vector
        def _(dve):
            def x_low(i, b, h):
                dve.wait_ge(xh_ready, i + 1)
                dve.tensor_tensor(xl[b][:], psT[:], xh[b][:], ALU.subtract).then_inc(xl_ready, 1)

            def hidden(chunks):
                def part(i, b, h):
                    if chunks[0] == 0:
                        dve.wait_ge(b_in[b], h * 32 + 32)
                        if past(i, 2):
                            dve.wait_ge(down_done, i - 1)
                    for c in chunks:
                        dve.wait_ge(gelu_done, i * HID + c + 1)
                        dve.wait_ge(up_done, i * HID + c + 1)
                        dve.scalar_tensor_tensor(hd[b][:, c, :], psU[c % 2][:], bu[b][:, c:c + 1], gl[c % 2][:],
                                                 ALU.add, ALU.mult).then_inc(h_ready, 1)
                return part

            def bias(i, b, h):
                dve.wait_ge(b_in[b], h * 32 + 32)
                dve.wait_ge(down_done, i + 1)
                if past(h, 1):
                    dve.wait_ge(y_out[b], h * 16)
                b2 = wd[b][:, H:].unsqueeze(1).to_broadcast([P, T4, P])
                dve.tensor_tensor(yt[b][:], psY[b][:].rearrange("p (j c) -> p j c", c=P), b2, ALU.add).then_inc(y_ready, 1)

            pipelined(dve, XTILES, (1, x_low), (2, hidden((0, 1))), (3, bias), (2, hidden((2, 3))))


def combine_parts(m, ys, sem, sb):
    yy = [sb(f"y_rows{b}", [P, 2 * T4, P]) for b in range(2)]
    ix = [sb(f"slot_list{b}", [P, T4, 2], U32) for b in range(2)]
    gt = [sb(f"gates{b}", [P, T4, 2]) for b in range(2)]
    listed, combined = sem("listed"), sem("combined")
    fetched = [sem(f"fetched{b}") for b in range(2)]

    def lists(dve):
        def part(i, b, h):
            if past(h, 1):
                dve.wait_ge(fetched[b], h * (2 * T4 * 16))
            if past(i, 2):
                dve.wait_ge(combined, 2 * i - 2)
            dve.tensor_copy(gt[b][:], tiles(m.gates, i))
            dve.tensor_copy(ix[b][:], tiles(m.pos, i)).then_inc(listed, 1)
        return part

    def fetch(pool, js):
        def part(i, b, h):
            pool.wait_ge(listed, i + 1)
            if past(i, 2):
                pool.wait_ge(combined, 2 * i - 2)
            pool.sem_inc(m.carrier, 1)
            for j in js:
                for k in range(2):
                    pool.indirect_dma_start(yy[b][:, 2 * j + k, :], None, ys,
                                            bass.IndirectOffsetOnAxis(ap=ix[b][:, j, k:k + 1], axis=0)).then_inc(fetched[b], 16)
        return part

    def add(dve):
        def part(i, b, h):
            dve.wait_ge(fetched[b], h * (2 * T4 * 16) + 2 * T4 * 16)
            dve.wait_ge(listed, i + 1)
            for k in range(2):
                for j in range(T4):
                    x = m.X[:, i * T4 + j, :]
                    last = dve.scalar_tensor_tensor(x, yy[b][:, 2 * j + k, :], gt[b][:, j, k:k + 1], x, ALU.mult, ALU.add)
                last.then_inc(combined, 1)
                if k == 0:
                    dve.wait_ge(combined, 2 * i + 1)
        return part

    return lists, fetch, add, combined, fetched


def attention(nc, m, ys, xs):
    ctx, sb, sem = phase(nc, "attn")
    with ctx:
        lists, fetch, add, combined, fetched = combine_parts(m, ys, sem, sb)
        st = [sb(f"stats{b}", [P, T4, 6]) for b in range(2)]
        mv = [sb(f"mean_var{b}", [P, T4, 2]) for b in range(2)]
        rv = [sb(f"var_eps{b}", [P, T4]) for b in range(2)]
        rs = [sb(f"rstd{b}", [P, T4]) for b in range(2)]
        nt = [sb(f"normed{b}", [P, T4, P]) for b in range(2)]
        xf = [sb(f"x_fm{b}", [P, SEQ]) for b in range(2)]
        hq = [sb(f"hidden_qk{b}", [P, 2, SEQ]) for b in range(2)]
        vf = [sb(f"v_fm{b}", [P, SEQ]) for b in range(2)]
        gf = [sb(f"g_fm{b}", [P, SEQ]) for b in range(2)]
        ab = sb("abs", [P, 2, SEQ])
        ee = sb("exp_minus_abs", [P, 2, SEQ])
        ln = sb("log1p", [P, 2, SEQ])
        qk = [sb(f"q_k_tm{b}", [P, 2, SEQ]) for b in range(2)]
        am = sb("a_masked", [P, P])
        ai = sb("a_plus_identity", [P, P])
        zz = sb("z", [P, 2])
        of = sb("out_fm", [P, SEQ])
        ot = sb("out_turned", [P, SEQ])
        sf = [sb(f"out_prime_fm{b}", [P, SEQ]) for b in range(2)]
        psT, psH, psQ, psP = m.banks[0], m.banks[1:3], m.banks[3:5], m.banks[7]
        psA = psO = m.banks[6]
        wq1, wq2, wk1, wk2, wv, wg, wp = (m.wb[:, k * P:(k + 1) * P] for k in range(7))

        stats_done, aggr_done, var_ready, rstd_ready = sem("stats_done"), sem("aggr_done"), sem("var_ready"), sem("rstd_ready")
        normed, transposed, x_ready = sem("normed"), sem("transposed"), sem("x_ready")
        up_done, gelu_done = sem("up_done"), sem("gelu_done")
        qk_done, abs_done, exp_done, ln_done, qk_ready = (
            sem("qk_done"), sem("abs_done"), sem("exp_done"), sem("ln_done"), sem("qk_ready"))
        a_done, a_masked, a_ready, z_done, z_shift, z_ready = (
            sem("a_done"), sem("a_masked"), sem("a_ready"), sem("z_done"), sem("z_shift"), sem("z_ready"))
        o_done, gated, p_done, x_updated = sem("o_done"), sem("gated"), sem("p_done"), sem("x_updated")
        turned, prime_done, prime_ready = sem("turned"), sem("prime_done"), sem("prime_ready")
        route = Route(m, xs, sem, sb, x_updated, psP, m.banks[5])
        block = ctx.enter_context(nc.Block())

        @block.gpsimd
        def _(pool):
            def rstd(i, b, h):
                pool.wait_ge(var_ready, i + 1)
                pool.tensor_tensor(rs[b][:], rv[b][:], m.half[:], ALU.pow).then_inc(rstd_ready, 1)

            pipelined(pool, SEQS, (1, fetch(pool, (0, 1))), (7, route.rstd(pool)), (1, fetch(pool, (2, 3))), (8, route.send(pool)), (2, rstd))
            route.all_sent(pool)

        @block.vector
        def _(dve):
            def stats(i, b, h):
                dve.wait_ge(combined, 2 * i + 2)
                dve.sem_inc(m.carrier, 1)
                for j in range(T4):
                    last = dve.bn_stats(st[b][:, j, :], m.X[:, i * T4 + j, :])
                last.then_inc(stats_done, 1)

            def aggregate(i, b, h):
                dve.wait_ge(stats_done, i + 1)
                dve.sem_inc(m.carrier, 1)
                for j in range(T4):
                    last = dve.bn_aggr(mv[b][:, j, :], st[b][:, j, :])
                last.then_inc(aggr_done, 1)
                dve.wait_ge(aggr_done, i + 1)
                dve.tensor_scalar(rv[b][:], mv[b][:, :, 1], 1.0, LN_EPS, ALU.mult, ALU.add).then_inc(var_ready, 1)

            def normalize(i, b, h):
                dve.wait_ge(rstd_ready, i + 1)
                if past(i, 2):
                    dve.wait_ge(transposed, i - 1)
                for j in range(T4):
                    last = dve.tensor_scalar(nt[b][:, j, :], m.X[:, i * T4 + j, :], mv[b][:, j, 0:1], rs[b][:, j:j + 1],
                                             ALU.subtract, ALU.mult)
                last.then_inc(normed, 1)

            def softplus(i, b, h):
                dve.wait_ge(ln_done, i + 1)
                if past(i, 2):
                    dve.wait_ge(a_done, i - 1)
                for k in range(2):
                    last = dve.scalar_tensor_tensor(qk[b][:, k, :], psQ[k][:], 0.0, ln[:, k, :], ALU.max, ALU.add)
                last.then_inc(qk_ready, 1)

            def matrices(i, b, h):
                dve.wait_ge(a_done, i + 1)
                if past(i, 1):
                    dve.wait_ge(o_done, i)
                dve.tensor_tensor(am[:], psA[:, 0:P], m.const[:, C_HEAD:C_HEAD + P], ALU.mult).then_inc(a_masked, 1)
                dve.wait_ge(a_masked, i + 1)
                dve.tensor_tensor(ai[:], am[:], m.ident, ALU.add).then_inc(a_ready, 1)
                dve.wait_ge(z_done, i + 1)
                dve.tensor_scalar(zz[:, 0:1], psA[:, P:P + 1], float(P), None, ALU.add).then_inc(z_shift, 1)
                dve.wait_ge(z_shift, i + 1)
                dve.reciprocal(zz[:, 1:2], zz[:, 0:1]).then_inc(z_ready, 1)

            def outputs(i, b, h):
                dve.wait_ge(z_ready, i + 1)
                dve.wait_ge(o_done, i + 1)
                dve.scalar_tensor_tensor(of[:], psO[:], zz[:, 1:2], gf[b][:], ALU.mult, ALU.mult).then_inc(gated, 1)
                if past(i, 1):
                    dve.wait_ge(prime_done, i)
                dve.wait_ge(gated, i + 1)
                dve.transpose(ot[:].rearrange("p (q r n) -> p r q n", q=4, n=HD), of[:].rearrange("p (r q n) -> p r q n", q=4, n=HD)).then_inc(turned, 1)

            def update(i, b, h):
                dve.wait_ge(p_done, i + 1)
                xs = tiles(m.X, i)
                dve.tensor_tensor(xs, psP[:].rearrange("p (j c) -> p j c", c=P), xs, ALU.add).then_inc(x_updated, 1)

            route.begin(dve)
            pipelined(dve, SEQS, (6, matrices), (3, normalize), (8, route.place(dve)), (6, outputs), (7, route.normalize(dve)), (5, softplus), (2, add(dve)), (7, route.rank(dve)), (0, lists(dve)), (6, update), (6, route.stats(dve)), (2, stats), (2, aggregate))
            route.plan(dve)

        @block.scalar
        def _(act):
            def copy(i, b, h):
                act.wait_ge(transposed, i + 1)
                if past(i, 2):
                    act.wait_ge(up_done, (i - 1) * 4)
                act.activation(xf[b][:].rearrange("p (r j a) -> p j a r", r=16, j=T4), psT[:].rearrange("p (j a r) -> p j a r", j=T4, r=16),
                               ACT.Copy).then_inc(x_ready, 1)

            def primed(i, b, h):
                act.wait_ge(prime_done, i + 1)
                if past(i, 2):
                    act.wait_ge(p_done, i - 1)
                act.activation(sf[b][:].rearrange("p (j q t) -> p q j t", q=4, j=T4), psO[:].rearrange("p (q j t) -> p q j t", q=4, j=T4), ACT.Copy).then_inc(prime_ready, 1)

            def gelus(i, b, h):
                if past(i, 2):
                    act.wait_ge(qk_done, (i - 1) * 2)
                outs = (hq[b][:, 0, :], hq[b][:, 1, :], vf[b][:], gf[b][:])
                for c, (out, bias) in enumerate(zip(outs, (QB1, KB1, VB, GB))):
                    if c == 2 and past(i, 2):
                        act.wait_ge(gated, i - 1)
                    act.wait_ge(up_done, i * 4 + c + 1)
                    act.activation(out, psH[c % 2][:], ACT.Gelu, bias=m.col(bias)).then_inc(gelu_done, 1)

            def log1p(i, b, h):
                if past(i, 1):
                    act.wait_ge(exp_done, i)
                for k in range(2):
                    act.wait_ge(qk_done, i * 2 + k + 1)
                    last = act.activation(ab[:, k, :], psQ[k][:], ACT.Abs)
                last.then_inc(abs_done, 1)
                act.wait_ge(abs_done, i + 1)
                act.activation(ee[:], ab[:], ACT.Exp, scale=-1.0).then_inc(exp_done, 1)
                act.wait_ge(exp_done, i + 1)
                if past(i, 1):
                    act.wait_ge(qk_ready, i)
                act.activation(ln[:], ee[:], ACT.Ln, bias=1.0).then_inc(ln_done, 1)

            pipelined(act, SEQS, (4, copy), (4, gelus), (6, primed), (7, route.copy(act)), (4, log1p), (7, route.exps(act)))

        @block.sync
        def _(sp):
            route.zero_tails(sp)

        @block.tensor
        def _(pe):
            def transpose(i, b, h):
                pe.wait_ge(normed, i + 1)
                if past(i, 1):
                    pe.wait_ge(x_ready, i)
                for j in range(T4):
                    last = pe.transpose(psT[:, j * P:(j + 1) * P], nt[b][:, j, :], m.ident)
                last.then_inc(transposed, 1)

            def up(i, b, h):
                pe.wait_ge(x_ready, i + 1)
                for c, w in enumerate((wq1, wk1, wv, wg)):
                    if past(i, 1) or c > 1:
                        pe.wait_ge(gelu_done, i * 4 + c - 1)
                    pe.matmul(psH[c % 2][:], w, xf[b][:], start=True, stop=True).then_inc(up_done, 1)

            def second(k, w):
                def part(i, b, h):
                    pe.wait_ge(gelu_done, i * 4 + k + 1)
                    if past(i, 1):
                        pe.wait_ge(qk_ready, i)
                    pe.matmul(psQ[k][:], m.ones[0:1, :], m.rows[0:1, k, :], start=True, stop=False, skip_group_check=True)
                    for j in range(T4):
                        last = pe.matmul(psQ[k][:, j * P:(j + 1) * P], hq[b][:, k, j * P:(j + 1) * P], w,
                                         start=False, stop=j == T4 - 1, skip_group_check=True)
                    last.then_inc(qk_done, 1)
                return part

            def product(i, b, h):
                pe.wait_ge(qk_ready, i + 1)
                if past(i, 1):
                    pe.wait_ge(prime_ready, i)
                for j in range(T4):
                    last = pe.matmul(psA[:, 0:P], qk[b][:, 1, j * P:(j + 1) * P], qk[b][:, 0, j * P:(j + 1) * P],
                                     start=j == 0, stop=j == T4 - 1)
                last.then_inc(a_done, 1)

            def sums(i, b, h):
                pe.wait_ge(a_masked, i + 1)
                pe.matmul(psA[:, P:P + 1], am[:], m.ones[:, 0:1], start=True, stop=True).then_inc(z_done, 1)

            def outputs(i, b, h):
                pe.wait_ge(a_ready, i + 1)
                pe.wait_ge(z_shift, i + 1)
                pe.wait_ge(gelu_done, i * 4 + 4)
                pe.matmul(psO[:], ai[:], vf[b][:], start=True, stop=True).then_inc(o_done, 1)

            def prime(i, b, h):
                pe.wait_ge(turned, i + 1)
                for q in range(4):
                    last = pe.transpose(psO[:, q * P:(q + 1) * P], ot[:, q * P:(q + 1) * P], m.ident)
                last.then_inc(prime_done, 1)

            def project(i, b, h):
                pe.wait_ge(prime_ready, i + 1)
                if past(i, 1):
                    pe.wait_ge(x_updated, i)
                    pe.wait_ge(route.x_ready, i)
                pe.matmul(psP[:], m.ones[0:1, :], m.rows[0:1, 2, :], start=True, stop=False, skip_group_check=True)
                for j in range(T4):
                    last = pe.matmul(psP[:, j * P:(j + 1) * P], sf[b][:, j * P:(j + 1) * P], wp,
                                     start=False, stop=j == T4 - 1, skip_group_check=True)
                last.then_inc(p_done, 1)

            pipelined(pe, SEQS, (6, product), (8, route.count(pe)), (4, transpose), (6, sums), (6, outputs), (4, up), (6, prime), (7, route.transpose(pe)), (4, second(0, wq2)), (7, route.logits(pe)), (6, project), (4, second(1, wk2)))


def finish(nc, m, ys, out):
    ctx, sb, sem = phase(nc, "fin")
    with ctx:
        lists, fetch, add, combined, fetched = combine_parts(m, ys, sem, sb)
        stored = sem("stored")
        block = ctx.enter_context(nc.Block())
        ov = out.rearrange("(s t p) d -> s p t d", p=P, t=T4)

        @block.gpsimd
        def _(pool):
            pipelined(pool, SEQS, (0, fetch(pool, (0, 1, 2, 3))))

        @block.vector
        def _(dve):
            pipelined(dve, SEQS, (0, lists(dve)), (1, add(dve)))

        @block.sync
        def _(sp):
            def store(i, b, h):
                sp.wait_ge(combined, 2 * i + 2)
                dst = ov[i] if isinstance(i, int) else ov[bass.ds(i, 1)].rearrange("a p t d -> (a p) t d")
                sp.dma_start(dst, tiles(m.X, i)).then_inc(stored, 16)

            pipelined(sp, SEQS, (0, store))
            sp.wait_ge(stored, SEQS * 16)


def program(nc, x, vecs, consts, wa, wb, wr, rows, moe_up, moe_b, moe_down, out):
    xs = nc.dram_tensor("expert_rows_in", [DUMMY + ROWS, P], FP32, kind="Internal").ap()
    ys = nc.dram_tensor("expert_rows_out", [XTILES * ROWS, P], FP32, kind="Internal").ap()
    with ExitStack() as ctx:
        m = Memory(nc, ctx)
        setup(nc, m, x, vecs, consts, wa, wb, wr, rows)
        with nc.sbuf_tensor("after_time_mix", [P, TILES, P], FP32) as XP:
            time_mix(nc, m, XP)
            channel_mix(nc, m, XP, xs)
        experts(nc, m, xs, ys, moe_up, moe_b, moe_down, "experts1")
        attention(nc, m, ys, xs)
        experts(nc, m, xs, ys, moe_up, moe_b, moe_down, "experts2")
        finish(nc, m, ys, out)


def constants():
    import numpy as np
    c = np.zeros((P, NCONST), np.float32)
    c[:, C_ID:C_ID + P] = np.eye(P)
    c[:, C_UP:C_UP + P] = np.triu(np.ones((P, P)), 1)
    c[:, C_HEAD:C_HEAD + P] = np.kron(np.eye(HEADS), np.full((HD, HD), SCALE))
    c[:, C_IM8:C_IM8 + E] = np.arange(E) - 8
    c[:, C_TILE0:C_TILE0 + 16] = np.arange(16) * ROWS
    c[:, C_J:C_J + XTILES] = np.arange(XTILES)
    c[:, C_BASE:C_BASE + E] = np.arange(E) * CAP
    return c


def kernel(**inputs):
    import numpy as np
    import concourse.bacc as bacc
    from concourse.bass_utils import run_bass_kernel_spmd

    v = {k: np.asarray(a) for k, a in inputs.items()}
    A, B, F = "L0_attn_a_", "L0_attn_b_", "L0_ffn_"
    vec_names = [A + k for k in ("ln1_g", "ln1_b", "ln2_g", "ln2_b", "att_time_mix", "att_combined_mix", "time_decay",
                                 "time_first", "ffn_time_mix", "ffn_combined_mix")] + [B + k for k in ("q_b1", "k_b1", "v_b", "g_b")]
    hid = HID * P
    w1, wg = v[F + "w1_w"].transpose(0, 2, 1), v[F + "wg_w"].transpose(0, 2, 1)
    w2 = v[F + "w2_w"].transpose(0, 2, 1).reshape(E, HID, P, P).transpose(0, 2, 1, 3).reshape(E, P, hid)
    b1, bg = (v[F + k].reshape(E, HID, P).transpose(0, 2, 1) for k in ("w1_b", "wg_b"))
    b2 = np.broadcast_to(v[F + "w2_b"][:, None, :], (E, P, P))
    arrays = {
        "x": v[A + "x"].reshape(SEQS * SEQ, P),
        "vecs": np.stack([v[k].reshape(P) for k in vec_names], 1),
        "consts": constants(),
        "wa": np.concatenate([v[A + k].T for k in ("Wk", "Wv", "Wr", "Wo", "Fr", "Fk")]
                             + [v[A + "Fv"].T.reshape(HID, P, P).transpose(1, 0, 2).reshape(P, hid)], 1),
        "wb": np.concatenate([v[B + k].T for k in ("q_w1", "q_w2", "k_w1", "k_w2", "v_w", "g_w", "p_w")], 1),
        "wr": v[F + "router_w"].T,
        "rows": np.stack([np.tile(v[B + k], T4) for k in ("q_b2", "k_b2", "p_b")])[None],
        "moe_up": np.concatenate([w1, wg], 2),
        "moe_b": np.concatenate([b1, bg], 2),
        "moe_down": np.concatenate([w2, b2], 2),
    }
    arrays = {f"in_{k}": np.ascontiguousarray(a) for k, a in arrays.items()}
    nc = bacc.Bacc("TRN2", target_bir_lowering=False, num_devices=1)
    args = [nc.dram_tensor(k, list(a.shape), FP32, kind="ExternalInput").ap() for k, a in arrays.items()]
    out = nc.dram_tensor("out", [SEQS * SEQ, P], FP32, kind="ExternalOutput").ap()
    program(nc, *args, out)
    r = run_bass_kernel_spmd(nc, [arrays], core_ids=[0])
    return r.results[0]["out"].reshape(SEQS, SEQ, P)
```

```python
import concourse.bass as bass
from concourse import mybir
from contextlib import ExitStack

FP32 = mybir.dt.float32
FP32R = mybir.dt.float32r
I32 = mybir.dt.int32
U32 = mybir.dt.uint32
ALU = mybir.AluOpType
ACT = mybir.ActivationFunctionType
AX = mybir.AxisListType.X

P = 128
SEQS, SEQ = 16, 512
T4 = SEQ // P
TILES = SEQS * T4
HID = 4
E = 8
HEADS = 16
HD = P // HEADS
ROWS = 512
CAP = TILES * P + ROWS
DUMMY = E * CAP
XTILES = 2 * TILES * P // ROWS + E - 1
LN_EPS = 1e-5
K_CLAMP = 60.0
SCALE = float(HD) ** -0.5

(G1, B1, G2, B2, TM1, CM1, TD, TF, TM2, CM2, QB1, KB1, VB, GB) = range(14)
NVEC = 14
C_ID, C_UP, C_HEAD = 0, 128, 256
C_IM8 = 384
C_TILE0 = C_IM8 + E
C_J = C_TILE0 + 16
C_BASE = C_J + XTILES
C_TOKEN = C_BASE + E
NCONST = C_TOKEN + TILES
TOKENS = TILES * P
ROWW = P + 2
NOWHERE = 4.0 * TOKENS


def past(i, n):
    return not isinstance(i, int) or i >= n


def pipelined(eng, n, *parts):
    lag_max = max(lag for lag, _ in parts)
    head = (lag_max + 3) // 2 * 2
    end = n // 2 * 2

    def step(s):
        for lag, part in parts:
            if 0 <= s - lag < n:
                part(s - lag, (s - lag) % 2, (s - lag) // 2)

    for s in range(min(head, end)):
        step(s)
    if head < end:
        with eng.Fori(head // 2, end // 2) as h:
            for u in range(2):
                for lag, part in parts:
                    k = u - lag
                    part(h * 2 + k, k % 2, h + k // 2)
    for s in range(end, n + lag_max):
        step(s)


class Memory:

    def __init__(self, nc, ctx):
        def sb(name, shape, dt=FP32):
            return ctx.enter_context(nc.sbuf_tensor(name, shape, dt))

        self.X = sb("residual", [P, TILES, P])
        self.vec = sb("vectors", [P, NVEC])
        self.const = sb("constants", [P, NCONST])
        self.wa = sb("mix_weights", [P, 5 * P + 2 * HID * P])
        self.wb = sb("attention_weights", [P, 7 * P])
        self.wr = sb("router_weights", [P, E])
        self.rows = sb("bias_rows", [1, 3, T4 * P])
        self.ones = sb("ones", [P, P])
        self.gates = sb("gates", [P, TILES, 2])
        self.carry = sb("next_slot", [P, E])
        self.tile_first = sb("tile_first", [P, XTILES])
        self.tile_expert = sb("tile_expert", [1, XTILES], I32)
        self.tile_row = sb("tile_row", [1, XTILES], I32)
        self.tail_row = sb("tail_row", [1, E], I32)
        self.zeros = sb("zeros", [P, SEQ])
        self.filler = sb("filler_rows", [P, ROWS // P, ROWW])
        self.half = sb("minus_half", [P, T4])
        self.banks = [ctx.enter_context(nc.psum_tensor(f"bank{b}", [P, 512], FP32)) for b in range(8)]
        self.carrier = ctx.enter_context(nc.semaphore("carrier"))
        self.ident = self.const[:, C_ID:C_ID + P]

    def col(self, k):
        return self.vec[:, k:k + 1]


def phase(nc, tag):
    ctx = ExitStack()

    def sb(name, shape, dt=FP32):
        return ctx.enter_context(nc.sbuf_tensor(f"{tag}_{name}", shape, dt))

    def sem(name):
        return ctx.enter_context(nc.semaphore(f"{tag}_{name}"))

    return ctx, sb, sem


def setup(nc, m, vecs, consts, wa, wb, wr, rows):
    ctx, sb, sem = phase(nc, "setup")
    with ctx:
        loaded = sem("loaded")
        block = ctx.enter_context(nc.Block())

        @block.sync
        def _(sp):
            sp.dma_start(m.rows[:], rows).then_inc(loaded, 16)
            sp.dma_start(m.wb[:], wb).then_inc(loaded, 16)
            sp.dma_start(m.wr[:], wr).then_inc(loaded, 16)
            sp.wait_ge(loaded, 6 * 16)

        @block.scalar
        def _(act):
            act.dma_start(m.vec[:], vecs).then_inc(loaded, 16)
            act.dma_start(m.const[:], consts).then_inc(loaded, 16)
            act.dma_start(m.wa[:], wa).then_inc(loaded, 16)
            act.wait_ge(loaded, 6 * 16)

        @block.gpsimd
        def _(pool):
            pool.memset(m.ones[:], 1.0)
            pool.memset(m.zeros[:], 0.0)
            pool.memset(m.filler[:, :, 0:P], 0.0)
            pool.memset(m.filler[:, :, P:P + 1], NOWHERE)
            pool.memset(m.filler[:, :, P + 1:], 0.0)
            pool.memset(m.half[:], -0.5)


def time_mix(nc, m, x, XP):
    ctx, sb, sem = phase(nc, "tmix")
    with ctx:
        coef = sb("coefficients", [P, 11])
        TMG, TMB, CPREV, CNEXT, ED, EU, PG, PB, NG, NB, HALF = range(11)
        decay = sb("decay", [P, 2, SEQ + 1])
        st = [sb(f"stats{b}", [P, T4, 6]) for b in range(2)]
        mv = [sb(f"mean_var{b}", [P, T4, 2]) for b in range(2)]
        rv = [sb(f"var_eps{b}", [P, T4]) for b in range(2)]
        rs = [sb(f"rstd{b}", [P, T4]) for b in range(2)]
        nm = [sb(f"minus_mean{b}", [P, T4]) for b in range(2)]
        nb = [sb(f"minus_mean_rstd{b}", [P, T4]) for b in range(2)]
        nt = [sb(f"normed{b}", [P, T4, P]) for b in range(2)]
        xf = [sb(f"x_fm{b}", [P, SEQ]) for b in range(2)]
        xm = [sb(f"x_mixed{b}", [P, SEQ]) for b in range(2)]
        xp = [sb(f"x_times_prev{b}", [P, SEQ + 1]) for b in range(2)]
        xn = [sb(f"x_times_next{b}", [P, SEQ + 1]) for b in range(2)]
        sg = [sb(f"sigmoid_r{b}", [P, SEQ]) for b in range(2)]
        kc = sb("k_clamped", [P, SEQ])
        kk = [sb(f"k_kv{b}", [P, 2, SEQ + 1]) for b in range(2)]
        ab = sb("a_b", [P, 2, SEQ + 1])
        nd = sb("num_den", [P, 2, SEQ])
        th = [sb(f"tanh_r{b}", [P, SEQ]) for b in range(2)]
        rd = sb("one_over_den", [P, SEQ])
        y = [sb(f"y_fm{b}", [P, SEQ]) for b in range(2)]
        psT, psK, psV, psR, psO = m.banks[0:2], m.banks[2], m.banks[3], m.banks[4], m.banks[5:7]

        cleared, coef_a, coef_b = sem("cleared"), sem("coef_a"), sem("coef_b")
        x_in = [sem(f"x_in{b}") for b in range(2)]
        stats_done, aggr_done, var_ready, rstd_ready = sem("stats_done"), sem("aggr_done"), sem("var_ready"), sem("rstd_ready")
        shift_ready = sem("shift_ready")
        normed, transposed, scaled, x_ready = sem("normed"), sem("transposed"), sem("scaled"), sem("x_ready")
        mixed_prev, mixed, kvr_done = sem("mixed_prev"), sem("mixed"), sem("kvr_done")
        k_clamped, k_ready, tanh_ready, sigmoid_ready, kv_ready = (
            sem("k_clamped"), sem("k_ready"), sem("tanh_ready"), sem("sigmoid_ready"), sem("kv_ready"))
        scanned, num_den, recip_done, u_ready, y_ready = sem("scanned"), sem("num_den"), sem("recip_done"), sem("u_ready"), sem("y_ready")
        o_done, xp_ready = sem("o_done"), sem("xp_ready")
        block = ctx.enter_context(nc.Block())
        W = {k: m.wa[:, i * P:(i + 1) * P] for i, k in enumerate("kvro")}

        xv = x.rearrange("(s t p) d -> s p t d", p=P, t=T4)

        @block.sync
        def _(sp):
            def load(i, b, h):
                src = xv[i] if isinstance(i, int) else xv[bass.ds(i, 1)].rearrange("a p t d -> (a p) t d")
                if past(h, 1):
                    sp.wait_ge(x_in[b], h * 16)
                sp.dma_start(tiles(m.X, i), src).then_inc(x_in[b], 16)

            pipelined(sp, SEQS, (0, load))

        @block.gpsimd
        def _(pool):
            for b in range(2):
                pool.memset(kk[b][:, :, 0:1], 0.0)
                pool.memset(xp[b][:, 0:1], 0.0)
                pool.memset(xn[b][:, SEQ:], 0.0)
            pool.memset(decay[:, :, 0:1], 0.0).then_inc(cleared, 1)

            def rstd(i, b, h):
                pool.wait_ge(var_ready, i + 1)
                if past(i, 2):
                    pool.wait_ge(normed, i - 1)
                pool.tensor_tensor(rs[b][:], rv[b][:], m.half[:], ALU.pow).then_inc(rstd_ready, 1)
                pool.wait_ge(rstd_ready, i + 1)
                pool.tensor_tensor(nb[b][:], nm[b][:], rs[b][:], ALU.mult).then_inc(shift_ready, 1)

            def mix(i, b, h):
                pool.wait_ge(scaled, i + 1)
                pool.tensor_tensor(xm[b][:], xm[b][:], xp[b][:, 0:SEQ], ALU.add).then_inc(mixed_prev, 1)
                pool.wait_ge(mixed_prev, i + 1)
                pool.tensor_tensor(xm[b][:], xm[b][:], xn[b][:, 1:], ALU.add).then_inc(mixed, 1)

            def gate(i, b, h):
                pool.wait_ge(sigmoid_ready, i + 1)
                pool.wait_ge(num_den, i + 1)
                if past(i, 2):
                    pool.wait_ge(o_done, i - 1)
                pool.tensor_tensor(y[b][:], sg[b][:], nd[:, 0, :], ALU.mult).then_inc(u_ready, 1)

            pipelined(pool, SEQS, (3, mix), (4, gate), (0, rstd))

        @block.vector
        def _(dve):
            dve.tensor_tensor(coef[:, TMG:TMG + 1], m.col(TM1), m.col(G1), ALU.mult)
            dve.tensor_tensor(coef[:, TMB:TMB + 1], m.col(TM1), m.col(B1), ALU.mult)
            dve.tensor_scalar(coef[:, CPREV:CPREV + 1], m.col(TM1), -1.0, 1.0, ALU.mult, ALU.add)
            dve.memset(coef[0:64, CNEXT:CNEXT + 1], 0.0)
            dve.tensor_copy(coef[64:P, CNEXT:CNEXT + 1], m.vec[64:P, CM1:CM1 + 1]).then_inc(coef_a, 1)
            dve.wait_ge(coef_a, 1)
            dve.tensor_tensor(coef[0:64, CPREV:CPREV + 1], coef[0:64, CPREV:CPREV + 1], m.vec[0:64, CM1:CM1 + 1], ALU.add).then_inc(coef_a, 1)
            dve.memset(coef[:, HALF:HALF + 1], 0.5)
            dve.wait_ge(coef_a, 2)
            dve.tensor_tensor(coef[:, PG:PG + 1], coef[:, CPREV:CPREV + 1], m.col(G1), ALU.mult)
            dve.tensor_tensor(coef[:, PB:PB + 1], coef[:, CPREV:CPREV + 1], m.col(B1), ALU.mult)
            dve.tensor_tensor(coef[:, NG:NG + 1], coef[:, CNEXT:CNEXT + 1], m.col(G1), ALU.mult)
            dve.tensor_tensor(coef[:, NB:NB + 1], coef[:, CNEXT:CNEXT + 1], m.col(B1), ALU.mult).then_inc(coef_a, 1)
            dve.wait_ge(coef_b, 3)
            dve.tensor_scalar(decay[:, 0, 1:], m.zeros[:], coef[:, ED:ED + 1], None, ALU.add)
            dve.tensor_scalar(decay[:, 1, 1:], m.zeros[:], coef[:, ED:ED + 1], None, ALU.add).then_inc(coef_b, 1)
            dve.wait_ge(cleared, 1)
            dve.wait_ge(coef_b, 4)

            def stats(i, b, h):
                dve.wait_ge(x_in[b], h * 16 + 16)
                dve.sem_inc(m.carrier, 1)
                for j in range(T4):
                    last = dve.bn_stats(st[b][:, j, :], m.X[:, i * T4 + j, :])
                last.then_inc(stats_done, 1)

            def aggregate(i, b, h):
                if past(i, 2):
                    dve.wait_ge(shift_ready, i - 1)
                dve.wait_ge(stats_done, i + 1)
                dve.sem_inc(m.carrier, 1)
                for j in range(T4):
                    last = dve.bn_aggr(mv[b][:, j, :], st[b][:, j, :])
                last.then_inc(aggr_done, 1)
                dve.wait_ge(aggr_done, i + 1)
                dve.tensor_scalar(nm[b][:], mv[b][:, :, 0], -1.0, None, ALU.mult)
                dve.tensor_scalar(rv[b][:], mv[b][:, :, 1], 1.0 + LN_EPS, LN_EPS * LN_EPS, ALU.mult, ALU.add).then_inc(var_ready, 1)

            def clamp(i, b, h):
                dve.wait_ge(kvr_done, i + 1)
                if past(i, 1):
                    dve.wait_ge(k_ready, i)
                dve.tensor_scalar(kc[:], psK[:], K_CLAMP, None, ALU.min).then_inc(k_clamped, 1)

            def wkv(i, b, h):
                dve.wait_ge(k_ready, i + 1)
                dve.tensor_tensor(kk[b][:, 0, 1:], kk[b][:, 1, 1:], psV[:], ALU.mult).then_inc(kv_ready, 1)
                dve.wait_ge(kv_ready, i + 1)
                dve.tensor_tensor_scan(ab[:].rearrange("p s t -> p (s t)"), decay[:].rearrange("p s t -> p (s t)"),
                                       kk[b][:].rearrange("p s t -> p (s t)"), 0.0, ALU.mult, ALU.add).then_inc(scanned, 1)
                dve.wait_ge(scanned, i + 1)
                if past(i, 1):
                    dve.wait_ge(u_ready, i)
                dve.scalar_tensor_tensor(nd[:], kk[b][:, :, 1:], coef[:, EU:EU + 1], ab[:, :, 0:SEQ],
                                         ALU.mult, ALU.add).then_inc(num_den, 1)
                dve.wait_ge(num_den, i + 1)
                dve.reciprocal(rd[:], nd[:, 1, :]).then_inc(recip_done, 1)

            def divide(i, b, h):
                dve.wait_ge(recip_done, i + 1)
                dve.wait_ge(u_ready, i + 1)
                dve.tensor_tensor(y[b][:], y[b][:], rd[:], ALU.mult).then_inc(y_ready, 1)

            pipelined(dve, SEQS, (4, clamp), (0, stats), (4, wkv), (0, aggregate), (4, divide))

        @block.scalar
        def _(act):
            act.activation(coef[:, ED:ED + 1], m.col(TD), ACT.Exp).then_inc(coef_b, 1)
            act.activation(coef[:, EU:EU + 1], m.col(TF), ACT.Exp).then_inc(coef_b, 1)
            act.wait_ge(coef_b, 2)
            act.activation(coef[:, ED:ED + 1], coef[:, ED:ED + 1], ACT.Exp, scale=-1.0).then_inc(coef_b, 1)
            act.wait_ge(coef_a, 3)
            act.wait_ge(cleared, 1)

            def normalize(i, b, h):
                act.wait_ge(shift_ready, i + 1)
                if past(i, 2):
                    act.wait_ge(transposed, i - 1)
                for j in range(T4):
                    last = act.activation(nt[b][:, j, :], m.X[:, i * T4 + j, :], ACT.Identity, bias=nb[b][:, j:j + 1], scale=rs[b][:, j:j + 1])
                last.then_inc(normed, 1)

            def scale(i, b, h):
                act.wait_ge(transposed, i + 1)
                if past(i, 2):
                    act.wait_ge(kvr_done, i - 1)
                act.activation(xm[b][:], psT[b][:], ACT.Identity, bias=coef[:, TMB:TMB + 1], scale=coef[:, TMG:TMG + 1])
                act.activation(xp[b][:, 1:], psT[b][:], ACT.Identity, bias=coef[:, PB:PB + 1], scale=coef[:, PG:PG + 1])
                act.activation(xn[b][:, 0:SEQ], psT[b][:], ACT.Identity, bias=coef[:, NB:NB + 1],
                               scale=coef[:, NG:NG + 1]).then_inc(scaled, 1)

            def affine(i, b, h):
                act.wait_ge(transposed, i + 1)
                if past(i, 2):
                    act.wait_ge(o_done, i - 1)
                act.activation(xf[b][:], psT[b][:], ACT.Identity, bias=m.col(B1), scale=m.col(G1)).then_inc(x_ready, 1)

            def exponentials(i, b, h):
                act.wait_ge(k_clamped, i + 1)
                if past(i, 2):
                    act.wait_ge(num_den, i - 1)
                act.activation(kk[b][:, 1, 1:], kc[:], ACT.Exp).then_inc(k_ready, 1)
                if past(i, 2):
                    act.wait_ge(u_ready, i - 1)
                act.activation(th[b][:], psR[:], ACT.Tanh, scale=0.5).then_inc(tanh_ready, 1)
                act.wait_ge(tanh_ready, i + 1)
                act.activation(sg[b][:], th[b][:], ACT.Identity, bias=coef[:, HALF:HALF + 1], scale=0.5).then_inc(sigmoid_ready, 1)

            def store(i, b, h):
                act.wait_ge(o_done, i + 1)
                act.activation(XP[:, bass.ds(i * T4, T4), :] if not isinstance(i, int) else XP[:, i * T4:i * T4 + T4, :],
                               psO[b][:].rearrange("p (j c) -> p j c", c=P), ACT.Copy).then_inc(xp_ready, 1)

            pipelined(act, SEQS, (3, scale), (4, exponentials), (3, affine), (5, store), (1, normalize))

        @block.tensor
        def _(pe):
            def transpose(i, b, h):
                pe.wait_ge(normed, i + 1)
                if past(i, 2):
                    pe.wait_ge(x_ready, i - 1)
                for j in range(T4):
                    last = pe.transpose(psT[b][:, j * P:(j + 1) * P], nt[b][:, j, :], m.ident)
                last.then_inc(transposed, 1)

            def kvr(i, b, h):
                pe.wait_ge(mixed, i + 1)
                if past(i, 1):
                    pe.wait_ge(tanh_ready, i)
                if past(i, 1):
                    pe.wait_ge(kv_ready, i)
                pe.matmul(psK[:], W["k"], xm[b][:], start=True, stop=True)
                pe.matmul(psV[:], W["v"], xm[b][:], start=True, stop=True)
                pe.matmul(psR[:], W["r"], xm[b][:], start=True, stop=True).then_inc(kvr_done, 1)

            def project(i, b, h):
                pe.wait_ge(y_ready, i + 1)
                pe.wait_ge(x_ready, i + 1)
                if past(i, 2):
                    pe.wait_ge(xp_ready, i - 1)
                for j in range(T4):
                    out = psO[b][:, j * P:(j + 1) * P]
                    pe.matmul(out, y[b][:, j * P:(j + 1) * P], W["o"], start=True, stop=False)
                    last = pe.matmul(out, xf[b][:, j * P:(j + 1) * P], m.ident, start=False, stop=True)
                last.then_inc(o_done, 1)

            pipelined(pe, SEQS, (4, kvr), (5, project), (2, transpose))


def channel_mix(nc, m, XP, xs):
    ctx, sb, sem = phase(nc, "cmix")
    with ctx:
        coef = sb("coefficients", [P, 4])
        TMG, TMB, CPREV, CNEXT = range(4)
        st = [sb(f"stats{b}", [P, T4, 6]) for b in range(2)]
        mv = [sb(f"mean_var{b}", [P, T4, 2]) for b in range(2)]
        rv = [sb(f"var_eps{b}", [P, T4]) for b in range(2)]
        rs = [sb(f"rstd{b}", [P, T4]) for b in range(2)]
        nm = [sb(f"minus_mean{b}", [P, T4]) for b in range(2)]
        nb = [sb(f"minus_mean_rstd{b}", [P, T4]) for b in range(2)]
        nt = [sb(f"normed{b}", [P, T4, P]) for b in range(2)]
        xf = [sb(f"x_fm{b}", [P, SEQ + 2]) for b in range(2)]
        xm = [sb(f"x_mixed{b}", [P, SEQ]) for b in range(2)]
        rl = sb("relu", [P, 2, SEQ])
        kq = [sb(f"k_fm{b}", [P, HID, SEQ]) for b in range(2)]
        th = sb("tanh_r", [P, SEQ])
        u = sb("gated", [P, SEQ])
        w = sb("gated_plus_x", [P, SEQ])
        psT, psF, psKV, psG, psX = m.banks[0], m.banks[1:3], m.banks[3], m.banks[4], m.banks[5]

        coef_a = sem("coef_a")
        stats_done, aggr_done, var_ready, rstd_ready = sem("stats_done"), sem("aggr_done"), sem("var_ready"), sem("rstd_ready")
        shift_ready = sem("shift_ready")
        normed, transposed, scaled = sem("normed"), sem("transposed"), sem("scaled")
        mixed_prev, mixed = sem("mixed_prev"), sem("mixed")
        fk_done, relu_done, k_ready = sem("fk_done"), sem("relu_done"), sem("k_ready")
        out_done, tanh_ready, gated, summed, x_updated = sem("out_done"), sem("tanh_ready"), sem("gated"), sem("summed"), sem("x_updated")
        route = Route(m, xs, sem, sb, x_updated, m.banks[6], m.banks[7])
        block = ctx.enter_context(nc.Block())
        WR = m.wa[:, 4 * P:5 * P]
        FK = m.wa[:, 5 * P:5 * P + HID * P]
        FV = m.wa[:, (5 + HID) * P:]

        @block.gpsimd
        def _(pool):
            def rstd(i, b, h):
                pool.wait_ge(var_ready, i + 1)
                if past(i, 2):
                    pool.wait_ge(normed, i - 1)
                pool.tensor_tensor(rs[b][:], rv[b][:], m.half[:], ALU.pow).then_inc(rstd_ready, 1)
                pool.wait_ge(rstd_ready, i + 1)
                pool.tensor_tensor(nb[b][:], nm[b][:], rs[b][:], ALU.mult).then_inc(shift_ready, 1)

            pipelined(pool, SEQS, (5, route.send(pool)), (3, route.rstd(pool)), (0, rstd))
            route.all_sent(pool)

        @block.vector
        def _(dve):
            for b in range(2):
                dve.memset(xf[b][:, 0:1], 0.0)
                dve.memset(xf[b][:, SEQ + 1:SEQ + 2], 0.0)
            dve.tensor_tensor(coef[:, TMG:TMG + 1], m.col(TM2), m.col(G2), ALU.mult)
            dve.tensor_tensor(coef[:, TMB:TMB + 1], m.col(TM2), m.col(B2), ALU.mult)
            dve.tensor_scalar(coef[:, CPREV:CPREV + 1], m.col(TM2), -1.0, 1.0, ALU.mult, ALU.add)
            dve.tensor_copy(coef[:, CNEXT:CNEXT + 1], m.col(CM2)).then_inc(coef_a, 1)
            dve.wait_ge(coef_a, 1)
            dve.tensor_tensor(coef[0:64, CPREV:CPREV + 1], coef[0:64, CPREV:CPREV + 1], m.vec[0:64, CM2:CM2 + 1], ALU.add).then_inc(coef_a, 1)
            dve.wait_ge(coef_a, 2)

            def stats(i, b, h):
                for j in range(T4):
                    last = dve.bn_stats(st[b][:, j, :], XP[:, i * T4 + j, :])
                last.then_inc(stats_done, 1)

            def aggregate(i, b, h):
                if past(i, 2):
                    dve.wait_ge(shift_ready, i - 1)
                dve.wait_ge(stats_done, i + 1)
                dve.sem_inc(m.carrier, 1)
                for j in range(T4):
                    last = dve.bn_aggr(mv[b][:, j, :], st[b][:, j, :])
                last.then_inc(aggr_done, 1)
                dve.wait_ge(aggr_done, i + 1)
                dve.tensor_scalar(nm[b][:], mv[b][:, :, 0], -1.0, None, ALU.mult)
                dve.tensor_scalar(rv[b][:], mv[b][:, :, 1], 1.0, LN_EPS, ALU.mult, ALU.add).then_inc(var_ready, 1)

            def mix(i, b, h):
                dve.wait_ge(scaled, i + 1)
                dve.scalar_tensor_tensor(xm[b][:], xf[b][:, 0:SEQ], coef[:, CPREV:CPREV + 1], xm[b][:],
                                         ALU.mult, ALU.add).then_inc(mixed_prev, 1)
                dve.wait_ge(mixed_prev, i + 1)
                dve.scalar_tensor_tensor(xm[b][64:P, :], xf[b][64:P, 2:], coef[64:P, CNEXT:CNEXT + 1], xm[b][64:P, :],
                                         ALU.mult, ALU.add).then_inc(mixed, 1)

            def update(i, b, h):
                dve.wait_ge(tanh_ready, i + 1)
                dve.scalar_tensor_tensor(u[:], th[:], 1.0, psKV[:], ALU.add, ALU.mult).then_inc(gated, 1)
                dve.wait_ge(gated, i + 1)
                dve.scalar_tensor_tensor(w[:], u[:], 0.5, psX[:], ALU.mult, ALU.add).then_inc(summed, 1)
                dve.wait_ge(summed, i + 1)
                xs = tiles(m.X, i)
                dve.tensor_tensor(xs, w[:].rearrange("p (j c) -> p j c", c=P), xs, ALU.add).then_inc(x_updated, 1)

            route.begin(dve)
            pipelined(dve, SEQS, (5, route.place(dve)), (2, mix), (4, route.rank(dve)),
                      (3, update), (3, route.stats(dve)), (0, stats), (0, aggregate), (3, route.normalize(dve)))
            route.plan(dve)

        @block.scalar
        def _(act):
            act.wait_ge(coef_a, 2)

            def normalize(i, b, h):
                act.wait_ge(shift_ready, i + 1)
                if past(i, 2):
                    act.wait_ge(transposed, i - 1)
                for j in range(T4):
                    last = act.activation(nt[b][:, j, :], XP[:, i * T4 + j, :], ACT.Identity, bias=nb[b][:, j:j + 1], scale=rs[b][:, j:j + 1])
                last.then_inc(normed, 1)

            def affine(i, b, h):
                act.wait_ge(transposed, i + 1)
                if past(i, 2):
                    act.wait_ge(out_done, i - 1)
                act.activation(xf[b][:, 1:SEQ + 1], psT[:], ACT.Identity, bias=m.col(B2), scale=m.col(G2))
                act.activation(xm[b][:], psT[:], ACT.Identity, bias=coef[:, TMB:TMB + 1],
                               scale=coef[:, TMG:TMG + 1]).then_inc(scaled, 1)

            def relu(pair):
                def part(i, b, h):
                    for c in pair:
                        act.wait_ge(fk_done, i * HID + c + 1)
                        if past(i, 1) or c > 1:
                            act.wait_ge(k_ready, i * 2 + c // 2)
                        act.activation(rl[:, c % 2, :], psF[c % 2][:], ACT.Relu).then_inc(relu_done, 1)
                    act.wait_ge(relu_done, i * HID + pair[-1] + 1)
                    if past(i, 2):
                        act.wait_ge(out_done, i - 1)
                    act.activation(kq[b][:, pair[0]:pair[0] + 2, :], rl[:], ACT.Square).then_inc(k_ready, 1)
                return part

            def gate(i, b, h):
                act.wait_ge(out_done, i + 1)
                if past(i, 1):
                    act.wait_ge(gated, i)
                act.activation(th[:], psG[:], ACT.Tanh, scale=0.5).then_inc(tanh_ready, 1)

            pipelined(act, SEQS, (5, route.exps(act)), (2, affine), (4, route.copy(act)), (3, gate), (1, normalize),
                      (2, relu((0, 1))), (2, relu((2, 3))))

        @block.sync
        def _(sp):
            route.fill_tails(sp)

        @block.tensor
        def _(pe):
            def transpose(i, b, h):
                pe.wait_ge(normed, i + 1)
                if past(i, 1):
                    pe.wait_ge(scaled, i)
                for j in range(T4):
                    last = pe.transpose(psT[:, j * P:(j + 1) * P], nt[b][:, j, :], m.ident)
                last.then_inc(transposed, 1)

            def up(i, b, h):
                pe.wait_ge(mixed, i + 1)
                for c in range(HID):
                    if past(i, 1) or c > 1:
                        pe.wait_ge(relu_done, i * HID + c - 1)
                    pe.matmul(psF[c % 2][:], FK[:, c * P:(c + 1) * P], xm[b][:], start=True, stop=True).then_inc(fk_done, 1)

            def down(js):
                def part(i, b, h):
                    pe.wait_ge(k_ready, (i + 1) * 2)
                    if past(i, 1):
                        pe.wait_ge(summed, i)
                    for j in js:
                        for c in range(HID):
                            pe.matmul(psKV[:, j * P:(j + 1) * P], kq[b][:, c, j * P:(j + 1) * P], FV[:, c * P:(c + 1) * P],
                                      start=c == 0, stop=c == HID - 1)
                return part

            def gate_and_x(i, b, h):
                for j in range(T4):
                    pe.matmul(psG[:, j * P:(j + 1) * P], xm[b][:, j * P:(j + 1) * P], WR, start=True, stop=True)
                for j in range(T4):
                    last = pe.matmul(psX[:, j * P:(j + 1) * P], xf[b][:, 1 + j * P:1 + (j + 1) * P], m.ident,
                                     start=True, stop=True)
                last.then_inc(out_done, 1)

            pipelined(pe, SEQS, (5, route.count(pe)), (3, down((0, 1))), (3, down((2, 3))), (4, route.transpose(pe)),
                      (3, gate_and_x), (4, route.logits(pe)), (2, up), (1, transpose))


def tiles(t, i):
    if isinstance(i, int):
        return t[:, i * T4:(i + 1) * T4, :]
    return t[:, bass.ds(i * T4, T4), :]


class Route:

    def __init__(self, m, xs, sem, sb, x_updated, psT, psLC):
        self.m, self.xs, self.x_updated = m, xs, x_updated
        self.st = sb("r_stats", [P, T4, 6])
        self.mv = [sb(f"r_mean_var{b}", [P, T4, 2]) for b in range(2)]
        self.rv = sb("r_var_eps", [P, T4])
        self.rs = [sb(f"r_rstd{b}", [P, T4]) for b in range(2)]
        self.nt = [sb(f"r_normed{b}", [P, T4, ROWW]) for b in range(2)]
        self.xf = sb("r_x_fm", [P, SEQ])
        self.lg = sb("logits", [P, T4, E])
        self.lg2 = sb("logits_but_max", [P, T4, E])
        self.mx = sb("max_1_2", [P, 2, T4])
        self.eq = sb("equals", [P, T4, E])
        self.first = sb("first", [P, 2, T4])
        self.mask = sb("masks", [P, 2, T4, E])
        self.both = sb("both_masks", [P, T4, E])
        self.d = sb("less_max", [P, T4, E + 1])
        self.ex = sb("exps", [P, T4, E + 1])
        self.ssum = sb("exp_sum", [P, T4])
        self.inv = sb("exp_sum_inverse", [P, T4])
        self.pk = sb("slot_masked", [P, 2, T4, E])
        self.pf = sb("slots_float", [P, 2, T4])
        self.idx = [sb(f"slot_lists{b}", [P, 2, T4], U32) for b in range(2)]
        self.tile_w = sb("tile_work", [P, 5, XTILES, E])
        self.small = sb("small_work", [P, 5, E])
        self.cmp16 = sb("count_compare", [P, E, 16])
        self.trow = sb("tile_rows", [P, 3, XTILES])
        self.psT = psT
        self.psL = psLC[:, 0:T4 * E].rearrange("p (j e) -> p j e", e=E)
        self.psC = psLC[:, T4 * E:(2 * T4 + 1) * E].rearrange("p (j e) -> p j e", e=E)
        self.stats_done, self.aggr_done, self.var_ready, self.rstd_ready = (
            sem("r_stats_done"), sem("r_aggr_done"), sem("r_var_ready"), sem("r_rstd_ready"))
        self.normed, self.transposed, self.x_ready, self.logits_done = (
            sem("r_normed"), sem("r_transposed"), sem("r_x_ready"), sem("r_logits_done"))
        self.step = sem("r_step")
        self.d_ready, self.exps_done, self.counted = sem("r_less_max_ready"), sem("r_exps_done"), sem("r_counted")
        self.idx_ready, self.rows_ready, self.filled = sem("r_idx_ready"), sem("r_rows_ready"), sem("r_filled")
        self.sent = [sem(f"r_sent{b}") for b in range(2)]

    RANK, PLACE = 13, 4
    STEPS = RANK + PLACE

    def rstd(self, pool):
        def part(i, b, h):
            pool.wait_ge(self.var_ready, i + 1)
            pool.tensor_tensor(self.rs[b][:], self.rv[:], self.m.half[:], ALU.pow).then_inc(self.rstd_ready, 1)
        return part

    def send(self, pool):
        def part(i, b, h):
            pool.wait_ge(self.idx_ready, i + 1)
            pool.sem_inc(self.m.carrier, 1)
            for j in range(T4):
                for k in range(2):
                    pool.indirect_dma_start(self.xs, bass.IndirectOffsetOnAxis(ap=self.idx[b][:, k, j:j + 1], axis=0),
                                            self.nt[b][:, j, :], None).then_inc(self.sent[b], 16)
        return part

    def all_sent(self, pool):
        for b in range(2):
            pool.wait_ge(self.sent[b], SEQS // 2 * T4 * 2 * 16)

    def stats(self, dve):
        def part(i, b, h):
            dve.wait_ge(self.x_updated, i + 1)
            dve.sem_inc(self.m.carrier, 1)
            for j in range(T4):
                last = dve.bn_stats(self.st[:, j, :], self.m.X[:, i * T4 + j, :])
            last.then_inc(self.stats_done, 1)
            dve.wait_ge(self.stats_done, i + 1)
            dve.sem_inc(self.m.carrier, 1)
            for j in range(T4):
                last = dve.bn_aggr(self.mv[b][:, j, :], self.st[:, j, :])
            last.then_inc(self.aggr_done, 1)
            dve.wait_ge(self.aggr_done, i + 1)
            if past(i, 1):
                dve.wait_ge(self.rstd_ready, i)
            dve.tensor_scalar(self.rv[:], self.mv[b][:, :, 1], 1.0, LN_EPS, ALU.mult, ALU.add).then_inc(self.var_ready, 1)
        return part

    def normalize(self, dve):
        def part(i, b, h):
            dve.wait_ge(self.rstd_ready, i + 1)
            if past(h, 1):
                dve.wait_ge(self.sent[b], h * (T4 * 2 * 16))
            for j in range(T4):
                last = dve.tensor_scalar(self.nt[b][:, j, 0:P], self.m.X[:, i * T4 + j, :], self.mv[b][:, j, 0:1],
                                         self.rs[b][:, j:j + 1], ALU.subtract, ALU.mult)
            last.then_inc(self.normed, 1)
        return part

    def rank(self, dve):
        m, lg, lg2, mx, eq, first, mask, d = self.m, self.lg, self.lg2, self.mx, self.eq, self.first, self.mask, self.d
        im8 = m.const[:, C_IM8:C_IM8 + E].unsqueeze(1).to_broadcast([P, T4, E])

        def over(x):
            return x.unsqueeze(2).to_broadcast([P, T4, E])

        def part(i, b, h):
            n = [0]

            def done(ins):
                n[0] += 1
                ins.then_inc(self.step, 1)
                dve.wait_ge(self.step, i * self.STEPS + n[0])

            dve.wait_ge(self.logits_done, i + 1)
            done(dve.tensor_copy(lg[:], self.psL))
            done(dve.tensor_reduce(mx[:, 0, :], lg[:], AX, ALU.max))
            dve.tensor_tensor(d[:, :, 0:E], lg[:], over(mx[:, 0, :]), ALU.subtract)
            done(dve.tensor_tensor(eq[:], lg[:], over(mx[:, 0, :]), ALU.is_equal))
            done(dve.tensor_tensor(eq[:], eq[:], im8, ALU.mult))
            done(dve.tensor_reduce(first[:, 0, :], eq[:], AX, ALU.min))
            dve.tensor_copy(self.nt[b][:, :, P + 1], first[:, 0, :])
            tokens = m.const[:, C_TOKEN + i * T4:C_TOKEN + (i + 1) * T4] if isinstance(i, int) else m.const[:, bass.ds(i * T4 + C_TOKEN, T4)]
            dve.tensor_copy(self.nt[b][:, :, P], tokens)
            done(dve.tensor_tensor(mask[:, 0], im8, over(first[:, 0, :]), ALU.is_equal))
            done(dve.scalar_tensor_tensor(lg2[:], mask[:, 0], -3e38, lg[:], ALU.mult, ALU.add))
            done(dve.tensor_reduce(mx[:, 1, :], lg2[:], AX, ALU.max))
            dve.tensor_tensor(d[:, :, E], mx[:, 1, :], mx[:, 0, :], ALU.subtract).then_inc(self.d_ready, 1)
            done(dve.tensor_tensor(eq[:], lg2[:], over(mx[:, 1, :]), ALU.is_equal))
            done(dve.tensor_tensor(eq[:], eq[:], im8, ALU.mult))
            done(dve.tensor_reduce(first[:, 1, :], eq[:], AX, ALU.min))
            done(dve.tensor_tensor(mask[:, 1], im8, over(first[:, 1, :]), ALU.is_equal))
            done(dve.tensor_tensor(self.both[:], mask[:, 0], mask[:, 1], ALU.add))
            assert n[0] == self.RANK, n[0]
        return part

    def place(self, dve):
        m = self.m

        def part(i, b, h):
            n = [self.RANK]

            def done(ins):
                n[0] += 1
                ins.then_inc(self.step, 1)
                dve.wait_ge(self.step, i * self.STEPS + n[0])

            dve.wait_ge(self.exps_done, i + 1)
            done(dve.tensor_reduce(self.ssum[:], self.ex[:, :, 0:E], AX, ALU.add))
            done(dve.reciprocal(self.inv[:], self.ssum[:]))
            g = tiles(m.gates, i)
            dve.tensor_copy(g[:, :, 0], self.inv[:])
            dve.tensor_tensor(g[:, :, 1], self.ex[:, :, E], self.inv[:], ALU.mult)
            dve.wait_ge(self.counted, i + 1)
            done(dve.tensor_tensor(self.pk[:], self.psC[:, 0:T4, :].unsqueeze(1).to_broadcast([P, 2, T4, E]), self.mask[:], ALU.mult))
            dve.tensor_copy(m.carry[:], self.psC[:, T4, :])
            done(dve.tensor_reduce(self.pf[:], self.pk[:], AX, ALU.add))
            if past(h, 1):
                dve.wait_ge(self.sent[b], h * (T4 * 2 * 16))
            dve.tensor_copy(self.idx[b][:], self.pf[:]).then_inc(self.idx_ready, 1)
            assert n[0] == self.STEPS, n[0]
        return part

    def copy(self, act):
        def part(i, b, h):
            act.wait_ge(self.transposed, i + 1)
            if past(i, 1):
                act.wait_ge(self.logits_done, i)
            act.activation(self.xf[:], self.psT[:], ACT.Copy).then_inc(self.x_ready, 1)
        return part

    def exps(self, act):
        def part(i, b, h):
            act.wait_ge(self.d_ready, i + 1)
            if past(i, 1):
                act.wait_ge(self.step, i * self.STEPS)
            act.activation(self.ex[:], self.d[:], ACT.Exp).then_inc(self.exps_done, 1)
        return part

    def transpose(self, pe):
        def part(i, b, h):
            pe.wait_ge(self.normed, i + 1)
            if past(i, 1):
                pe.wait_ge(self.x_ready, i)
            for j in range(T4):
                last = pe.transpose(self.psT[:, j * P:(j + 1) * P], self.nt[b][:, j, 0:P], self.m.ident)
            last.then_inc(self.transposed, 1)
        return part

    def logits(self, pe):
        def part(i, b, h):
            pe.wait_ge(self.x_ready, i + 1)
            if past(i, 1):
                pe.wait_ge(self.step, i * self.STEPS)
            for j in range(T4):
                last = pe.matmul(self.psL[:, j, :], self.xf[:, j * P:(j + 1) * P], self.m.wr[:], start=True, stop=True)
            last.then_inc(self.logits_done, 1)
        return part

    def count(self, pe):
        m = self.m

        def part(i, b, h):
            pe.wait_ge(self.step, i * self.STEPS + self.RANK)
            pe.matmul(self.psC, m.ident, m.carry[:].unsqueeze(1).to_broadcast([P, T4 + 1, E]),
                      start=True, stop=False, skip_group_check=True)
            for j in range(T4):
                later = self.both[:, j, :].unsqueeze(1).to_broadcast([P, T4 - j, E])
                pe.matmul(self.psC[:, j + 1:, :], m.ones[:], later, start=False, stop=False, skip_group_check=True)
            pe.matmul(self.psC[:, 0:T4, :], m.const[:, C_UP:C_UP + P], self.both[:],
                      start=False, stop=True, skip_group_check=True).then_inc(self.counted, 1)
        return part

    def begin(self, dve):
        dve.tensor_copy(self.m.carry[:], self.m.const[:, C_BASE:C_BASE + E])

    def plan(self, dve):
        m, trow = self.m, self.trow
        n = [0]

        def link(ins):
            n[0] += 1
            ins.then_inc(self.step, 1)
            dve.wait_ge(self.step, SEQS * self.STEPS + n[0])

        dve.wait_ge(self.step, SEQS * self.STEPS)
        base = m.const[:, C_BASE:C_BASE + E]
        cnt, nt8, inc8, exc8, rb = (self.small[:, k, :] for k in range(5))
        link(dve.tensor_copy(m.tail_row[:], m.carry[0:1, :]))
        link(dve.tensor_tensor(cnt, m.carry[:], base, ALU.subtract))
        link(dve.tensor_tensor(self.cmp16[:], cnt.unsqueeze(2).to_broadcast([P, E, 16]),
                               m.const[:, C_TILE0:C_TILE0 + 16].unsqueeze(1).to_broadcast([P, E, 16]), ALU.is_gt))
        link(dve.tensor_reduce(nt8, self.cmp16[:], AX, ALU.add))
        link(dve.tensor_tensor_scan(inc8, m.ones[:, 0:E], nt8, 0.0, ALU.mult, ALU.add))
        link(dve.tensor_tensor(exc8, inc8, nt8, ALU.subtract))
        link(dve.scalar_tensor_tensor(rb, exc8, -float(ROWS), base, ALU.mult, ALU.add))
        jj = m.const[:, C_J:C_J + XTILES].unsqueeze(2).to_broadcast([P, XTILES, E])

        def by_tile(x):
            return x.unsqueeze(1).to_broadcast([P, XTILES, E])

        after, begun, own, roff, sel = (self.tile_w[:, k] for k in range(5))
        dve.tensor_tensor(after, jj, by_tile(inc8), ALU.is_ge)
        dve.tensor_scalar(trow[:, 0, :], m.const[:, C_J:C_J + XTILES], float(ROWS), -float(DUMMY), ALU.mult, ALU.add)
        link(dve.tensor_tensor(begun, jj, by_tile(exc8), ALU.is_ge))
        link(dve.tensor_tensor(own, begun, after, ALU.subtract))
        link(dve.tensor_tensor(roff, trow[:, 0, :].unsqueeze(2).to_broadcast([P, XTILES, E]), by_tile(rb), ALU.add))
        link(dve.tensor_tensor(sel, own, roff, ALU.mult))
        dve.tensor_reduce(trow[:, 1, :], sel, AX, ALU.add)
        link(dve.tensor_reduce(trow[:, 2, :], after, AX, ALU.add))
        dve.tensor_scalar(m.tile_first[:], trow[:, 2, :], float(E - 1), -8.0, ALU.min, ALU.add)
        dve.tensor_scalar(m.tile_row[:], trow[0:1, 1, :], float(DUMMY), None, ALU.add)
        dve.tensor_scalar(m.tile_expert[:], trow[0:1, 2, :], float(E - 1), None, ALU.min).then_inc(self.rows_ready, 1)

    def fill_tails(self, sp):
        rows = self.xs[DUMMY:DUMMY + ROWS, :].rearrange("(p r) d -> p (r d)", p=P)
        sp.dma_start(rows, self.m.filler[:].rearrange("p r d -> p (r d)")).then_inc(self.filled, 16)
        sp.wait_ge(self.step, SEQS * self.STEPS + 1)
        for e in range(E):
            r = sp.value_load(self.m.tail_row[0:1, e:e + 1], min_val=e * CAP, max_val=e * CAP + TILES * P)
            rows = self.xs[bass.ds(r, ROWS), :].rearrange("(p r) d -> p (r d)", p=P)
            sp.dma_start(rows, self.m.filler[:].rearrange("p r d -> p (r d)")).then_inc(self.filled, 16)
        sp.wait_ge(self.filled, (E + 1) * 16)


def experts(nc, m, xs, ys, moe_up, moe_b, moe_down, tag):
    ctx, sb, sem = phase(nc, tag)
    with ctx:
        H = HID * P
        w = [sb(f"w_up{b}", [P, 2 * H]) for b in range(2)]
        wh = [sb(f"w_up_high{b}", [P, 2 * H], FP32R) for b in range(2)]
        wl = [sb(f"w_up_low{b}", [P, 2 * H], FP32R) for b in range(2)]
        bu = [sb(f"b1_bg{b}", [P, 2 * HID]) for b in range(2)]
        wd = [sb(f"w_down{b}", [P, H + P]) for b in range(2)]
        xt = [sb(f"x_tm{b}", [P, T4, ROWW]) for b in range(2)]
        mt = [sb(f"token_first{b}", [P, T4, 2]) for b in range(2)]
        to = sb("to_second", [P, T4])
        ids = [sb(f"places{b}", [P, T4], U32) for b in range(2)]
        xh = [sb(f"x_high{b}", [P, ROWS], FP32R) for b in range(2)]
        xl = [sb(f"x_low{b}", [P, ROWS], FP32R) for b in range(2)]
        gl = [sb(f"gelu{b}", [P, ROWS]) for b in range(2)]
        hd = [sb(f"hidden{b}", [P, HID, ROWS]) for b in range(2)]
        yt = [sb(f"y_tm{b}", [P, T4, P]) for b in range(2)]
        psT, psG, psU, psY = m.banks[0], m.banks[1:3], m.banks[3:5], m.banks[5:7]
        w_in, x_in, b_in, y_out = ([sem(f"{k}{b}") for b in range(2)] for k in ("w_in", "x_in", "b_in", "y_out"))
        wh_ready, wl_ready = sem("w_high_ready"), sem("w_low_ready")
        transposed, xh_ready, xl_ready, gate_done, up_done = (
            sem("transposed"), sem("x_high_ready"), sem("x_low_ready"), sem("gate_done"), sem("up_done"))
        gelu_done, h_ready = sem("gelu_done"), sem("h_ready")
        down_done, y_ready, ids_ready = sem("down_done"), sem("y_ready"), sem("places_ready")
        block = ctx.enter_context(nc.Block())

        @block.sync
        def _(sp):
            def expert(i, t):
                e = sp.value_load(m.tile_expert[0:1, bass.ds(i, 1)], min_val=0, max_val=E - 1)
                return t[bass.ds(e, 1), :, :].rearrange("a p c -> (a p) c")

            def load_w(i, b, h):
                src = expert(i, moe_up)
                if past(i, 2):
                    sp.wait_ge(wl_ready, i - 1)
                sp.dma_start(w[b][:], src).then_inc(w_in[b], 16)

            def load_x(i, b, h):
                r = sp.value_load(m.tile_row[0:1, bass.ds(i, 1)], min_val=0, max_val=DUMMY)
                if past(i, 2):
                    sp.wait_ge(xl_ready, i - 1)
                sp.dma_start(xt[b][:], xs[bass.ds(r, ROWS), :].rearrange("(p r) d -> p r d", p=P)).then_inc(x_in[b], 16)

            def load_biases(i, b, h):
                src = expert(i, moe_b)
                if past(i, 2):
                    sp.wait_ge(h_ready, (i - 1) * HID)
                sp.dma_start(bu[b][:], src).then_inc(b_in[b], 16)

            def load_down(i, b, h):
                src = expert(i, moe_down)
                if past(i, 2):
                    sp.wait_ge(y_ready, i - 1)
                sp.dma_start(wd[b][:], src).then_inc(b_in[b], 16)

            pipelined(sp, XTILES, (0, load_w), (0, load_x), (1, load_biases), (1, load_down))

        @block.gpsimd
        def _(pool):
            def low(i, b, h):
                pool.wait_ge(wh_ready, i + 1)
                if past(i, 2):
                    pool.wait_ge(up_done, (i - 1) * HID)
                pool.tensor_tensor(wl[b][:], w[b][:], wh[b][:], ALU.subtract).then_inc(wl_ready, 1)

            def store(i, b, h):
                pool.wait_ge(y_ready, i + 1)
                pool.wait_ge(ids_ready, i * 2 + 2)
                pool.sem_inc(m.carrier, 1)
                for j in range(T4):
                    pool.indirect_dma_start(ys, bass.IndirectOffsetOnAxis(ap=ids[b][:, j:j + 1], axis=0), yt[b][:, j, :], None,
                                            bounds_check=2 * TOKENS - 1, oob_is_err=False).then_inc(y_out[b], 16)

            pipelined(pool, XTILES, (1, low), (3, store))
            for b in range(2):
                pool.wait_ge(y_out[b], (XTILES + 1 - b) // 2 * T4 * 16)

        @block.tensor
        def _(pe):
            def transpose(i, b, h):
                pe.wait_ge(x_in[b], h * 16 + 16)
                if past(i, 1):
                    pe.wait_ge(xl_ready, i)
                for j in range(T4):
                    last = pe.transpose(psT[:, j * P:(j + 1) * P], xt[b][:, j, 0:P], m.ident)
                last.then_inc(transposed, 1)

            def product(out, lhs, rhs):
                (lh, ll), (rh, rl) = lhs, rhs
                pe.matmul(out, lh, rh, start=True, stop=False)
                pe.matmul(out, lh, rl, start=False, stop=False)
                return pe.matmul(out, ll, rh, start=False, stop=True)

            def up(chunks):
                def part(i, b, h):
                    if chunks[0] == 0:
                        pe.wait_ge(wl_ready, i + 1)
                        pe.wait_ge(xl_ready, i + 1)
                    for c in chunks:
                        if past(i, 1) or c > 1:
                            pe.wait_ge(h_ready, i * HID + c - 1)
                        x = (xh[b][:], xl[b][:])
                        wg, w1 = (slice(k * H + c * P, k * H + (c + 1) * P) for k in (1, 0))
                        product(psG[c % 2][:], (wh[b][:, wg], wl[b][:, wg]), x).then_inc(gate_done, 1)
                        product(psU[c % 2][:], (wh[b][:, w1], wl[b][:, w1]), x).then_inc(up_done, 1)
                return part

            def down(i, b, h):
                pe.wait_ge(b_in[b], h * 32 + 32)
                pe.wait_ge(h_ready, (i + 1) * HID)
                if past(i, 2):
                    pe.wait_ge(y_ready, i - 1)
                for j in range(T4):
                    for c in range(HID):
                        last = pe.matmul(psY[b][:, j * P:(j + 1) * P], hd[b][:, c, j * P:(j + 1) * P],
                                         wd[b][:, c * P:(c + 1) * P], start=c == 0, stop=c == HID - 1)
                last.then_inc(down_done, 1)

            pipelined(pe, XTILES, (1, transpose), (2, up((0, 1))), (3, down), (2, up((2, 3))))

        @block.scalar
        def _(act):
            def x_high(i, b, h):
                act.wait_ge(transposed, i + 1)
                if past(i, 2):
                    act.wait_ge(up_done, (i - 1) * HID)
                act.activation(xh[b][:], psT[:], ACT.Copy).then_inc(xh_ready, 1)

            def w_high(i, b, h):
                act.wait_ge(w_in[b], h * 16 + 16)
                if past(i, 2):
                    act.wait_ge(up_done, (i - 1) * HID)
                act.activation(wh[b][:], w[b][:], ACT.Copy).then_inc(wh_ready, 1)

            def gelu(chunks):
                def part(i, b, h):
                    if chunks[0] == 0:
                        act.wait_ge(b_in[b], h * 32 + 32)
                    for c in chunks:
                        act.wait_ge(gate_done, i * HID + c + 1)
                        if past(i, 1) or c > 1:
                            act.wait_ge(h_ready, i * HID + c - 1)
                        act.activation(gl[c % 2][:], psG[c % 2][:], ACT.Gelu, bias=bu[b][:, HID + c:HID + c + 1]).then_inc(gelu_done, 1)
                return part

            pipelined(act, XTILES, (1, w_high), (1, x_high), (2, gelu((0, 1))), (2, gelu((2, 3))))

        @block.vector
        def _(dve):
            def x_low(i, b, h):
                dve.wait_ge(xh_ready, i + 1)
                if past(i, 2):
                    dve.wait_ge(ids_ready, (i - 1) * 2)
                dve.tensor_copy(mt[b][:], xt[b][:, :, P:])
                dve.tensor_tensor(xl[b][:], psT[:], xh[b][:], ALU.subtract).then_inc(xl_ready, 1)

            def hidden(chunks):
                def part(i, b, h):
                    if chunks[0] == 0:
                        dve.wait_ge(b_in[b], h * 32 + 32)
                        if past(i, 2):
                            dve.wait_ge(down_done, i - 1)
                    for c in chunks:
                        dve.wait_ge(gelu_done, i * HID + c + 1)
                        dve.wait_ge(up_done, i * HID + c + 1)
                        dve.scalar_tensor_tensor(hd[b][:, c, :], psU[c % 2][:], bu[b][:, c:c + 1], gl[c % 2][:],
                                                 ALU.add, ALU.mult).then_inc(h_ready, 1)
                return part

            def bias(i, b, h):
                dve.wait_ge(b_in[b], h * 32 + 32)
                dve.wait_ge(down_done, i + 1)
                if past(h, 1):
                    dve.wait_ge(y_out[b], h * (T4 * 16))
                b2 = wd[b][:, H:].unsqueeze(1).to_broadcast([P, T4, P])
                dve.tensor_tensor(yt[b][:], psY[b][:].rearrange("p (j c) -> p j c", c=P), b2, ALU.add).then_inc(y_ready, 1)

            def places(i, b, h):
                dve.tensor_scalar(to[:], mt[b][:, :, 1], m.tile_first[:, i:i + 1] if isinstance(i, int) else m.tile_first[:, bass.ds(i, 1)],
                                  float(TOKENS), ALU.not_equal, ALU.mult).then_inc(ids_ready, 1)
                dve.wait_ge(ids_ready, i * 2 + 1)
                if past(h, 1):
                    dve.wait_ge(y_out[b], h * (T4 * 16))
                dve.tensor_tensor(ids[b][:], to[:], mt[b][:, :, 0], ALU.add).then_inc(ids_ready, 1)

            pipelined(dve, XTILES, (1, x_low), (2, places), (2, hidden((0, 1))), (3, bias), (2, hidden((2, 3))))


def combine_parts(m, ys, sem, sb):
    yy = [sb(f"y_rows{b}", [P, 2, T4, P]) for b in range(2)]
    combined = sem("combined")
    fetched = [sem(f"fetched{b}") for b in range(2)]

    def fetch(sp):
        def part(i, b, h):
            if past(i, 2):
                sp.wait_ge(combined, 2 * i - 2)
            for k in range(2):
                rows = ys[bass.ds(i * SEQ + k * TOKENS, SEQ), :].rearrange("(t p) d -> p t d", p=P)
                sp.dma_start(yy[b][:, k], rows).then_inc(fetched[b], 16)
        return part

    def add(dve):
        def part(i, b, h):
            dve.wait_ge(fetched[b], h * 32 + 32)
            g = tiles(m.gates, i)
            for k in range(2):
                for j in range(T4):
                    x = m.X[:, i * T4 + j, :]
                    last = dve.scalar_tensor_tensor(x, yy[b][:, k, j, :], g[:, j, k:k + 1], x, ALU.mult, ALU.add)
                last.then_inc(combined, 1)
                if k == 0:
                    dve.wait_ge(combined, 2 * i + 1)
        return part

    return fetch, add, combined


def attention(nc, m, ys, xs):
    ctx, sb, sem = phase(nc, "attn")
    with ctx:
        fetch, add, combined = combine_parts(m, ys, sem, sb)
        st = [sb(f"stats{b}", [P, T4, 6]) for b in range(2)]
        mv = [sb(f"mean_var{b}", [P, T4, 2]) for b in range(2)]
        rv = [sb(f"var_eps{b}", [P, T4]) for b in range(2)]
        rs = [sb(f"rstd{b}", [P, T4]) for b in range(2)]
        nt = [sb(f"normed{b}", [P, T4, P]) for b in range(2)]
        xf = [sb(f"x_fm{b}", [P, SEQ]) for b in range(2)]
        hq = [sb(f"hidden_qk{b}", [P, 2, SEQ]) for b in range(2)]
        vf = [sb(f"v_fm{b}", [P, SEQ]) for b in range(2)]
        gf = [sb(f"g_fm{b}", [P, SEQ]) for b in range(2)]
        ab = sb("abs", [P, 2, SEQ])
        ee = sb("exp_minus_abs", [P, 2, SEQ])
        ln = sb("log1p", [P, 2, SEQ])
        qk = [sb(f"q_k_tm{b}", [P, 2, SEQ]) for b in range(2)]
        am = sb("a_masked", [P, P])
        ai = sb("a_plus_identity", [P, P])
        zz = sb("z", [P, 2])
        of = sb("out_fm", [P, SEQ])
        ot = sb("out_turned", [P, SEQ])
        sf = [sb(f"out_prime_fm{b}", [P, SEQ]) for b in range(2)]
        psT, psH, psQ, psP = m.banks[0], m.banks[1:3], m.banks[3:5], m.banks[7]
        psA = psO = m.banks[6]
        wq1, wq2, wk1, wk2, wv, wg, wp = (m.wb[:, k * P:(k + 1) * P] for k in range(7))

        stats_done, aggr_done, var_ready, rstd_ready = sem("stats_done"), sem("aggr_done"), sem("var_ready"), sem("rstd_ready")
        normed, transposed, x_ready = sem("normed"), sem("transposed"), sem("x_ready")
        up_done, gelu_done = sem("up_done"), sem("gelu_done")
        qk_done, exp_step, ln_done, qk_ready = sem("qk_done"), sem("exp_step"), sem("ln_done"), sem("qk_ready")
        a_done, a_masked, z_done, z_shift, z_ready = (
            sem("a_done"), sem("a_masked"), sem("z_done"), sem("z_shift"), sem("z_ready"))
        o_done, gated, p_done, x_updated = sem("o_done"), sem("gated"), sem("p_done"), sem("x_updated")
        turned, prime_done, prime_ready = sem("turned"), sem("prime_done"), sem("prime_ready")
        ones_r = sb("ones_rounded", [1, P], FP32R)
        row_h = sb("bias_rows_high", [1, 3, SEQ], FP32R)
        row_l = sb("bias_rows_low", [1, 3, SEQ], FP32R)
        rows_split = sem("rows_split")
        route = Route(m, xs, sem, sb, x_updated, psP, m.banks[5])
        block = ctx.enter_context(nc.Block())

        @block.gpsimd
        def _(pool):
            def rstd(i, b, h):
                pool.wait_ge(var_ready, i + 1)
                pool.tensor_tensor(rs[b][:], rv[b][:], m.half[:], ALU.pow).then_inc(rstd_ready, 1)

            pipelined(pool, SEQS, (7, route.rstd(pool)), (8, route.send(pool)), (2, rstd))
            route.all_sent(pool)

        @block.vector
        def _(dve):
            def stats(i, b, h):
                dve.wait_ge(combined, 2 * i + 2)
                dve.sem_inc(m.carrier, 1)
                for j in range(T4):
                    last = dve.bn_stats(st[b][:, j, :], m.X[:, i * T4 + j, :])
                last.then_inc(stats_done, 1)

            def aggregate(i, b, h):
                dve.wait_ge(stats_done, i + 1)
                dve.sem_inc(m.carrier, 1)
                for j in range(T4):
                    last = dve.bn_aggr(mv[b][:, j, :], st[b][:, j, :])
                last.then_inc(aggr_done, 1)
                dve.wait_ge(aggr_done, i + 1)
                dve.tensor_scalar(rv[b][:], mv[b][:, :, 1], 1.0, LN_EPS, ALU.mult, ALU.add).then_inc(var_ready, 1)

            def normalize(i, b, h):
                dve.wait_ge(rstd_ready, i + 1)
                if past(i, 2):
                    dve.wait_ge(transposed, i - 1)
                for j in range(T4):
                    last = dve.tensor_scalar(nt[b][:, j, :], m.X[:, i * T4 + j, :], mv[b][:, j, 0:1], rs[b][:, j:j + 1],
                                             ALU.subtract, ALU.mult)
                last.then_inc(normed, 1)

            def softplus(i, b, h):
                dve.wait_ge(ln_done, i + 1)
                if past(i, 2):
                    dve.wait_ge(a_done, i - 1)
                for k in range(2):
                    last = dve.scalar_tensor_tensor(qk[b][:, k, :], psQ[k][:], 0.0, ln[:, k, :], ALU.max, ALU.add)
                last.then_inc(qk_ready, 1)

            def matrices(i, b, h):
                dve.wait_ge(a_done, i + 1)
                if past(i, 1):
                    dve.wait_ge(o_done, i)
                dve.tensor_tensor(am[:], psA[:, 0:P], m.const[:, C_HEAD:C_HEAD + P], ALU.mult).then_inc(a_masked, 1)
                dve.wait_ge(a_masked, i + 1)
                dve.tensor_tensor(ai[:], am[:], m.ident, ALU.add)

            def denominator(i, b, h):
                dve.wait_ge(z_done, i + 1)
                dve.tensor_scalar(zz[:, 0:1], psA[:, P:P + 1], float(P), None, ALU.add).then_inc(z_shift, 1)
                dve.wait_ge(z_shift, i + 1)
                dve.reciprocal(zz[:, 1:2], zz[:, 0:1]).then_inc(z_ready, 1)

            def outputs(i, b, h):
                dve.wait_ge(z_ready, i + 1)
                dve.wait_ge(o_done, i + 1)
                dve.scalar_tensor_tensor(of[:], psO[:], zz[:, 1:2], gf[b][:], ALU.mult, ALU.mult).then_inc(gated, 1)
                if past(i, 1):
                    dve.wait_ge(prime_done, i)
                dve.wait_ge(gated, i + 1)
                dve.transpose(ot[:].rearrange("p (q r n) -> p r q n", q=4, n=HD), of[:].rearrange("p (r q n) -> p r q n", q=4, n=HD)).then_inc(turned, 1)

            def update(i, b, h):
                dve.wait_ge(p_done, i + 1)
                xs = tiles(m.X, i)
                dve.tensor_tensor(xs, psP[:].rearrange("p (j c) -> p j c", c=P), xs, ALU.add).then_inc(x_updated, 1)

            dve.wait_ge(rows_split, 1)
            dve.tensor_tensor(row_l[:], m.rows[:], row_h[:], ALU.subtract).then_inc(rows_split, 1)
            route.begin(dve)
            pipelined(dve, SEQS, (6, denominator), (3, normalize), (8, route.place(dve)), (6, outputs),
                      (7, route.normalize(dve)), (5, softplus), (2, add(dve)), (2, stats), (2, aggregate),
                      (7, route.rank(dve)), (6, update), (5, matrices), (6, route.stats(dve)))
            route.plan(dve)

        @block.scalar
        def _(act):
            def copy(i, b, h):
                act.wait_ge(transposed, i + 1)
                if past(i, 2):
                    act.wait_ge(up_done, (i - 1) * 4)
                act.activation(xf[b][:].rearrange("p (r j a) -> p j a r", r=16, j=T4), psT[:].rearrange("p (j a r) -> p j a r", j=T4, r=16),
                               ACT.Copy).then_inc(x_ready, 1)

            def primed(i, b, h):
                act.wait_ge(prime_done, i + 1)
                if past(i, 2):
                    act.wait_ge(p_done, i - 1)
                act.activation(sf[b][:].rearrange("p (j q t) -> p q j t", q=4, j=T4), psO[:].rearrange("p (q j t) -> p q j t", q=4, j=T4), ACT.Copy).then_inc(prime_ready, 1)

            def gelus(i, b, h):
                if past(i, 2):
                    act.wait_ge(qk_done, (i - 1) * 2)
                outs = (hq[b][:, 0, :], hq[b][:, 1, :], vf[b][:], gf[b][:])
                for c, (out, bias) in enumerate(zip(outs, (QB1, KB1, VB, GB))):
                    if c == 2 and past(i, 2):
                        act.wait_ge(gated, i - 1)
                    act.wait_ge(up_done, i * 4 + c + 1)
                    act.activation(out, psH[c % 2][:], ACT.Gelu, bias=m.col(bias)).then_inc(gelu_done, 1)

            def log1p(i, b, h):
                if past(i, 1):
                    act.wait_ge(exp_step, i * 2)
                for k in range(2):
                    act.wait_ge(qk_done, i * 2 + k + 1)
                    last = act.activation(ab[:, k, :], psQ[k][:], ACT.Abs)
                last.then_inc(exp_step, 1)
                act.wait_ge(exp_step, i * 2 + 1)
                act.activation(ee[:], ab[:], ACT.Exp, scale=-1.0).then_inc(exp_step, 1)
                act.wait_ge(exp_step, i * 2 + 2)
                if past(i, 1):
                    act.wait_ge(qk_ready, i)
                act.activation(ln[:], ee[:], ACT.Ln, bias=1.0).then_inc(ln_done, 1)

            act.activation(ones_r[:], m.ones[0:1, :], ACT.Copy)
            act.activation(row_h[:], m.rows[:], ACT.Copy).then_inc(rows_split, 1)
            pipelined(act, SEQS, (4, copy), (4, gelus), (7, route.copy(act)), (6, primed), (7, route.exps(act)),
                      (4, log1p))

        @block.sync
        def _(sp):
            pipelined(sp, SEQS, (0, fetch(sp)))
            route.fill_tails(sp)

        @block.tensor
        def _(pe):
            def transpose(i, b, h):
                pe.wait_ge(normed, i + 1)
                if past(i, 1):
                    pe.wait_ge(x_ready, i)
                for j in range(T4):
                    last = pe.transpose(psT[:, j * P:(j + 1) * P], nt[b][:, j, :], m.ident)
                last.then_inc(transposed, 1)

            def up(i, b, h):
                pe.wait_ge(x_ready, i + 1)
                for c, w in enumerate((wq1, wk1, wv, wg)):
                    if past(i, 1) or c > 1:
                        pe.wait_ge(gelu_done, i * 4 + c - 1)
                    pe.matmul(psH[c % 2][:], w, xf[b][:], start=True, stop=True).then_inc(up_done, 1)

            def second(k, w):
                def part(i, b, h):
                    pe.wait_ge(gelu_done, i * 4 + k + 1)
                    if past(i, 1):
                        pe.wait_ge(qk_ready, i)
                    pe.matmul(psQ[k][:], ones_r[:], row_h[:, k, :], start=True, stop=False, skip_group_check=True)
                    pe.matmul(psQ[k][:], ones_r[:], row_l[:, k, :], start=False, stop=False, skip_group_check=True)
                    for j in range(T4):
                        last = pe.matmul(psQ[k][:, j * P:(j + 1) * P], hq[b][:, k, j * P:(j + 1) * P], w,
                                         start=False, stop=j == T4 - 1, skip_group_check=True)
                    last.then_inc(qk_done, 1)
                return part

            def product(i, b, h):
                pe.wait_ge(qk_ready, i + 1)
                if past(i, 1):
                    pe.wait_ge(prime_ready, i)
                for j in range(T4):
                    last = pe.matmul(psA[:, 0:P], qk[b][:, 1, j * P:(j + 1) * P], qk[b][:, 0, j * P:(j + 1) * P],
                                     start=j == 0, stop=j == T4 - 1)
                last.then_inc(a_done, 1)

            def sums(i, b, h):
                pe.wait_ge(a_masked, i + 1)
                pe.matmul(psA[:, P:P + 1], am[:], m.ones[:, 0:1], start=True, stop=True).then_inc(z_done, 1)

            def outputs(i, b, h):
                pe.wait_ge(z_shift, i + 1)
                pe.wait_ge(gelu_done, i * 4 + 4)
                pe.matmul(psO[:], ai[:], vf[b][:], start=True, stop=True).then_inc(o_done, 1)

            def prime(i, b, h):
                pe.wait_ge(turned, i + 1)
                for q in range(4):
                    last = pe.transpose(psO[:, q * P:(q + 1) * P], ot[:, q * P:(q + 1) * P], m.ident)
                last.then_inc(prime_done, 1)

            def project(i, b, h):
                pe.wait_ge(prime_ready, i + 1)
                if past(i, 1):
                    pe.wait_ge(x_updated, i)
                    pe.wait_ge(route.x_ready, i)
                pe.matmul(psP[:], ones_r[:], row_h[:, 2, :], start=True, stop=False, skip_group_check=True)
                pe.matmul(psP[:], ones_r[:], row_l[:, 2, :], start=False, stop=False, skip_group_check=True)
                for j in range(T4):
                    last = pe.matmul(psP[:, j * P:(j + 1) * P], sf[b][:, j * P:(j + 1) * P], wp,
                                     start=False, stop=j == T4 - 1, skip_group_check=True)
                last.then_inc(p_done, 1)

            pe.wait_ge(rows_split, 2)
            pipelined(pe, SEQS, (8, route.count(pe)), (4, transpose), (6, outputs), (4, up), (6, prime),
                      (7, route.transpose(pe)), (4, second(0, wq2)), (7, route.logits(pe)), (4, second(1, wk2)),
                      (6, project), (5, product), (5, sums))


def finish(nc, m, ys, out):
    ctx, sb, sem = phase(nc, "fin")
    with ctx:
        fetch, add, combined = combine_parts(m, ys, sem, sb)
        stored = sem("stored")
        block = ctx.enter_context(nc.Block())
        ov = out.rearrange("(s t p) d -> s p t d", p=P, t=T4)

        @block.vector
        def _(dve):
            pipelined(dve, SEQS, (1, add(dve)))

        @block.sync
        def _(sp):
            def store(i, b, h):
                sp.wait_ge(combined, 2 * i + 2)
                dst = ov[i] if isinstance(i, int) else ov[bass.ds(i, 1)].rearrange("a p t d -> (a p) t d")
                sp.dma_start(dst, tiles(m.X, i)).then_inc(stored, 16)

            pipelined(sp, SEQS, (0, fetch(sp)), (2, store))
            sp.wait_ge(stored, SEQS * 16)


def program(nc, x, vecs, consts, wa, wb, wr, rows, moe_up, moe_b, moe_down, out):
    xs = nc.dram_tensor("expert_rows_in", [DUMMY + ROWS, ROWW], FP32, kind="Internal").ap()
    ys = nc.dram_tensor("expert_results", [2 * TOKENS, P], FP32, kind="Internal").ap()
    with ExitStack() as ctx:
        m = Memory(nc, ctx)
        setup(nc, m, vecs, consts, wa, wb, wr, rows)
        with nc.sbuf_tensor("after_time_mix", [P, TILES, P], FP32) as XP:
            time_mix(nc, m, x, XP)
            channel_mix(nc, m, XP, xs)
        experts(nc, m, xs, ys, moe_up, moe_b, moe_down, "experts1")
        attention(nc, m, ys, xs)
        experts(nc, m, xs, ys, moe_up, moe_b, moe_down, "experts2")
        finish(nc, m, ys, out)


def constants():
    import numpy as np
    c = np.zeros((P, NCONST), np.float32)
    c[:, C_ID:C_ID + P] = np.eye(P)
    c[:, C_UP:C_UP + P] = np.triu(np.ones((P, P)), 1)
    c[:, C_HEAD:C_HEAD + P] = np.kron(np.eye(HEADS), np.full((HD, HD), SCALE))
    c[:, C_IM8:C_IM8 + E] = np.arange(E) - 8
    c[:, C_TILE0:C_TILE0 + 16] = np.arange(16) * ROWS
    c[:, C_J:C_J + XTILES] = np.arange(XTILES)
    c[:, C_BASE:C_BASE + E] = np.arange(E) * CAP
    c[:, C_TOKEN:C_TOKEN + TILES] = np.arange(TILES)[None, :] * P + np.arange(P)[:, None]
    return c


def kernel(**inputs):
    import numpy as np
    import concourse.bacc as bacc
    from concourse.bass_utils import run_bass_kernel_spmd

    v = {k: np.asarray(a) for k, a in inputs.items()}
    A, B, F = "L0_attn_a_", "L0_attn_b_", "L0_ffn_"
    vec_names = [A + k for k in ("ln1_g", "ln1_b", "ln2_g", "ln2_b", "att_time_mix", "att_combined_mix", "time_decay",
                                 "time_first", "ffn_time_mix", "ffn_combined_mix")] + [B + k for k in ("q_b1", "k_b1", "v_b", "g_b")]
    hid = HID * P
    w1, wg = v[F + "w1_w"].transpose(0, 2, 1), v[F + "wg_w"].transpose(0, 2, 1)
    w2 = v[F + "w2_w"].transpose(0, 2, 1).reshape(E, HID, P, P).transpose(0, 2, 1, 3).reshape(E, P, hid)
    b1, bg = (v[F + k].reshape(E, HID, P).transpose(0, 2, 1) for k in ("w1_b", "wg_b"))
    b2 = np.broadcast_to(v[F + "w2_b"][:, None, :], (E, P, P))
    arrays = {
        "x": v[A + "x"].reshape(SEQS * SEQ, P),
        "vecs": np.stack([v[k].reshape(P) for k in vec_names], 1),
        "consts": constants(),
        "wa": np.concatenate([v[A + k].T for k in ("Wk", "Wv", "Wr", "Wo", "Fr", "Fk")]
                             + [v[A + "Fv"].T.reshape(HID, P, P).transpose(1, 0, 2).reshape(P, hid)], 1),
        "wb": np.concatenate([v[B + k].T for k in ("q_w1", "q_w2", "k_w1", "k_w2", "v_w", "g_w", "p_w")], 1),
        "wr": v[F + "router_w"].T,
        "rows": np.stack([np.tile(v[B + k], T4) for k in ("q_b2", "k_b2", "p_b")])[None],
        "moe_up": np.concatenate([w1, wg], 2),
        "moe_b": np.concatenate([b1, bg], 2),
        "moe_down": np.concatenate([w2, b2], 2),
    }
    arrays = {f"in_{k}": np.ascontiguousarray(a) for k, a in arrays.items()}
    nc = bacc.Bacc("TRN2", target_bir_lowering=False, num_devices=1)
    args = [nc.dram_tensor(k, list(a.shape), FP32, kind="ExternalInput").ap() for k, a in arrays.items()]
    out = nc.dram_tensor("out", [SEQS * SEQ, P], FP32, kind="ExternalOutput").ap()
    program(nc, *args, out)
    r = run_bass_kernel_spmd(nc, [arrays], core_ids=[0])
    return r.results[0]["out"].reshape(SEQS, SEQ, P)
```
